# Optimizing a Trainium2 kernel written in Bass

```python
import numpy as np
import jax
import jax.numpy as jnp

def _softmax(x, axis=-1):
    return jax.nn.softmax(x, axis=axis)

def _gelu(x):
    return jax.nn.gelu(x, approximate=True)

def _silu(x):
    return jax.nn.silu(x)

def _sigmoid(x):
    return jax.nn.sigmoid(x)

def _layernorm(x, axis=-1, eps=1e-05):
    m = jnp.mean(x, axis=axis, keepdims=True)
    v = jnp.var(x, axis=axis, keepdims=True)
    return (x - m) / jnp.sqrt(v + eps)

def _scatter_add(tgt, idx, src, axis=0):
    return tgt.at[idx].add(src)

def _segment_sum(src, seg, n):
    return jax.ops.segment_sum(src, seg, n)
kernel_name = 'mk_vit_tower_d2_tok_img768_r4_4e2b5f'

def setup_inputs(seed: int=0):
    np.random.seed(seed)
    _w = jnp.asarray

    def _rec_inputs():
        import jax
        import jax.numpy as jnp
        _rk = jax.random.key(seed)
        x = -0.000222058 + 0.999998 * jax.random.normal(jax.random.fold_in(_rk, 1), (64, 3, 84, 84), jnp.float32)
        return x
    x = _rec_inputs()

    def _L0_tok_setup():
        import jax, jax.numpy as jnp
        import numpy as np
        from jax import lax
        HIDDEN = 192
        C_IN = 3
        PATCH = 16
        SIDE = 32
        NUM_PATCHES = SIDE * SIDE

        def _position_ids(nb_h, nb_w):
            boundaries = np.arange(1.0 / SIDE, 1.0, 1.0 / SIDE, dtype=np.float32)
            frac_h = np.arange(0.0, 1.0 - 1e-06, 1.0 / nb_h, dtype=np.float32)
            frac_w = np.arange(0.0, 1.0 - 1e-06, 1.0 / nb_w, dtype=np.float32)
            bh = np.searchsorted(boundaries, frac_h, side='right')
            bw = np.searchsorted(boundaries, frac_w, side='right')
            return jnp.asarray((bh[:, None] * SIDE + bw).reshape(-1), dtype=jnp.int32)
        key = jax.random.key(seed)
        k1, k2, k3 = jax.random.split(key, 3)
        pixel_values = jax.random.normal(k1, (32, C_IN, 128, 128), dtype=jnp.float32)
        conv_w = jax.random.normal(k2, (HIDDEN, C_IN, PATCH, PATCH), dtype=jnp.float32) * 0.02
        conv_b = jnp.zeros((HIDDEN,), dtype=jnp.float32)
        pos_table = jax.random.normal(k3, (NUM_PATCHES, HIDDEN), dtype=jnp.float32) * 0.02
        return {'pixel_values': pixel_values, 'conv_w': conv_w, 'conv_b': conv_b, 'pos_table': pos_table}
    _L0_tok_all = _L0_tok_setup()
    _L0_tok_in = {k: v for k, v in _L0_tok_all.items() if k in ('conv_w', 'conv_b', 'pos_table')}
    del _L0_tok_all

    def _L0_attn_setup():
        import jax, jax.numpy as jnp
        import numpy as np
        DIM, HEADS, DH, G = (192, 12, 64, 4)
        INNER = HEADS * DH
        B, N = (8, 1024)
        LN_EPS = 1e-05

        def _ln(x, g, b):
            m = x.mean(-1, keepdims=True)
            v = ((x - m) ** 2).mean(-1, keepdims=True)
            return (x - m) * jax.lax.rsqrt(v + LN_EPS) * g + b

        def _phi(x):
            return jnp.concatenate([jax.nn.relu(x), jax.nn.relu(-x)], axis=-1)
        key = jax.random.key(seed)
        ks = jax.random.split(key, 12)
        s = 0.02
        return {'x': jax.random.normal(ks[0], (B, N, DIM), jnp.float32), 'Wk': jax.random.normal(ks[1], (DIM, INNER), jnp.float32) * s, 'Wv': jax.random.normal(ks[2], (DIM, INNER), jnp.float32) * s, 'Wq': jax.random.normal(ks[3], (G, DIM, INNER), jnp.float32) * s, 'Wt': jax.random.normal(ks[4], (G, DH, DH), jnp.float32) * s, 'bt': jax.random.normal(ks[5], (G, DH), jnp.float32) * s, 'gt': jnp.ones((G, DH), jnp.float32), 'betat': jnp.zeros((G, DH), jnp.float32), 'Wf': jax.random.normal(ks[6], (G * INNER, INNER), jnp.float32) * s, 'bf': jax.random.normal(ks[7], (INNER,), jnp.float32) * s, 'gf': jnp.ones((INNER,), jnp.float32), 'betaf': jnp.zeros((INNER,), jnp.float32), 'Wo': jax.random.normal(ks[8], (INNER, DIM), jnp.float32) * s, 'bo': jax.random.normal(ks[9], (DIM,), jnp.float32) * s}
    _L0_attn_all = _L0_attn_setup()
    _L0_attn_in = {k: v for k, v in _L0_attn_all.items() if k in ('Wk', 'Wv', 'Wq', 'Wt', 'bt', 'gt', 'betat', 'Wf', 'bf', 'gf', 'betaf', 'Wo', 'bo')}
    del _L0_attn_all

    def _L0_ffn_setup():
        import jax, jax.numpy as jnp
        import numpy as np
        B, N, DIM, HEADS = (4, 256, 192, 12)
        HIDDEN, E, TOPK = (768, 8, 2)
        EPS = 1e-05

        def _layernorm(x, g, b):
            mu = jnp.mean(x, axis=-1, keepdims=True)
            var = jnp.var(x, axis=-1, keepdims=True)
            return (x - mu) * jax.lax.rsqrt(var + EPS) * g + b
        key = jax.random.key(seed)
        ks = jax.random.split(key, 10)
        s = 0.02
        return {'x': jax.random.normal(ks[0], (B, N, DIM), dtype=jnp.float32), 'ln1_g': jnp.ones((DIM,), jnp.float32), 'ln1_b': jnp.zeros((DIM,), jnp.float32), 'qkv_w': jax.random.normal(ks[1], (3 * DIM, DIM), jnp.float32) * s, 'proj_w': jax.random.normal(ks[2], (DIM, DIM), jnp.float32) * s, 'proj_b': jnp.zeros((DIM,), jnp.float32), 'ln2_g': jnp.ones((DIM,), jnp.float32), 'ln2_b': jnp.zeros((DIM,), jnp.float32), 'gate_w': jax.random.normal(ks[3], (E, DIM), jnp.float32) * s, 'gate_b': jnp.zeros((E,), jnp.float32), 'w1': jax.random.normal(ks[4], (E, HIDDEN, DIM), jnp.float32) * s, 'b1': jnp.zeros((E, HIDDEN), jnp.float32), 'w2': jax.random.normal(ks[5], (E, DIM, HIDDEN), jnp.float32) * s, 'b2': jnp.zeros((E, DIM), jnp.float32)}
    _L0_ffn_all = _L0_ffn_setup()
    _L0_ffn_in = {k: v for k, v in _L0_ffn_all.items() if k in ('ln1_g', 'ln1_b', 'qkv_w', 'proj_w', 'proj_b', 'ln2_g', 'ln2_b', 'gate_w', 'gate_b', 'w1', 'b1', 'w2', 'b2')}
    del _L0_ffn_all

    def _L1_attn_setup():
        import jax, jax.numpy as jnp
        import numpy as np
        B, S, D, H = (8, 256, 192, 12)
        HS = D // H
        key = jax.random.key(seed)
        k1, k2, k3 = jax.random.split(key, 3)
        x = jax.random.normal(k1, (B, S, D), dtype=jnp.float32)
        W_attn = jax.random.normal(k2, (D, 3 * H * HS), dtype=jnp.float32) * 0.02
        b_attn = jnp.zeros((3 * H * HS,), dtype=jnp.float32)
        W_proj = jax.random.normal(k3, (H * HS, D), dtype=jnp.float32) * 0.02
        b_proj = jnp.zeros((D,), dtype=jnp.float32)
        return {'x': x, 'W_attn': W_attn, 'b_attn': b_attn, 'W_proj': W_proj, 'b_proj': b_proj}
    _L1_attn_all = _L1_attn_setup()
    _L1_attn_in = {k: v for k, v in _L1_attn_all.items() if k in ('W_attn', 'b_attn', 'W_proj', 'b_proj')}
    del _L1_attn_all

    def _L1_ffn_setup():
        import jax, jax.numpy as jnp
        import numpy as np
        DIM = 192
        FF = 768
        E = 8
        K = 2
        H = 12
        HD = DIM // H
        LN_EPS = 1e-05

        def _layernorm(x, g, b):
            m = jnp.mean(x, axis=-1, keepdims=True)
            v = jnp.var(x, axis=-1, keepdims=True)
            return (x - m) * jax.lax.rsqrt(v + LN_EPS) * g + b

        def _attention(x, Wqkv, Wproj):
            B, T, D = x.shape
            qkv = (x @ Wqkv).reshape(B, T, 3, H, HD)
            q, k, v = (qkv[:, :, 0], qkv[:, :, 1], qkv[:, :, 2])
            scores = jnp.einsum('bqhd,bkhd->bhqk', q, k) * jnp.float32(HD) ** (-0.5)
            attn = jax.nn.softmax(scores, axis=-1)
            out = jnp.einsum('bhqk,bkhd->bqhd', attn, v).reshape(B, T, D)
            return out @ Wproj

        def _moe(x, Wrouter, W1, W2):
            B, T, D = x.shape
            xf = x.reshape(-1, D)
            N = xf.shape[0]
            logits = xf @ Wrouter
            topk_w, topk_idx = jax.lax.top_k(logits, K)
            topk_w = jax.nn.softmax(topk_w.astype(jnp.float32), axis=-1).astype(x.dtype)
            we = jnp.zeros((N, E), x.dtype).at[jnp.arange(N)[:, None], topk_idx].add(topk_w)

            def body(acc, expert):
                W1e, W2e, we_e = expert
                h = jax.nn.gelu(xf @ W1e, approximate=False)
                return (acc + we_e[:, None] * (h @ W2e), None)
            out, _ = jax.lax.scan(body, jnp.zeros_like(xf), (W1, W2, we.T))
            return out.reshape(B, T, D)
        key = jax.random.key(seed)
        ks = jax.random.split(key, 7)
        B, T = (4, 256)
        init = lambda k, shape, fan: jax.random.normal(k, shape, jnp.float32) * fan ** (-0.5)
        return {'x': jax.random.normal(ks[0], (B, T, DIM), jnp.float32), 'Wqkv': init(ks[1], (DIM, 3 * DIM), DIM), 'Wproj': init(ks[2], (DIM, DIM), DIM), 'Wrouter': init(ks[3], (DIM, E), DIM), 'W1': init(ks[4], (E, DIM, FF), DIM), 'W2': init(ks[5], (E, FF, DIM), FF), 'ln1_g': jnp.ones((DIM,), jnp.float32), 'ln1_b': jnp.zeros((DIM,), jnp.float32), 'ln2_g': jnp.ones((DIM,), jnp.float32), 'ln2_b': jnp.zeros((DIM,), jnp.float32)}
    _L1_ffn_all = _L1_ffn_setup()
    _L1_ffn_in = {k: v for k, v in _L1_ffn_all.items() if k in ('Wqkv', 'Wproj', 'Wrouter', 'W1', 'W2', 'ln1_g', 'ln1_b', 'ln2_g', 'ln2_b')}
    del _L1_ffn_all
    return {'x': x, 'L0_tok_conv_w': _L0_tok_in['conv_w'], 'L0_tok_conv_b': _L0_tok_in['conv_b'], 'L0_tok_pos_table': _L0_tok_in['pos_table'], 'L0_attn_Wk': _L0_attn_in['Wk'], 'L0_attn_Wv': _L0_attn_in['Wv'], 'L0_attn_Wq': _L0_attn_in['Wq'], 'L0_attn_Wt': _L0_attn_in['Wt'], 'L0_attn_bt': _L0_attn_in['bt'], 'L0_attn_gt': _L0_attn_in['gt'], 'L0_attn_betat': _L0_attn_in['betat'], 'L0_attn_Wf': _L0_attn_in['Wf'], 'L0_attn_bf': _L0_attn_in['bf'], 'L0_attn_gf': _L0_attn_in['gf'], 'L0_attn_betaf': _L0_attn_in['betaf'], 'L0_attn_Wo': _L0_attn_in['Wo'], 'L0_attn_bo': _L0_attn_in['bo'], 'L0_ffn_ln1_g': _L0_ffn_in['ln1_g'], 'L0_ffn_ln1_b': _L0_ffn_in['ln1_b'], 'L0_ffn_qkv_w': _L0_ffn_in['qkv_w'], 'L0_ffn_proj_w': _L0_ffn_in['proj_w'], 'L0_ffn_proj_b': _L0_ffn_in['proj_b'], 'L0_ffn_ln2_g': _L0_ffn_in['ln2_g'], 'L0_ffn_ln2_b': _L0_ffn_in['ln2_b'], 'L0_ffn_gate_w': _L0_ffn_in['gate_w'], 'L0_ffn_gate_b': _L0_ffn_in['gate_b'], 'L0_ffn_w1': _L0_ffn_in['w1'], 'L0_ffn_b1': _L0_ffn_in['b1'], 'L0_ffn_w2': _L0_ffn_in['w2'], 'L0_ffn_b2': _L0_ffn_in['b2'], 'L1_attn_W_attn': _L1_attn_in['W_attn'], 'L1_attn_b_attn': _L1_attn_in['b_attn'], 'L1_attn_W_proj': _L1_attn_in['W_proj'], 'L1_attn_b_proj': _L1_attn_in['b_proj'], 'L1_ffn_Wqkv': _L1_ffn_in['Wqkv'], 'L1_ffn_Wproj': _L1_ffn_in['Wproj'], 'L1_ffn_Wrouter': _L1_ffn_in['Wrouter'], 'L1_ffn_W1': _L1_ffn_in['W1'], 'L1_ffn_W2': _L1_ffn_in['W2'], 'L1_ffn_ln1_g': _L1_ffn_in['ln1_g'], 'L1_ffn_ln1_b': _L1_ffn_in['ln1_b'], 'L1_ffn_ln2_g': _L1_ffn_in['ln2_g'], 'L1_ffn_ln2_b': _L1_ffn_in['ln2_b']}

def reference(x, L0_tok_conv_w, L0_tok_conv_b, L0_tok_pos_table, L0_attn_Wk, L0_attn_Wv, L0_attn_Wq, L0_attn_Wt, L0_attn_bt, L0_attn_gt, L0_attn_betat, L0_attn_Wf, L0_attn_bf, L0_attn_gf, L0_attn_betaf, L0_attn_Wo, L0_attn_bo, L0_ffn_ln1_g, L0_ffn_ln1_b, L0_ffn_qkv_w, L0_ffn_proj_w, L0_ffn_proj_b, L0_ffn_ln2_g, L0_ffn_ln2_b, L0_ffn_gate_w, L0_ffn_gate_b, L0_ffn_w1, L0_ffn_b1, L0_ffn_w2, L0_ffn_b2, L1_attn_W_attn, L1_attn_b_attn, L1_attn_W_proj, L1_attn_b_proj, L1_ffn_Wqkv, L1_ffn_Wproj, L1_ffn_Wrouter, L1_ffn_W1, L1_ffn_W2, L1_ffn_ln1_g, L1_ffn_ln1_b, L1_ffn_ln2_g, L1_ffn_ln2_b):
    import jax
    import jax.numpy as jnp

    def _L0_tok_ref(pixel_values, conv_w, conv_b, pos_table):
        import jax, jax.numpy as jnp
        import numpy as np
        from jax import lax
        HIDDEN = 192
        C_IN = 3
        PATCH = 16
        SIDE = 32
        NUM_PATCHES = SIDE * SIDE

        def _position_ids(nb_h, nb_w):
            boundaries = np.arange(1.0 / SIDE, 1.0, 1.0 / SIDE, dtype=np.float32)
            frac_h = np.arange(0.0, 1.0 - 1e-06, 1.0 / nb_h, dtype=np.float32)
            frac_w = np.arange(0.0, 1.0 - 1e-06, 1.0 / nb_w, dtype=np.float32)
            bh = np.searchsorted(boundaries, frac_h, side='right')
            bw = np.searchsorted(boundaries, frac_w, side='right')
            return jnp.asarray((bh[:, None] * SIDE + bw).reshape(-1), dtype=jnp.int32)
        B, _, H, W = pixel_values.shape
        nb_h, nb_w = (H // PATCH, W // PATCH)
        patches = lax.conv_general_dilated(pixel_values, conv_w, window_strides=(PATCH, PATCH), padding='VALID', dimension_numbers=('NCHW', 'OIHW', 'NCHW'))
        patches = patches + conv_b[None, :, None, None]
        embeddings = patches.reshape(B, HIDDEN, nb_h * nb_w).transpose(0, 2, 1)
        pos_ids = _position_ids(nb_h, nb_w)
        pos_emb = pos_table[pos_ids]
        return embeddings + pos_emb[None, :, :]

    def _L0_attn_ref(x, Wk, Wv, Wq, Wt, bt, gt, betat, Wf, bf, gf, betaf, Wo, bo):
        import jax, jax.numpy as jnp
        import numpy as np
        DIM, HEADS, DH, G = (192, 12, 64, 4)
        INNER = HEADS * DH
        B, N = (8, 1024)
        LN_EPS = 1e-05

        def _ln(x, g, b):
            m = x.mean(-1, keepdims=True)
            v = ((x - m) ** 2).mean(-1, keepdims=True)
            return (x - m) * jax.lax.rsqrt(v + LN_EPS) * g + b

        def _phi(x):
            return jnp.concatenate([jax.nn.relu(x), jax.nn.relu(-x)], axis=-1)
        b, n, _ = x.shape
        k = (x @ Wk).reshape(b, n, HEADS, DH).transpose(0, 2, 1, 3)
        v = (x @ Wv).reshape(b, n, HEADS, DH).transpose(0, 2, 1, 3)
        q = jnp.einsum('bnd,gde->gbne', x, Wq).reshape(G, b, n, HEADS, DH)
        q = q.transpose(0, 1, 3, 2, 4)
        q = jnp.einsum('gbhnd,gde->gbhne', q, Wt) + bt[:, None, None, None, :]
        q = jax.nn.gelu(q, approximate=False)
        q = _ln(q, gt[:, None, None, None, :], betat[:, None, None, None, :])
        qf = _phi(q) / jnp.sqrt(jnp.float32(2 * DH))
        kf = _phi(k)
        kv = jnp.einsum('bhnd,bhnm->bhdm', kf, v)
        out = jnp.einsum('gbhnd,bhdm->gbhnm', qf, kv)
        ksum = kf.sum(axis=2)
        norm = jnp.einsum('gbhnd,bhd->gbhn', qf, ksum)
        out = out / (norm[..., None] + 1e-06)
        out = out.transpose(1, 3, 0, 2, 4).reshape(b, n, G * INNER)
        fused = jax.nn.gelu(_ln(out @ Wf + bf, gf, betaf), approximate=False)
        return fused @ Wo + bo

    def _L0_ffn_ref(x, ln1_g, ln1_b, qkv_w, proj_w, proj_b, ln2_g, ln2_b, gate_w, gate_b, w1, b1, w2, b2):
        import jax, jax.numpy as jnp
        import numpy as np
        B, N, DIM, HEADS = (4, 256, 192, 12)
        HIDDEN, E, TOPK = (768, 8, 2)
        EPS = 1e-05

        def _layernorm(x, g, b):
            mu = jnp.mean(x, axis=-1, keepdims=True)
            var = jnp.var(x, axis=-1, keepdims=True)
            return (x - mu) * jax.lax.rsqrt(var + EPS) * g + b
        b, n, d = x.shape
        hd = d // HEADS
        scale = hd ** (-0.5)
        h = _layernorm(x, ln1_g, ln1_b)
        qkv = h @ qkv_w.T
        qkv = qkv.reshape(b, n, 3, HEADS, hd).transpose(2, 0, 3, 1, 4)
        q, k, v = (qkv[0], qkv[1], qkv[2])
        attn = jax.nn.softmax(jnp.einsum('bhnd,bhmd->bhnm', q, k) * scale, axis=-1)
        a = jnp.einsum('bhnm,bhmd->bhnd', attn, v)
        a = a.transpose(0, 2, 1, 3).reshape(b, n, d)
        a = a @ proj_w.T + proj_b
        x = x + a
        h2 = _layernorm(x, ln2_g, ln2_b)
        t = h2.reshape(-1, d)
        T = t.shape[0]
        logits = t @ gate_w.T + gate_b
        top_val, top_idx = jax.lax.top_k(logits, TOPK)
        score = jax.nn.softmax(top_val, axis=-1)
        cw = jnp.zeros((T, E), t.dtype).at[jnp.arange(T)[:, None], top_idx].add(score)
        out = jnp.zeros_like(t)
        for e in range(E):
            he = jax.nn.gelu(t @ w1[e].T + b1[e], approximate=False)
            ye = he @ w2[e].T + b2[e]
            out = out + cw[:, e:e + 1] * ye
        return x + out.reshape(b, n, d)

    def _L1_attn_ref(x, W_attn, b_attn, W_proj, b_proj):
        import jax, jax.numpy as jnp
        import numpy as np
        B, S, D, H = (8, 256, 192, 12)
        HS = D // H
        b, s, d = x.shape
        qkv = (x @ W_attn + b_attn).reshape(b, s, 3, H, HS)
        q, k, v = (qkv[:, :, 0], qkv[:, :, 1], qkv[:, :, 2])
        scale = jnp.sqrt(jnp.asarray(HS, dtype=x.dtype))
        scores = jnp.einsum('bqhd,bkhd->bhqk', q, k) / scale
        causal = jnp.tril(jnp.ones((s, s), dtype=bool))
        scores = jnp.where(causal, scores, -jnp.inf)
        attn = jax.nn.softmax(scores, axis=-1)
        out = jnp.einsum('bhqk,bkhd->bqhd', attn, v).reshape(b, s, H * HS)
        return out @ W_proj + b_proj

    def _L1_ffn_ref(x, Wqkv, Wproj, Wrouter, W1, W2, ln1_g, ln1_b, ln2_g, ln2_b):
        import jax, jax.numpy as jnp
        import numpy as np
        DIM = 192
        FF = 768
        E = 8
        K = 2
        H = 12
        HD = DIM // H
        LN_EPS = 1e-05

        def _layernorm(x, g, b):
            m = jnp.mean(x, axis=-1, keepdims=True)
            v = jnp.var(x, axis=-1, keepdims=True)
            return (x - m) * jax.lax.rsqrt(v + LN_EPS) * g + b

        def _attention(x, Wqkv, Wproj):
            B, T, D = x.shape
            qkv = (x @ Wqkv).reshape(B, T, 3, H, HD)
            q, k, v = (qkv[:, :, 0], qkv[:, :, 1], qkv[:, :, 2])
            scores = jnp.einsum('bqhd,bkhd->bhqk', q, k) * jnp.float32(HD) ** (-0.5)
            attn = jax.nn.softmax(scores, axis=-1)
            out = jnp.einsum('bhqk,bkhd->bqhd', attn, v).reshape(B, T, D)
            return out @ Wproj

        def _moe(x, Wrouter, W1, W2):
            B, T, D = x.shape
            xf = x.reshape(-1, D)
            N = xf.shape[0]
            logits = xf @ Wrouter
            topk_w, topk_idx = jax.lax.top_k(logits, K)
            topk_w = jax.nn.softmax(topk_w.astype(jnp.float32), axis=-1).astype(x.dtype)
            we = jnp.zeros((N, E), x.dtype).at[jnp.arange(N)[:, None], topk_idx].add(topk_w)

            def body(acc, expert):
                W1e, W2e, we_e = expert
                h = jax.nn.gelu(xf @ W1e, approximate=False)
                return (acc + we_e[:, None] * (h @ W2e), None)
            out, _ = jax.lax.scan(body, jnp.zeros_like(xf), (W1, W2, we.T))
            return out.reshape(B, T, D)
        x = x + _attention(_layernorm(x, ln1_g, ln1_b), Wqkv, Wproj)
        x = x + _moe(_layernorm(x, ln2_g, ln2_b), Wrouter, W1, W2)
        return x
    h = _L0_tok_ref(x, L0_tok_conv_w, L0_tok_conv_b, L0_tok_pos_table)
    h = h + _L0_attn_ref(_layernorm(h, axis=-1), L0_attn_Wk, L0_attn_Wv, L0_attn_Wq, L0_attn_Wt, L0_attn_bt, L0_attn_gt, L0_attn_betat, L0_attn_Wf, L0_attn_bf, L0_attn_gf, L0_attn_betaf, L0_attn_Wo, L0_attn_bo)
    h = h + _L0_ffn_ref(_layernorm(h, axis=-1), L0_ffn_ln1_g, L0_ffn_ln1_b, L0_ffn_qkv_w, L0_ffn_proj_w, L0_ffn_proj_b, L0_ffn_ln2_g, L0_ffn_ln2_b, L0_ffn_gate_w, L0_ffn_gate_b, L0_ffn_w1, L0_ffn_b1, L0_ffn_w2, L0_ffn_b2)
    h = h + _L1_attn_ref(_layernorm(h, axis=-1), L1_attn_W_attn, L1_attn_b_attn, L1_attn_W_proj, L1_attn_b_proj)
    h = h + _L1_ffn_ref(_layernorm(h, axis=-1), L1_ffn_Wqkv, L1_ffn_Wproj, L1_ffn_Wrouter, L1_ffn_W1, L1_ffn_W2, L1_ffn_ln1_g, L1_ffn_ln1_b, L1_ffn_ln2_g, L1_ffn_ln2_b)
    return h

_drawn_inputs = setup_inputs


def setup_inputs(seed=0):
    import zlib

    import numpy as np

    out = dict(_drawn_inputs(seed))
    spreads = {'L0_tok_conv_b': (0.0, 0.1),
     'L0_attn_gt': (1.0, 0.599),
     'L0_attn_betat': (0.0, 0.48),
     'L0_attn_gf': (1.0, 0.2),
     'L0_attn_betaf': (0.0, 0.1),
     'L0_ffn_ln1_g': (1.0, 0.6),
     'L0_ffn_ln1_b': (0.0, 0.615),
     'L0_ffn_proj_b': (0.0, 0.1),
     'L0_ffn_ln2_g': (1.0, 0.542),
     'L0_ffn_ln2_b': (0.0, 0.421),
     'L0_ffn_gate_b': (0.0, 0.1),
     'L0_ffn_b1': (0.0, 0.448),
     'L0_ffn_b2': (0.0, 0.1),
     'L1_attn_b_attn': (0.0, 0.371),
     'L1_attn_b_proj': (0.0, 0.1),
     'L1_ffn_ln1_g': (1.0, 0.2),
     'L1_ffn_ln1_b': (0.0, 0.1),
     'L1_ffn_ln2_g': (1.0, 0.2),
     'L1_ffn_ln2_b': (0.0, 0.1)}
    factors = {}
    for name, (base, spread) in spreads.items():
        noise = np.random.default_rng([zlib.crc32(name.encode()), seed]).standard_normal(out[name].shape)
        drawn = base * np.exp(spread * noise) if base else spread * noise
        out[name] = jnp.asarray(drawn.astype(out[name].dtype))
    for name, factor in factors.items():
        out[name] = (out[name] * factor).astype(out[name].dtype)
    return out
```

```python
from contextlib import ExitStack

import concourse.bass as bass
import concourse.mybir as mybir
import numpy as np
from concourse.alu_op_type import AluOpType as ALU

ACT = mybir.ActivationFunctionType
AX = mybir.AxisListType
F32 = mybir.dt.float32

IMAGES, PATCHES, PITCH = 64, 25, 32
PER_TILE = 128 // PITCH
TILES = IMAGES // PER_TILE
GROUPS = 4
GT = TILES // GROUPS
GI = GT * PER_TILE
TOK = GI * PATCHES
PAD = GI * PITCH
D, FC = 192, 96
KC = D // FC
PATCH_K = 3 * 16 * 16
PK = PATCH_K // 128
EPS = 1e-5
LH, LD, LG = 12, 64, 4
INNER = LH * LD
PAIRS = LH // 2
CHUNKS = PAIRS * LG
WM = INNER // 128
QQ = LG * PATCHES
NORM_EPS = 1e-6 * float(np.sqrt(2 * LD))
H, HD = 12, 16
HPC = FC // HD
E, FF = 8, 768
FM = FF // 128


def load_shapes():
    shapes = {
        "patches": [TILES, 128, PATCH_K], "conv_w": [128, PK * D], "conv_b": [1, D], "pos": [128, D],
        "wk": [FC, KC * INNER], "wv": [FC, KC * INNER], "wqT": [128, CHUNKS * D], "wt2": [128, LG * 128],
        "bt2": [128, LG], "gt2": [128, LG], "betat2": [128, LG],
        "wf": [WM, 128, CHUNKS * 128], "bf": [128, WM], "gf": [128, WM], "betaf": [128, WM],
        "wo": [128, WM * D], "bo": [1, D],
        "ident": [128, 128], "center": [128, 128], "mean768": [128, 128], "den_sum": [128, 2 * 128],
        "var_pick": [128, CHUNKS * 2 * CHUNKS], "rstd_pick": [2 * CHUNKS, CHUNKS * 128],
        "slot_mask": [128, 2 * 2], "v_mask": [128, 2 * 128],
        "head_mask": [FC, HPC], "causal": [128, PATCHES], "before": [128, E * E],
    }
    for a in ("a0", "a1", "a2"):
        shapes |= {f"{a}_qkv": [FC, KC * 3 * D], f"{a}_proj": [FC, KC * D]}
    shapes |= {"a0_projb": [1, D], "a1_projb": [1, D], "a1_qkb": [FC, 2 * KC], "a1_vb": [1, D]}
    for m in ("m0", "m1"):
        shapes |= {f"{m}_ln1": [FC, 2 * KC], f"{m}_ln2": [FC, 2 * KC], f"{m}_gate": [FC, KC * E],
                   f"{m}_w1": [FC, KC * E * FF], f"{m}_w2": [128, E * FM * D]}
    shapes |= {"m0_gateb": [1, E], "m0_b1": [128, E * FM], "m0_b2": [E, D]}
    return shapes


def build(nc, dram, out, stages=7):
    ctx = ExitStack()
    with ctx:
        def sem(name):
            return ctx.enter_context(nc.semaphore(name))

        def sb(name, shape, scope=ctx):
            return scope.enter_context(nc.sbuf_tensor(name, shape, F32))

        bank = [ctx.enter_context(nc.psum_tensor(f"bank{k}", [128, 512], F32)) for k in range(2)]
        psum_s = ctx.enter_context(nc.psum_tensor("psum_s", [128, H, 128], F32))
        psum_o = ctx.enter_context(nc.psum_tensor("psum_o", [128, H, 128], F32))
        s_flat = psum_s[:, :, :].rearrange("p h f -> p (h f)")
        o_flat = psum_o[:, :, :].rearrange("p h f -> p (h f)")
        PB = [bank[0][:, :], bank[1][:, :]] + [s_flat[:, 512 * k:512 * k + 512] for k in range(3)] \
            + [o_flat[:, 512 * k:512 * k + 512] for k in range(3)]

        hid = sb("hid", [128, TILES, D])
        ident = sb("ident_sb", [128, 128])
        half = sb("half", [128, GT])
        eps = sb("eps_sb", [128, 1])
        neps = sb("neps_sb", [128, 1])
        stats = sb("stats", [128, GT, 6])
        mv = sb("mv", [128, GT, 2])
        ve = sb("ve", [128, GT])
        rstd = sb("rstd", [128, GT])
        junk = sb("junk", [128, 1])
        pool_junk = sb("pool_junk", [128, 1])
        xn = sb("xn", [128, GT, D])
        xT = sb("xT", [FC, KC, PAD])

        ident_in = sem("ident_in")
        fills = sem("fills")

        lin = ExitStack()
        patch_t = sb("patch_t", [128, GT, PK, 128], lin)
        conv_w = sb("conv_w_sb", [128, PK, D], lin)
        posb = sb("posb", [128, D], lin)
        feat = sb("feat", [128, CHUNKS, TOK], lin)
        wqt = sb("wqt", [FC, KC, CHUNKS, 128], lin)
        wfs = [sb(f"wfs{k}", [128, CHUNKS, 128], lin) for k in range(2)]
        kpos = sb("kpos", [128, GI, 2, PITCH], lin)
        kneg = sb("kneg", [128, GI, 2, PITCH], lin)
        upos = sb("upos", [128, 2, LG, TOK], lin)
        uneg = sb("uneg", [128, 2, LG, TOK], lin)
        vblk = sb("vblk", [128, 2, 2, 2, 128], lin)
        scor = sb("scor", [128, 2, 2 * QQ], lin)
        denb = sb("denb", [128, 2, TOK], lin)
        rec = sb("rec", [128, TOK], lin)
        gq = sb("gq", [128, 2, TOK], lin)
        wk = sb("wk_sb", [FC, KC, INNER], lin)
        wv = sb("wv_sb", [FC, KC, INNER], lin)
        wo = sb("wo_sb", [128, WM, D], lin)
        bob = sb("bob", [128, D], lin)
        center = sb("center_sb", [128, 128], lin)
        mean768 = sb("mean768_sb", [128, 128], lin)
        den_sum = sb("den_sum_sb", [128, 2, 128], lin)
        var_pick = sb("var_pick_sb", [128, CHUNKS, 2 * CHUNKS], lin)
        rstd_pick = sb("rstd_pick_sb", [2 * CHUNKS, CHUNKS, 128], lin)
        slot_mask = sb("slot_mask_sb", [128, 2, 2], lin)
        v_mask = sb("v_mask_sb", [128, 2, 128], lin)
        lcol = sb("lcol", [128, 5, LG], lin)
        fcol = sb("fcol", [128, 3, WM], lin)
        sqb = denb
        xdup = patch_t[0:FC, :, :, :].rearrange("p t k n -> p (t k n)")[:, 0:KC * GI * 2 * PITCH]\
            .rearrange("p (k b h t) -> p k b h t", k=KC, b=GI, h=2)
        qstd = rec[0:2 * CHUNKS, :]
        qrstd = sb("qrstd", [2 * CHUNKS, TOK], lin)
        wqT = feat[:, :, :].rearrange("p c t -> p (c t)")[:, 0:CHUNKS * D].rearrange("p (c d) -> p c d", d=D)
        wt2 = upos[:, 0, :, 0:128]
        y768 = upos[:, :, :, :].rearrange("p a g t -> p (a g t)")[:, 0:WM * TOK].rearrange("p (m t) -> p m t", t=TOK)
        ysq = uneg[:, :, :, :].rearrange("p a g t -> p (a g t)")[:, 0:WM * TOK].rearrange("p (m t) -> p m t", t=TOK)
        fused = feat[:, :, :].rearrange("p c t -> p (c t)")[:, 0:WM * PAD].rearrange("p (m t) -> p m t", t=PAD)
        lin.close()

        late = ExitStack()
        xres = sb("xres", [128, TILES, D], late)
        w1 = sb("w1_sb", [FC, KC, E, FF], late)
        w2 = sb("w2_sb", [128, E, FM, D], late)
        gate_w = sb("gate_w_sb", [FC, KC, E], late)
        gate_b = sb("gate_b_sb", [128, E], late)
        bias1 = sb("b1_sb", [128, E * FM], late)
        bias2 = sb("b2_sb", [E, D], late)
        before = sb("before_sb", [128, E, E], late)
        head_mask = sb("head_mask_sb", [FC, HPC], late)
        causal = sb("causal_sb", [128, PATCHES], late)
        qkv_w = [sb(f"qkv_w{a}", [FC, KC, 3 * D], late) for a in range(3)]
        proj_w = [sb(f"proj_w{a}", [FC, KC, D], late) for a in range(3)]
        proj_b = [sb(f"proj_b{a}", [128, D], late) for a in range(2)]
        qk_b = sb("qk_b", [FC, 2, KC], late)
        v_b = sb("v_b", [128, D], late)
        ln_cols = sb("ln_cols", [FC, 4, 2, KC], late)
        att = ExitStack()
        qT = sb("qT", [FC, KC, PAD], att)
        kexp = sb("kexp", [FC, KC, HPC, PAD], att)
        vt = sb("vt", [128, GT, D], att)
        sx = sb("sx", [128, 2, H, PATCHES], att)
        pr = sb("pr", [128, 2, H, PITCH], att)
        pT = sb("pT", [128, 2, H, 128], att)
        smax = sb("smax", [128, H], att)
        ssum = sb("ssum", [128, H], att)
        srec = sb("srec", [128, 2, H], att)
        ao = sb("ao", [128, 2, D], att)
        aoT = sb("aoT", [FC, KC, 128], att)
        att.close()
        moe = ExitStack()
        he = sb("he", [128, 2, FM, GI, PITCH], moe)
        lg = sb("lg", [128, GT, E], moe)
        gtr = sb("gtr", [128, GT, E, E], moe)
        eqr = sb("eqr", [128, GT, E, E], moe)
        rank = sb("rank", [128, GT, E], moe)
        picked = sb("picked", [128, GT, E], moe)
        lmax = sb("lmax", [128, GT], moe)
        lexp = sb("lexp", [128, GT, E], moe)
        lsum = sb("lsum", [128, GT], moe)
        lrec = sb("lrec", [128, GT], moe)
        cw = sb("cw", [128, GT, E], moe)
        cwT = sb("cwT", [E, PAD], moe)
        moe.close()
        late.close()

        ATT = [dict(a=0, src="hid", double=True, causal=False, ln=0),
               dict(a=1, src="hid", double=False, causal=True, ln=None),
               dict(a=2, src="hid", double=True, causal=False, ln=2)]
        MOE = [dict(m=0, ln=1, biased=True), dict(m=1, ln=3, biased=False)]

        patch_in = [sem(f"patch_in{t}") for t in range(GT)]
        conv_in = sem("conv_in")
        emb_ready, emb_free = sem("emb_ready"), sem("emb_free")
        wq_in, lin_in = sem("wq_in"), sem("lin_in")
        wqt_ready, wqt_kept = sem("wqt_ready"), sem("wqt_kept")
        lin_fill = sem("lin_fill")
        lfront = dict(ln=sem("l_ln"), rs=sem("l_rs"), xTp=sem("l_xTp"), xTs=sem("l_xTs"))
        q_ready, gelu_done, c_ready, c_kept, sq_done, var_acc = map(
            sem, ("q_ready", "gelu_done", "c_ready", "c_kept", "sq_done", "var_acc"))
        std_ready, rstd_ready, rb_ready, w_ready, u_done = map(
            sem, ("std_ready", "rstd_ready", "rb_ready", "w_ready", "u_done"))
        xdup_done = sem("xdup_done")
        k_ready, kpm_done, v_ready, vblk_done, s_ready, st_done = map(
            sem, ("k_ready", "kpm_done", "v_ready", "vblk_done", "s_ready", "st_done"))
        den_ready, num_ready, den_kept, rec_done, out_done = map(
            sem, ("den_ready", "num_ready", "den_kept", "rec_done", "out_done"))
        wf_in = [sem(f"wf_in{k}") for k in range(2)]
        y_ready, wf_free, mean_ready, yc_done, ysq_done, yvar_ready, ystd_done, yrec_done, yn_done = map(
            sem, ("y_ready", "wf_free", "mean_ready", "yc_done", "ysq_done", "yvar_ready", "ystd_done",
                  "yrec_done", "yn_done"))
        fused_done, z_ready, z_added, hid_done = map(sem, ("fused_done", "z_ready", "z_added", "hid_done"))
        late_in = sem("late_in")
        late_fill = sem("late_fill")
        att_all = {n: sem(f"a_{n}") for n in (
            "xTp", "xTs", "qk_p", "q_sb", "k_sb", "v_p", "v_sb", "s_p", "sx_act", "shifted",
            "exp_done", "p_t", "o_p", "ao_done", "oT_p", "oT_sb", "y_p", "y_done", "fill")}
        moe_all = {n: sem(f"m_{n}") for n in (
            "xTp", "xTs", "g_p", "shifted", "exp_done", "cw_ready", "cwT_p", "cwT_sb", "h_p", "h_act", "chain",
            "fill", "done")}
        AS = [att_all | {n: sem(f"a{a}_{n}") for n in ("ln", "rs", "chain")} for a in range(3)]
        MS = [moe_all | {n: sem(f"m{m}_{n}") for n in ("w_in", "ln", "rs", "y_p", "y_acc")} for m in range(2)]
        out_sem = sem("out_sem")

        class Chain:

            def __init__(self, eng, counter, i, per):
                self.eng, self.counter, self.base, self.per, self.n = eng, counter, i * per, per, 0

            def step(self, ins):
                ins.then_inc(self.counter, 1)
                self.n += 1

            def wait(self):
                self.eng.wait_ge(self.counter, self.base + self.n)

            def end(self):
                assert self.n == self.per, (self.n, self.per)

        def row(name, parts, size):
            a = dram[name]
            return bass.AP(a.tensor, 0, [[0, parts], [1, size]])

        def compact(view):
            return view.rearrange("p (b q) -> p b q", q=PITCH)[:, :, 0:PATCHES]

        def front_dve(dve, i, S, src, double):
            rounds = 2 if double else 1
            ch = Chain(dve, S["ln"], i, 4 * rounds)
            for r in range(rounds):
                tiles = src if r == 0 else xres
                if r:
                    ch.wait()
                    dve.memset(junk[:, :], 0.0)
                for t in range(GT):
                    last = dve.bn_stats(stats[:, t, :], tiles[:, bass.ds(i * GT + t, 1), :])
                ch.step(last)
                ch.wait()
                dve.memset(junk[:, :], 0.0)
                for t in range(GT):
                    last = dve.bn_aggr(mv[:, t, :], stats[:, t, :])
                ch.step(last)
                ch.wait()
                ch.step(dve.tensor_scalar(ve[:, :], mv[:, :, 1], EPS, None, ALU.add))
                dve.wait_ge(S["rs"], i * rounds + r + 1)
                for t in range(GT):
                    dst = xres[:, bass.ds(i * GT + t, 1), :] if r + 1 < rounds else xn[:, t, :]
                    last = dve.tensor_scalar(dst, tiles[:, bass.ds(i * GT + t, 1), :], mv[:, t, 0:1],
                                             rstd[:, t:t + 1], ALU.subtract, ALU.mult)
                ch.step(last)
            ch.end()

        def front_pool(pool, i, S, double):
            rounds = 2 if double else 1
            for r in range(rounds):
                pool.wait_ge(S["ln"], i * (4 * rounds) + 4 * r + 3)
                pool.tensor_tensor(rstd[:, :], ve[:, :], half[:, :], ALU.pow).then_inc(S["rs"], 1)

        def front_pe(pe, i, S, double):
            per = 8 if double else 4
            pe.wait_ge(S["ln"], i * per + per)
            for t in range(GT):
                for k in range(KC):
                    last = pe.transpose(PB[k][0:FC, 128 * t:128 * t + 128], xn[:, t, FC * k:FC * k + FC],
                                        ident[:, :])
            last.then_inc(S["xTp"], 1)

        def front_act(act, v, S, ln):
            act.wait_ge(S["xTp"], v + 1)
            for k in range(KC):
                if ln is None:
                    last = act.activation(xT[:, k, :], PB[k][0:FC, :], ACT.Copy)
                else:
                    last = act.activation(xT[:, k, :], PB[k][0:FC, :], ACT.Identity,
                                          scale=ln_cols[:, ln, 0, k:k + 1], bias=ln_cols[:, ln, 1, k:k + 1])
                last.then_inc(S["xTs"], 1)

        def stage_done(n):
            return [(emb_free, TILES + 2), (hid_done, TILES), (att_all["y_done"], TILES), (moe_all["done"], GROUPS),
                    (att_all["y_done"], 2 * TILES), (att_all["y_done"], 3 * TILES), (moe_all["done"], 2 * GROUPS)][n]

        block = ctx.enter_context(nc.Block())

        @block.sync
        def _(sp):
            sp.dma_start(conv_w[:, :, :].rearrange("p k d -> p (k d)"), dram["conv_w"][:, :]).then_inc(conv_in, 16)
            sp.dma_start(posb[:, :], dram["pos"][:, :]).then_inc(conv_in, 16)
            sp.dma_start(xn[:, 0, :], row("conv_b", 128, D)).then_inc(conv_in, 16)

            def load_patches(i, t):
                sp.dma_start(patch_t[:, t, :, :].rearrange("p k n -> p (k n)"),
                             dram["patches"][bass.ds(i * GT + t, 1), :, :].rearrange("o p n -> p (o n)"))\
                  .then_inc(patch_in[t], 16)

            for t in range(GT):
                load_patches(0, t)
            with sp.Fori(1, GROUPS) as i:
                for t in range(GT):
                    sp.wait_ge(emb_ready, i * GT + t + 1 - GT)
                    load_patches(i, t)
            if stages < 2:
                sp.wait_ge(*stage_done(0))
            if stages >= 2:
                sp.wait_ge(wf_free, 2)
                with sp.Fori(0, GROUPS) as i:
                    for m in range(WM):
                        sp.wait_ge(wf_free, i * WM + m + 1)
                        sp.dma_start(wfs[m % 2][:, :, :].rearrange("p c n -> p (c n)"), dram["wf"][m, :, :])\
                          .then_inc(wf_in[m % 2], 16)
            if stages >= 3:
                sp.wait_ge(*stage_done(1))
                for a in range(3):
                    sp.dma_start(qkv_w[a][:, :, :].rearrange("p k n -> p (k n)"), dram[f"a{a}_qkv"][:, :]).then_inc(late_in, 16)
                    sp.dma_start(proj_w[a][:, :, :].rearrange("p k n -> p (k n)"), dram[f"a{a}_proj"][:, :]).then_inc(late_in, 16)
                for a in range(2):
                    sp.dma_start(proj_b[a][:, :], row(f"a{a}_projb", 128, D)).then_inc(late_in, 16)
                sp.dma_start(qk_b[:, :, :].rearrange("p a k -> p (a k)"), dram["a1_qkb"][:, :]).then_inc(late_in, 16)
                sp.dma_start(v_b[:, :], row("a1_vb", 128, D)).then_inc(late_in, 16)
                for n, name in enumerate(("m0_ln1", "m0_ln2", "m1_ln1", "m1_ln2")):
                    sp.dma_start(ln_cols[:, n, :, :].rearrange("p a k -> p (a k)"), dram[name][:, :]).then_inc(late_in, 16)
                sp.dma_start(head_mask[:, :], dram["head_mask"][:, :]).then_inc(late_in, 16)
                sp.dma_start(causal[:, :], dram["causal"][:, :]).then_inc(late_in, 16)
                sp.dma_start(before[:, :, :].rearrange("p a b -> p (a b)"), dram["before"][:, :]).then_inc(late_in, 16)
                sp.dma_start(gate_b[:, :], row("m0_gateb", 128, E)).then_inc(late_in, 16)
                sp.dma_start(bias1[:, :], dram["m0_b1"][:, :]).then_inc(late_in, 16)
                sp.dma_start(bias2[:, :], dram["m0_b2"][:, :]).then_inc(late_in, 16)
                for m in range(2):
                    if m == 1:
                        if stages < 5:
                            break
                        sp.wait_ge(*stage_done(3))
                    sp.dma_start(gate_w[:, :, :].rearrange("p k n -> p (k n)"), dram[f"m{m}_gate"][:, :]).then_inc(MS[m]["w_in"], 16)
                    sp.dma_start(w1[:, :, :, :].rearrange("p k e n -> p (k e n)"), dram[f"m{m}_w1"][:, :]).then_inc(MS[m]["w_in"], 16)
                    sp.dma_start(w2[:, :, :, :].rearrange("p e m n -> p (e m n)"), dram[f"m{m}_w2"][:, :]).then_inc(MS[m]["w_in"], 16)
                for m in range(2):
                    if m == 0 or stages >= 5:
                        sp.wait_ge(MS[m]["w_in"], 48)
            if stages < 7:
                sp.wait_ge(*stage_done(stages - 1))
                for t in range(TILES):
                    sp.dma_start(out[t, :, :], hid[:, t, :]).then_inc(out_sem, 16)
                sp.wait_ge(out_sem, 16 * TILES)
            else:
                with sp.Fori(0, GROUPS) as i:
                    sp.wait_ge(MS[1]["done"], i + GROUPS + 1)
                    sp.dma_start(out[bass.ds(i * GT, GT), :, :].rearrange("t p d -> p t d"),
                                 hid[:, bass.ds(i * GT, GT), :]).then_inc(out_sem, 16)
                sp.wait_ge(out_sem, 16 * GROUPS)

        @block.gpsimd
        def _(pool):
            if stages >= 2:
                pool.wait_ge(fills, 3)
                pool.memset(kpos[:, :, :, :], 0.0).then_inc(lin_fill, 1)
                pool.memset(kneg[:, :, :, :], 0.0).then_inc(lin_fill, 1)
                with pool.Fori(0, GROUPS) as i:
                    front_pool(pool, i, lfront, False)
                    pool.wait_ge(lfront["xTs"], i * 2 + 2)
                    pool.tensor_tensor(pool_junk[:, :], half[:, 0:1], half[:, 0:1], ALU.mult)
                    for k in range(KC):
                        pool.tensor_copy(xdup[:, k, :, :, :], xT[:, k, :].rearrange("p (b t) -> p b t", t=PITCH).unsqueeze(2)
                                         .to_broadcast([FC, GI, 2, PITCH])).then_inc(xdup_done, 1)

            def attention_pool(n, s):
                pool.wait_ge(*stage_done(s - 1))
                pool.memset(pr[:, :, :, :], 0.0).then_inc(AS[n]["fill"], 1)
                pool.memset(pT[:, :, :, :], 0.0).then_inc(AS[n]["fill"], 1)
                with pool.Fori(0, GROUPS) as i:
                    front_pool(pool, i, AS[n], ATT[n]["double"])

            def moe_pool(n, s):
                pool.wait_ge(*stage_done(s - 1))
                pool.memset(he[:, :, :, :, PATCHES:PITCH], 0.0).then_inc(MS[n]["fill"], 1)
                with pool.Fori(0, GROUPS) as i:
                    front_pool(pool, i, MS[n], False)

            for s, (what, n) in enumerate(PLAN, 2):
                if stages > s:
                    (attention_pool if what == "att" else moe_pool)(n, s)

        @block.scalar
        def _(act):
            act.dma_start(ident[:, :], dram["ident"][:, :]).then_inc(ident_in, 16)
            if stages >= 2:
                act.dma_start(wqT, dram["wqT"].rearrange("p (c d) -> p c d", d=D)).then_inc(wq_in, 16)
                act.dma_start(wt2, dram["wt2"].rearrange("p (g n) -> p g n", g=LG)).then_inc(wq_in, 16)
                for dst, name in ((wk[:, :, :].rearrange("p k n -> p (k n)"), "wk"), (wv[:, :, :].rearrange("p k n -> p (k n)"), "wv"),
                                  (wo[:, :, :].rearrange("p m n -> p (m n)"), "wo"), (center[:, :], "center"), (mean768[:, :], "mean768"),
                                  (den_sum[:, :, :].rearrange("p a n -> p (a n)"), "den_sum"),
                                  (var_pick[:, :, :].rearrange("p c n -> p (c n)"), "var_pick"),
                                  (rstd_pick[:, :, :].rearrange("p c n -> p (c n)"), "rstd_pick"),
                                  (slot_mask[:, :, :].rearrange("p a n -> p (a n)"), "slot_mask"),
                                  (v_mask[:, :, :].rearrange("p a n -> p (a n)"), "v_mask"),
                                  (lcol[:, 0, :], "bt2"), (lcol[:, 1, :], "gt2"), (lcol[:, 2, :], "betat2"),
                                  (fcol[:, 0, :], "bf"), (fcol[:, 1, :], "gf"), (fcol[:, 2, :], "betaf")):
                    act.dma_start(dst, dram[name][:, :]).then_inc(lin_in, 16)
                act.dma_start(bob[:, :], row("bo", 128, D)).then_inc(lin_in, 16)
                act.sem_inc(wf_free, 2)
                for c in range(CHUNKS):
                    for k in range(KC):
                        n = c * KC + k
                        act.wait_ge(wqt_ready, n + 1)
                        act.activation(wqt[:, k, c, :], PB[n % 4][0:FC, 0:128], ACT.Copy).then_inc(wqt_kept, 1)
                act.wait_ge(lin_in, LIN_LOADS * 16)
                act.wait_ge(lin_fill, 3)
                with act.Fori(0, GROUPS) as i:
                    front_act(act, i, lfront, None)
                    for c in range(CHUNKS + 1):
                        if c < CHUNKS:
                            act.wait_ge(q_ready, i * CHUNKS + c + 1)
                            if c >= 2:
                                act.wait_ge(c_ready, i * CHUNKS + c - 1)
                            act.activation(gq[:, c % 2, :], PB[c % 2][:, 0:TOK], ACT.Gelu,
                                           bias=lcol[:, 0, c % LG:c % LG + 1]).then_inc(gelu_done, 1)
                        if c >= 1:
                            b = c - 1
                            act.wait_ge(c_kept, i * CHUNKS + b + 1)
                            if b >= 2:
                                act.wait_ge(var_acc, i * CHUNKS + b - 1)
                            act.activation(sqb[:, b % 2, :], feat[:, b, :], ACT.Square).then_inc(sq_done, 1)
                    act.wait_ge(var_acc, i * CHUNKS + CHUNKS)
                    act.activation(qstd, PB[4][0:2 * CHUNKS, 0:TOK], ACT.Sqrt, bias=eps[0:2 * CHUNKS, :])\
                       .then_inc(std_ready, 1)
                    for c in range(CHUNKS + LG + 1):
                        p, g = c // LG, c % LG
                        if c < CHUNKS:
                            act.wait_ge(w_ready, i * CHUNKS + c + 1)
                            if p >= 2:
                                act.wait_ge(s_ready, i * CHUNKS + LG * (p - 1))
                            act.activation(upos[:, p % 2, g, :], feat[:, c, :], ACT.Relu,
                                           scale=lcol[:, 1, g:g + 1], bias=lcol[:, 2, g:g + 1]).then_inc(u_done, 1)
                            act.activation(uneg[:, p % 2, g, :], feat[:, c, :], ACT.Relu,
                                           scale=lcol[:, 3, g:g + 1], bias=lcol[:, 4, g:g + 1]).then_inc(u_done, 1)
                        n = c - LG
                        if 0 <= n < CHUNKS:
                            act.wait_ge(s_ready, i * CHUNKS + n + 1)
                            if n >= 2:
                                act.wait_ge(num_ready, i * CHUNKS + n - 1)
                            act.activation(scor[:, n % 2, :], PB[4 + n % 2][:, 0:2 * QQ], ACT.Copy).then_inc(st_done, 1)
                        n = c - LG - 1
                        if n >= 0:
                            act.wait_ge(den_ready, i * CHUNKS + n + 1)
                            if n >= 2:
                                act.wait_ge(rec_done, i * CHUNKS + n - 1)
                            act.activation(denb[:, n % 2, :], PB[7][:, 0:TOK], ACT.Identity, bias=neps[:, :])\
                               .then_inc(den_kept, 1)
                    for m in range(WM):
                        act.wait_ge(y_ready, i * WM + m + 1)
                        act.activation(y768[:, m, :], PB[m % 2][:, 0:TOK], ACT.Identity, bias=fcol[:, 0, m:m + 1])\
                           .then_inc(wf_free, 1)
                    act.wait_ge(yc_done, i + 1)
                    act.activation(ysq, y768, ACT.Square).then_inc(ysq_done, 1)
                    act.wait_ge(yvar_ready, i + 1)
                    act.activation(denb[:, 0, :], PB[3][:, 0:TOK], ACT.Sqrt, bias=eps[:, :]).then_inc(ystd_done, 1)
                    act.wait_ge(yn_done, i + 1)
                    for m in range(WM):
                        act.activation(compact(fused[:, m, :]), y768[:, m, :].rearrange("p (b q) -> p b q", q=PATCHES),
                                       ACT.Gelu, scale=fcol[:, 1, m:m + 1], bias=fcol[:, 2, m:m + 1]).then_inc(fused_done, 1)

            def attention_act(n, s):
                S, L = AS[n], ATT[n]
                act.wait_ge(*stage_done(s - 1))
                if s == 2:
                    act.wait_ge(late_in, 16 * LATE_LOADS)
                act.wait_ge(S["fill"], 2 * n + 2)
                with act.Fori(0, GROUPS) as i:
                    v = i + GROUPS * n
                    front_act(act, v, S, L["ln"])
                    for m in range(KC):
                        act.wait_ge(S["qk_p"], v * 4 + m + 1)
                        if n == 1:
                            last = act.activation(qT[:, m, :], PB[2 + m][0:FC, :], ACT.Identity, bias=qk_b[:, 0, m:m + 1])
                        else:
                            last = act.activation(qT[:, m, :], PB[2 + m][0:FC, :], ACT.Copy)
                        last.then_inc(S["q_sb"], 1)
                    for j in range(2):
                        act.wait_ge(S["v_p"], v * 2 + j + 1)
                        act.activation(vt[:, 2 * j:2 * j + 2, :], PB[4 + 3 * j][:, 0:2 * D].rearrange("p (t d) -> p t d", d=D),
                                       ACT.Copy).then_inc(S["v_sb"], 1)
                    for t in range(GT + 2):
                        if t < GT:
                            act.wait_ge(S["s_p"], v * GT + t + 1)
                            for b in (2, 3):
                                last = act.activation(sx[32 * b:32 * b + 32, t % 2, :, :],
                                                      psum_s[32 * b:32 * b + 32, :, 32 * b:32 * b + PATCHES], ACT.Copy)
                            last.then_inc(S["sx_act"], 1)
                            act.wait_ge(S["shifted"], v * GT + t + 1)
                            if t >= 2:
                                act.wait_ge(S["p_t"], v * GT + t - 1)
                            act.activation(pr[:, t % 2, :, 0:PATCHES], sx[:, t % 2, :, :], ACT.Exp).then_inc(S["exp_done"], 1)
                        if t >= 2:
                            u = t - 2
                            act.wait_ge(S["oT_p"], v * GT + u + 1)
                            if u >= 1:
                                act.wait_ge(S["y_p"], v * GT + u)
                            act.activation(aoT[:, :, :], PB[0][0:FC, 0:2 * 128].rearrange("p (k n) -> p k n", n=128),
                                           ACT.Copy).then_inc(S["oT_sb"], 1)

            def moe_act(n, s):
                S, L = MS[n], MOE[n]
                ny = E + L["biased"]
                act.wait_ge(*stage_done(s - 1))
                with act.Fori(0, GROUPS) as i:
                    v = i + GROUPS * n
                    front_act(act, v, S, L["ln"])
                    act.wait_ge(S["shifted"], v + 1)
                    act.activation(lexp[:, :, :], lexp[:, :, :], ACT.Exp).then_inc(S["exp_done"], 1)
                    for e in range(E):
                        if e == 1 and L["biased"]:
                            act.wait_ge(S["cwT_p"], v + 1)
                            act.activation(cwT[:, :], PB[3][0:E, :], ACT.Copy).then_inc(S["cwT_sb"], 1)
                        if e >= 2:
                            act.wait_ge(S["y_p"], i * ny + e - 1 + L["biased"])
                        for m in range(FM):
                            k = e * FM + m
                            act.wait_ge(S["h_p"], v * (E * FM) + k + 1)
                            act.activation(he[:, e % 2, m, :, 0:PATCHES],
                                           PB[k % 2][:, 0:TOK].rearrange("p (b q) -> p b q", q=PATCHES), ACT.Gelu,
                                           bias=bias1[:, k:k + 1] if L["biased"] else 0.0).then_inc(S["h_act"], 1)

            for s, (what, n) in enumerate(PLAN, 2):
                if stages > s:
                    (attention_act if what == "att" else moe_act)(n, s)
            if stages < 2:
                act.wait_ge(ident_in, 16)

        @block.vector
        def _(dve):
            dve.memset(half[:, :], -0.5).then_inc(fills, 1)
            dve.memset(eps[:, :], EPS).then_inc(fills, 1)
            dve.memset(neps[:, :], NORM_EPS).then_inc(fills, 1)
            dve.wait_ge(conv_in, 48)
            dve.tensor_tensor(posb[:, :], posb[:, :], xn[:, 0, :], ALU.add).then_inc(fills, 1)
            dve.wait_ge(fills, 4)
            dve.sem_inc(emb_free, 2)
            with dve.Fori(0, GROUPS) as i:
                for t in range(GT):
                    dve.wait_ge(emb_ready, i * GT + t + 1)
                    dve.tensor_tensor(hid[:, bass.ds(i * GT + t, 1), :], PB[t % 2][:, 0:D], posb[:, :], ALU.add)\
                       .then_inc(emb_free, 1)
            if stages >= 2:
                dve.wait_ge(lin_in, LIN_LOADS * 16)
                dve.tensor_scalar(lcol[:, 3:5, :], lcol[:, 1:3, :], -1.0, None, ALU.mult).then_inc(lin_fill, 1)
                dve.wait_ge(lin_fill, 3)
                dve.wait_ge(*stage_done(0))
                dve.wait_ge(wqt_kept, CHUNKS * KC)
                with dve.Fori(0, GROUPS) as i:
                    front_dve(dve, i, lfront, hid, False)
                    for c in range(CHUNKS):
                        dve.wait_ge(c_ready, i * CHUNKS + c + 1)
                        dve.tensor_copy(feat[:, c, :], PB[2 + c % 2][:, 0:TOK]).then_inc(c_kept, 1)
                    dve.wait_ge(std_ready, i + 1)
                    dve.reciprocal(qrstd[:, :], qstd).then_inc(rstd_ready, 1)
                    for c in range(CHUNKS + LG + 1):
                        p, g = c // LG, c % LG
                        if c < CHUNKS:
                            dve.wait_ge(rb_ready, i * CHUNKS + c + 1)
                            dve.tensor_tensor(feat[:, c, :], feat[:, c, :], PB[c % 2][:, 0:TOK], ALU.mult)\
                               .then_inc(w_ready, 1)
                        n = c - LG
                        if 0 <= n < CHUNKS:
                            dve.wait_ge(v_ready, i * CHUNKS + n + 1)
                            if n >= 2:
                                dve.wait_ge(num_ready, i * CHUNKS + n - 1)
                            dve.tensor_tensor(
                                vblk[:, n % 2, :, :, :],
                                PB[3][:, 0:256].rearrange("p (j m) -> p j m", m=128).unsqueeze(2).to_broadcast([128, 2, 2, 128]),
                                v_mask[:, :, :].unsqueeze(1).to_broadcast([128, 2, 2, 128]), ALU.mult).then_inc(vblk_done, 1)
                        n = c - LG - 1
                        if n >= 0:
                            dve.wait_ge(den_kept, i * CHUNKS + n + 1)
                            if n >= 1:
                                dve.wait_ge(out_done, i * CHUNKS + n)
                            dve.reciprocal(rec[:, :], denb[:, n % 2, :]).then_inc(rec_done, 1)
                            dve.wait_ge(rec_done, i * CHUNKS + n + 1)
                            dve.wait_ge(num_ready, i * CHUNKS + n + 1)
                            pp, bg = n // LG, n % LG
                            for b2 in range(2):
                                dst = feat[:, LG * pp:LG * pp + LG, :].rearrange(
                                    "p g (n j b q) -> p n b j g q", j=2, b=2, q=PATCHES)[:, bg, b2, :, :, :]
                                half_cols = slice(2 * QQ * b2, 2 * QQ * b2 + 2 * QQ)
                                last = dve.tensor_tensor(
                                    dst, PB[6][:, half_cols].rearrange("p (j g q) -> p j g q", j=2, g=LG),
                                    rec[:, half_cols].rearrange("p (j g q) -> p j g q", j=2, g=LG), ALU.mult)
                            last.then_inc(out_done, 1)
                        if g == LG - 1 and p < PAIRS:
                            dve.wait_ge(k_ready, i * PAIRS + p + 1)
                            if p >= 1:
                                dve.wait_ge(s_ready, i * CHUNKS + LG * p)
                            kin = PB[2][:, 0:TOK].rearrange("p (b q) -> p b q", q=PATCHES).unsqueeze(2)\
                                .to_broadcast([128, GI, 2, PATCHES])
                            for slot in range(2):
                                for dst, op, sign in ((kpos, ALU.max, 0), (kneg, ALU.min, 1)):
                                    last = dve.tensor_scalar(
                                        dst[:, :, slot, 0:PATCHES], PB[2][:, 0:TOK].rearrange("p (b q) -> p b q", q=PATCHES),
                                        0.0, slot_mask[:, sign, slot:slot + 1], op, ALU.mult)
                                    last.then_inc(kpm_done, 1)
                    dve.wait_ge(mean_ready, i + 1)
                    dve.tensor_tensor(y768, y768, PB[2][:, 0:TOK].unsqueeze(1).to_broadcast([128, WM, TOK]), ALU.subtract)\
                       .then_inc(yc_done, 1)
                    dve.wait_ge(ystd_done, i + 1)
                    dve.reciprocal(rec[:, :], denb[:, 0, :]).then_inc(yrec_done, 1)
                    dve.wait_ge(yrec_done, i + 1)
                    dve.tensor_tensor(y768, y768, rec[:, :].unsqueeze(1).to_broadcast([128, WM, TOK]), ALU.mult)\
                       .then_inc(yn_done, 1)
                    for t in range(GT):
                        tile = hid[:, bass.ds(i * GT + t, 1), :]
                        dve.wait_ge(z_ready, i * GT + t + 1)
                        dve.tensor_tensor(tile, tile, PB[4 + t % 2][:, 0:D], ALU.add).then_inc(z_added, 1)
                        dve.wait_ge(z_added, i * GT + t + 1)
                        dve.tensor_tensor(tile, tile, bob[:, :], ALU.add).then_inc(hid_done, 1)

            def attention_dve(n, s):
                S, L = AS[n], ATT[n]
                dve.wait_ge(*stage_done(s - 1))
                if s == 2:
                    dve.wait_ge(late_in, 16 * LATE_LOADS)
                dve.wait_ge(S["fill"], 2 * n + 2)
                base = xres if L["double"] else hid
                with dve.Fori(0, GROUPS) as i:
                    v = i + GROUPS * n
                    front_dve(dve, i, S, hid, L["double"])
                    for m in range(KC):
                        dve.wait_ge(S["qk_p"], v * 4 + KC + m + 1)
                        for j in range(HPC):
                            last = dve.tensor_scalar(kexp[:, m, j, :], PB[5 + m][0:FC, :],
                                                     qk_b[:, 1, m:m + 1] if n == 1 else 0.0, head_mask[:, j:j + 1],
                                                     ALU.add, ALU.mult)
                        last.then_inc(S["k_sb"], 1)
                    ch = Chain(dve, S["chain"], i, GT * (4 + L["causal"] + (n == 1) + (n < 2)))
                    for t in range(GT + 3):
                        if t < GT:
                            dve.wait_ge(S["s_p"], v * GT + t + 1)
                            for b in (0, 1):
                                last = dve.tensor_copy(sx[32 * b:32 * b + 32, t % 2, :, :],
                                                       psum_s[32 * b:32 * b + 32, :, 32 * b:32 * b + PATCHES])
                            ch.step(last)
                            ch.wait()
                            dve.wait_ge(S["sx_act"], v * GT + t + 1)
                            if L["causal"]:
                                ch.step(dve.tensor_tensor(sx[:, t % 2, :, :], sx[:, t % 2, :, :],
                                                          causal[:, :].unsqueeze(1).to_broadcast([128, H, PATCHES]), ALU.add))
                                ch.wait()
                            ch.step(dve.tensor_reduce(smax[:, :], sx[:, t % 2, :, :], AX.X, ALU.max))
                            ch.wait()
                            dve.tensor_tensor(sx[:, t % 2, :, :], sx[:, t % 2, :, :],
                                              smax[:, :].unsqueeze(2).to_broadcast([128, H, PATCHES]), ALU.subtract)\
                               .then_inc(S["shifted"], 1)
                        if 1 <= t <= GT:
                            u = t - 1
                            dve.wait_ge(S["o_p"], v * GT + u + 1)
                            if u >= 2:
                                dve.wait_ge(S["oT_p"], v * GT + u - 1)
                            full = psum_o[:, :, :]
                            diag = bass.AP(full.tensor, full.offset, [full.ap[0], [HPC * 128, KC], [128 + HD, HPC], [1, HD]])
                            last = dve.tensor_tensor(
                                ao[:, u % 2, :].rearrange("p (c j x) -> p c j x", c=KC, x=HD), diag,
                                srec[:, u % 2, :].rearrange("p (c j) -> p c j", c=KC).unsqueeze(3)
                                .to_broadcast([128, KC, HPC, HD]), ALU.mult)
                            if n == 1:
                                ch.step(last)
                                ch.wait()
                                last = dve.tensor_tensor(ao[:, u % 2, :], ao[:, u % 2, :], v_b[:, :], ALU.add)
                            last.then_inc(S["ao_done"], 1)
                        if t < GT:
                            dve.wait_ge(S["exp_done"], v * GT + t + 1)
                            ch.step(dve.tensor_reduce(ssum[:, :], pr[:, t % 2, :, 0:PATCHES], AX.X, ALU.add))
                            ch.wait()
                            ch.step(dve.reciprocal(srec[:, t % 2, :], ssum[:, :]))
                            ch.wait()
                            if t >= 2:
                                dve.wait_ge(S["o_p"], v * GT + t - 1)
                            for b in range(PER_TILE):
                                last = dve.transpose(pT[32 * b:32 * b + 32, t % 2, :, 32 * b:32 * b + 32],
                                                     pr[32 * b:32 * b + 32, t % 2, :, :])
                            last.then_inc(S["p_t"], 1)
                        if t >= 3:
                            u = t - 3
                            tile = base[:, bass.ds(i * GT + u, 1), :]
                            dve.wait_ge(S["y_p"], v * GT + u + 1)
                            last = dve.tensor_tensor(tile, tile, PB[1][:, 0:D], ALU.add)
                            if n < 2:
                                ch.step(last)
                                ch.wait()
                                last = dve.tensor_tensor(tile, tile, proj_b[n][:, :], ALU.add)
                            last.then_inc(S["y_done"], 1)
                    ch.end()

            def moe_dve(n, s):
                S, L = MS[n], MOE[n]
                ny = E + L["biased"]
                dve.wait_ge(*stage_done(s - 1))
                with dve.Fori(0, GROUPS) as i:
                    v = i + GROUPS * n
                    front_dve(dve, i, S, xres, False)
                    ch = Chain(dve, S["chain"], v, 10)
                    dve.wait_ge(S["g_p"], v + 1)
                    logits = PB[2][:, 0:GT * E].rearrange("p (t e) -> p t e", e=E)
                    if L["biased"]:
                        last = dve.tensor_tensor(lg[:, :, :], logits, gate_b[:, :].unsqueeze(1).to_broadcast([128, GT, E]), ALU.add)
                    else:
                        last = dve.tensor_copy(lg[:, :, :], logits)
                    ch.step(last)
                    ch.wait()
                    ch.step(dve.tensor_reduce(lmax[:, :], lg[:, :, :], AX.X, ALU.max))
                    ch.wait()
                    dve.tensor_tensor(lexp[:, :, :], lg[:, :, :], lmax[:, :].unsqueeze(2).to_broadcast([128, GT, E]), ALU.subtract)\
                       .then_inc(S["shifted"], 1)
                    other = lg[:, :, :].unsqueeze(2).to_broadcast([128, GT, E, E])
                    own = lg[:, :, :].unsqueeze(3).to_broadcast([128, GT, E, E])
                    ch.step(dve.tensor_tensor(gtr[:, :, :, :], other, own, ALU.is_gt))
                    ch.step(dve.tensor_tensor(eqr[:, :, :, :], other, own, ALU.is_equal))
                    ch.wait()
                    ch.step(dve.tensor_tensor(eqr[:, :, :, :], eqr[:, :, :, :], before[:, :, :].unsqueeze(1).to_broadcast([128, GT, E, E]), ALU.mult))
                    ch.wait()
                    ch.step(dve.tensor_tensor(gtr[:, :, :, :], gtr[:, :, :, :], eqr[:, :, :, :], ALU.add))
                    ch.wait()
                    ch.step(dve.tensor_reduce(rank[:, :, :], gtr[:, :, :, :], AX.X, ALU.add))
                    ch.wait()
                    dve.wait_ge(S["exp_done"], v + 1)
                    ch.step(dve.scalar_tensor_tensor(picked[:, :, :], rank[:, :, :], 1.5, lexp[:, :, :], ALU.is_lt, ALU.mult))
                    ch.wait()
                    ch.step(dve.tensor_reduce(lsum[:, :], picked[:, :, :], AX.X, ALU.add))
                    ch.wait()
                    ch.step(dve.reciprocal(lrec[:, :], lsum[:, :]))
                    ch.wait()
                    dve.tensor_tensor(cw[:, :, :], picked[:, :, :], lrec[:, :].unsqueeze(2).to_broadcast([128, GT, E]), ALU.mult)\
                       .then_inc(S["cw_ready"], 1)
                    dve.wait_ge(S["cw_ready"], v + 1)
                    ch.end()
                    for q in range(ny):
                        e = q - L["biased"]
                        dve.wait_ge(S["y_p"], i * ny + q + 1)
                        if q >= 1:
                            dve.wait_ge(S["y_acc"], i * ny + q)
                        for t in range(GT):
                            tile = xres[:, bass.ds(i * GT + t, 1), :]
                            part = PB[4 + 2 * (q % 2) + t // 2][:, D * (t % 2):D * (t % 2) + D]
                            if e < 0:
                                last = dve.tensor_tensor(tile, tile, part, ALU.add)
                            else:
                                last = dve.scalar_tensor_tensor(tile, part, cw[:, t, e:e + 1], tile, ALU.mult, ALU.add)
                        last.then_inc(S["y_acc"], 1)
                    dve.wait_ge(S["y_acc"], i * ny + ny)
                    for t in range(GT):
                        tile = hid[:, bass.ds(i * GT + t, 1), :]
                        last = dve.tensor_tensor(tile, tile, xres[:, bass.ds(i * GT + t, 1), :], ALU.add)
                    last.then_inc(S["done"], 1)

            for s, (what, n) in enumerate(PLAN, 2):
                if stages > s:
                    (attention_dve if what == "att" else moe_dve)(n, s)

        @block.tensor
        def _(pe):
            pe.wait_ge(conv_in, 48)
            with pe.Fori(0, GROUPS) as i:
                for t in range(GT):
                    pe.wait_ge(patch_in[t], i * 16 + 16)
                    pe.wait_ge(emb_free, i * GT + t + 1)
                    for k in range(PK):
                        last = pe.matmul(PB[t % 2][:, 0:D], patch_t[:, t, k, :], conv_w[:, k, :],
                                         start=(k == 0), stop=(k == PK - 1))
                    last.then_inc(emb_ready, 1)
            pe.wait_ge(ident_in, 16)
            if stages >= 2:
                pe.wait_ge(*stage_done(0))
                pe.wait_ge(wq_in, 32)
                for c in range(CHUNKS):
                    for k in range(KC):
                        n = c * KC + k
                        if n >= 4:
                            pe.wait_ge(wqt_kept, n - 3)
                        pe.matmul(PB[n % 4][0:FC, 0:128], wqT[:, c, FC * k:FC * k + FC], wt2[:, c % LG, :],
                                  start=True, stop=True).then_inc(wqt_ready, 1)
                pe.wait_ge(wqt_kept, CHUNKS * KC)
                pe.wait_ge(lin_in, LIN_LOADS * 16)
                with pe.Fori(0, GROUPS) as i:
                    front_pe(pe, i, lfront, False)
                    pe.wait_ge(lfront["xTs"], i * 2 + 2)
                    for s in range(CHUNKS + 2):
                        if s < CHUNKS:
                            if s >= 2:
                                pe.wait_ge(gelu_done, i * CHUNKS + s - 1)
                            for k in range(KC):
                                last = pe.matmul(PB[s % 2][:, 0:TOK], wqt[:, k, s, :], compact(xT[:, k, :]),
                                                 start=(k == 0), stop=(k == KC - 1))
                            last.then_inc(q_ready, 1)
                        if 1 <= s <= CHUNKS:
                            c = s - 1
                            pe.wait_ge(gelu_done, i * CHUNKS + c + 1)
                            if c >= 2:
                                pe.wait_ge(c_kept, i * CHUNKS + c - 1)
                            pe.matmul(PB[2 + c % 2][:, 0:TOK], center[:, :], gq[:, c % 2, :], start=True, stop=True)\
                              .then_inc(c_ready, 1)
                        if s >= 2:
                            c = s - 2
                            pe.wait_ge(sq_done, i * CHUNKS + c + 1)
                            pe.matmul(PB[4][0:2 * CHUNKS, 0:TOK], var_pick[:, c, :], sqb[:, c % 2, :],
                                      start=(c == 0), stop=(c == CHUNKS - 1)).then_inc(var_acc, 1)
                    for c in range(CHUNKS + LG + 1):
                        p, g = c // LG, c % LG
                        if c < CHUNKS:
                            if c == 0:
                                pe.wait_ge(rstd_ready, i + 1)
                            if c >= 2:
                                pe.wait_ge(w_ready, i * CHUNKS + c - 1)
                            pe.matmul(PB[c % 2][:, 0:TOK], rstd_pick[:, c, :], qrstd[:, :], start=True, stop=True)\
                              .then_inc(rb_ready, 1)
                            if g == 1:
                                if p >= 1:
                                    pe.wait_ge(kpm_done, i * (4 * PAIRS) + 4 * p)
                                for k in range(KC):
                                    last = pe.matmul(PB[2][:, 0:TOK], wk[:, k, 128 * p:128 * p + 128], compact(xT[:, k, :]),
                                                     start=(k == 0), stop=(k == KC - 1))
                                last.then_inc(k_ready, 1)
                        n = c - LG
                        if 0 <= n < CHUNKS:
                            pp, bg = n // LG, n % LG
                            if n >= 1:
                                pe.wait_ge(vblk_done, i * CHUNKS + n)
                            if n == 0:
                                pe.wait_ge(xdup_done, i * 2 + 2)
                            for j in range(2):
                                for k in range(KC):
                                    b = PER_TILE * bg + 2 * j
                                    image = xdup[:, k, b:b + 2, :, :]
                                    last = pe.matmul(PB[3][:, 128 * j:128 * j + 128], image, wv[:, k, 128 * pp:128 * pp + 128],
                                                     start=(k == 0), stop=(k == KC - 1))
                            last.then_inc(v_ready, 1)
                            if n >= 2:
                                pe.wait_ge(st_done, i * CHUNKS + n - 1)
                            if bg == 0:
                                pe.wait_ge(kpm_done, i * (4 * PAIRS) + 4 * pp + 4)
                                pe.wait_ge(u_done, i * (2 * CHUNKS) + 8 * pp + 8)
                            for j in range(2):
                                for b2 in range(2):
                                    b = PER_TILE * bg + 2 * j + b2
                                    dst = PB[4 + n % 2][64 * b2:64 * b2 + 64, QQ * j:QQ * j + QQ]
                                    pe.matmul(dst, kpos[:, b, :, :], upos[:, pp % 2, :, PATCHES * b:PATCHES * b + PATCHES],
                                              start=True, stop=False)
                                    last = pe.matmul(dst, kneg[:, b, :, :], uneg[:, pp % 2, :, PATCHES * b:PATCHES * b + PATCHES],
                                                     start=False, stop=True)
                            last.then_inc(s_ready, 1)
                        n = c - LG - 1
                        if n >= 0:
                            pe.wait_ge(st_done, i * CHUNKS + n + 1)
                            if n >= 1:
                                pe.wait_ge(den_kept, i * CHUNKS + n)
                                pe.wait_ge(out_done, i * CHUNKS + n)
                            for b2 in range(2):
                                last = pe.matmul(PB[7][:, 2 * QQ * b2:2 * QQ * b2 + 2 * QQ], den_sum[:, b2, :], scor[:, n % 2, :],
                                                 start=True, stop=True)
                            last.then_inc(den_ready, 1)
                            pe.wait_ge(vblk_done, i * CHUNKS + n + 1)
                            for b2 in range(2):
                                for j in range(2):
                                    col = 2 * QQ * b2 + QQ * j
                                    last = pe.matmul(PB[6][:, col:col + QQ], vblk[:, n % 2, j, b2, :],
                                                     scor[:, n % 2, QQ * j:QQ * j + QQ], start=True, stop=True)
                            last.then_inc(num_ready, 1)
                    pe.wait_ge(out_done, i * CHUNKS + CHUNKS)
                    for m in range(WM):
                        pe.wait_ge(wf_in[m % 2], i * (16 * WM // 2) + 16 * (m // 2) + 16)
                        if m >= 2:
                            pe.wait_ge(wf_free, i * WM + m + 1)
                        for c in range(CHUNKS):
                            last = pe.matmul(PB[m % 2][:, 0:TOK], wfs[m % 2][:, c, :], feat[:, c, :],
                                             start=(c == 0), stop=(c == CHUNKS - 1))
                        last.then_inc(y_ready, 1)
                    pe.wait_ge(wf_free, i * WM + WM + 2)
                    for m in range(WM):
                        last = pe.matmul(PB[2][:, 0:TOK], mean768[:, :], y768[:, m, :], start=(m == 0), stop=(m == WM - 1))
                    last.then_inc(mean_ready, 1)
                    pe.wait_ge(ysq_done, i + 1)
                    for m in range(WM):
                        last = pe.matmul(PB[3][:, 0:TOK], mean768[:, :], ysq[:, m, :], start=(m == 0), stop=(m == WM - 1))
                    last.then_inc(yvar_ready, 1)
                    pe.wait_ge(fused_done, i * WM + WM)
                    for t in range(GT):
                        if t >= 2:
                            pe.wait_ge(z_added, i * GT + t - 1)
                        for m in range(WM):
                            last = pe.matmul(PB[4 + t % 2][:, 0:D], fused[:, m, 128 * t:128 * t + 128], wo[:, m, :],
                                             start=(m == 0), stop=(m == WM - 1))
                        last.then_inc(z_ready, 1)

            def attention_pe(n, s):
                S, L = AS[n], ATT[n]
                pe.wait_ge(*stage_done(s - 1))
                if s == 2:
                    pe.wait_ge(late_in, 16 * LATE_LOADS)
                pe.wait_ge(S["fill"], 2 * n + 2)
                with pe.Fori(0, GROUPS) as i:
                    v = i + GROUPS * n
                    front_pe(pe, i, S, L["double"])
                    pe.wait_ge(S["xTs"], v * 2 + 2)
                    for j in range(2 * KC):
                        dst = PB[(2, 3, 5, 6)[j]][0:FC, :]
                        for k in range(KC):
                            last = pe.matmul(dst, qkv_w[n][:, k, FC * j:FC * j + FC], xT[:, k, :],
                                             start=(k == 0), stop=(k == KC - 1))
                        last.then_inc(S["qk_p"], 1)
                    for t in range(GT):
                        for k in range(KC):
                            last = pe.matmul(PB[4 + 3 * (t // 2)][:, D * (t % 2):D * (t % 2) + D], xT[:, k, 128 * t:128 * t + 128],
                                             qkv_w[n][:, k, 2 * D:3 * D], start=(k == 0), stop=(k == KC - 1))
                        if t % 2:
                            last.then_inc(S["v_p"], 1)
                    for t in range(GT + 3):
                        if t < GT:
                            if t == 0:
                                pe.wait_ge(S["q_sb"], v * KC + KC)
                                pe.wait_ge(S["k_sb"], v * KC + KC)
                                pe.wait_ge(S["v_sb"], v * 2 + 2)
                            else:
                                pe.wait_ge(S["sx_act"], v * GT + t)
                                pe.wait_ge(S["shifted"], v * GT + t)
                            for m, h0, nh in ((0, 0, 4), (0, 4, 2), (1, 0, 2), (1, 2, 4)):
                                last = pe.matmul(psum_s[:, HPC * m + h0:HPC * m + h0 + nh, :], qT[:, m, 128 * t:128 * t + 128],
                                                 kexp[:, m, h0:h0 + nh, 128 * t:128 * t + 128], start=True, stop=True)
                            last.then_inc(S["s_p"], 1)
                        if 1 <= t <= GT:
                            u = t - 1
                            pe.wait_ge(S["p_t"], v * GT + u + 1)
                            if u >= 1:
                                pe.wait_ge(S["ao_done"], v * GT + u)
                            for h in range(H):
                                m = h // HPC
                                last = pe.matmul(psum_o[:, h, 0:FC], pT[:, u % 2, h, :], vt[:, u, FC * m:FC * m + FC],
                                                 start=True, stop=True)
                            last.then_inc(S["o_p"], 1)
                        if 2 <= t <= GT + 1:
                            u = t - 2
                            pe.wait_ge(S["ao_done"], v * GT + u + 1)
                            if u >= 1:
                                pe.wait_ge(S["oT_sb"], v * GT + u)
                            for k in range(KC):
                                last = pe.transpose(PB[0][0:FC, 128 * k:128 * k + 128], ao[:, u % 2, FC * k:FC * k + FC], ident[:, :])
                            last.then_inc(S["oT_p"], 1)
                        if t >= 3:
                            u = t - 3
                            pe.wait_ge(S["oT_sb"], v * GT + u + 1)
                            if u >= 1:
                                pe.wait_ge(S["y_done"], v * GT + u)
                            for k in range(KC):
                                last = pe.matmul(PB[1][:, 0:D], aoT[:, k, :], proj_w[n][:, k, :], start=(k == 0), stop=(k == KC - 1))
                            last.then_inc(S["y_p"], 1)

            def moe_pe(n, s):
                S, L = MS[n], MOE[n]
                ny = E + L["biased"]
                pe.wait_ge(*stage_done(s - 1))
                pe.wait_ge(S["w_in"], 48)
                pe.wait_ge(S["fill"], n + 1)
                with pe.Fori(0, GROUPS) as i:
                    v = i + GROUPS * n
                    front_pe(pe, i, S, False)
                    pe.wait_ge(S["xTs"], v * 2 + 2)
                    for t in range(GT):
                        for k in range(KC):
                            last = pe.matmul(PB[2][:, E * t:E * t + E], xT[:, k, 128 * t:128 * t + 128], gate_w[:, k, :],
                                             start=(k == 0), stop=(k == KC - 1))
                    last.then_inc(S["g_p"], 1)

                    def second(e):
                        q = e + L["biased"]
                        if q >= 2:
                            pe.wait_ge(S["y_acc"], i * ny + q - 1)
                        if e >= 0:
                            pe.wait_ge(S["h_act"], v * (E * FM) + e * FM + FM)
                        for t in range(GT):
                            dst = PB[4 + 2 * (q % 2) + t // 2][:, D * (t % 2):D * (t % 2) + D]
                            if e < 0:
                                last = pe.matmul(dst, cwT[:, 128 * t:128 * t + 128], bias2[:, :], start=True, stop=True)
                                continue
                            for m in range(FM):
                                tok = he[:, e % 2, m, PER_TILE * t:PER_TILE * t + PER_TILE, :]
                                last = pe.matmul(dst, tok, w2[:, e, m, :], start=(m == 0), stop=(m == FM - 1))
                        last.then_inc(S["y_p"], 1)

                    for e in range(E):
                        for m in range(FM):
                            k2 = e * FM + m
                            if k2 >= 2:
                                pe.wait_ge(S["h_act"], v * (E * FM) + k2 - 1)
                            for k in range(KC):
                                last = pe.matmul(PB[k2 % 2][:, 0:TOK], w1[:, k, e, 128 * m:128 * m + 128], compact(xT[:, k, :]),
                                                 start=(k == 0), stop=(k == KC - 1))
                            last.then_inc(S["h_p"], 1)
                        if e == 0 and L["biased"]:
                            pe.wait_ge(S["cw_ready"], v + 1)
                            for t in range(GT):
                                last = pe.transpose(PB[3][0:E, 128 * t:128 * t + 128], cw[:, t, :], ident[:, :])
                            last.then_inc(S["cwT_p"], 1)
                        elif e == 1 and L["biased"]:
                            pe.wait_ge(S["cwT_sb"], v + 1)
                            second(-1)
                        if e >= 1:
                            second(e - 1)
                    second(E - 1)

            for s, (what, n) in enumerate(PLAN, 2):
                if stages > s:
                    (attention_pe if what == "att" else moe_pe)(n, s)


PLAN = [("att", 0), ("moe", 0), ("att", 1), ("att", 2), ("moe", 1)]
LIN_LOADS = 17
LATE_LOADS = 20


def layout(x):
    def chunks(w, size):
        return w.reshape(w.shape[0] // size, size, -1).transpose(1, 0, 2).reshape(size, -1)

    def cols(v, size):
        return v.reshape(-1, size).T

    zeros = np.zeros
    f4 = np.float32
    a = {}
    pt = x["x"][:, :, :80, :80].reshape(IMAGES, 3, 5, 16, 5, 16).transpose(1, 3, 5, 0, 2, 4)
    padded = zeros((PATCH_K, IMAGES, PITCH), f4)
    padded[:, :, :PATCHES] = pt.reshape(PATCH_K, IMAGES, PATCHES)
    a["patches"] = padded.reshape(PK, 128, TILES, 128).transpose(2, 1, 0, 3).reshape(TILES, 128, PATCH_K)
    a["conv_w"] = chunks(x["L0_tok_conv_w"].reshape(D, PATCH_K).T, 128)
    a["conv_b"] = x["L0_tok_conv_b"][None]
    ids = np.searchsorted(np.arange(1 / 32, 1, 1 / 32, dtype=f4), np.arange(0, 1 - 1e-6, 1 / 5, dtype=f4), side="right")
    rows = (ids[:, None] * 32 + ids).reshape(-1)
    pos = zeros((PER_TILE, PITCH, D), f4)
    pos[:, :PATCHES] = x["L0_tok_pos_table"][rows]
    a["pos"] = pos.reshape(128, D)
    a["wk"], a["wv"] = chunks(x["L0_attn_Wk"], FC), chunks(x["L0_attn_Wv"], FC)
    wq = x["L0_attn_Wq"].reshape(LG, D, PAIRS, 128).transpose(3, 2, 0, 1)
    a["wqT"] = wq.reshape(128, CHUNKS * D)
    wt = zeros((2, LD, LG, 2, LD), f4)
    for h in range(2):
        wt[h, :, :, h, :] = x["L0_attn_Wt"].transpose(1, 0, 2)
    a["wt2"] = wt.reshape(128, LG * 128)
    for n in ("bt", "gt", "betat"):
        a[n + "2"] = np.concatenate([x["L0_attn_" + n].T] * 2, 0)
    wf = x["L0_attn_Wf"].reshape(LG, PAIRS, 128, WM, 128).transpose(3, 2, 1, 0, 4)
    a["wf"] = wf.reshape(WM, 128, CHUNKS * 128)
    a["bf"], a["gf"], a["betaf"] = (cols(x["L0_attn_" + n], 128) for n in ("bf", "gf", "betaf"))
    a["wo"], a["bo"] = chunks(x["L0_attn_Wo"], 128), x["L0_attn_bo"][None]
    a["ident"] = np.eye(128, dtype=f4)
    same = np.kron(np.eye(2), np.ones((LD, LD))).astype(f4)
    a["center"] = (np.eye(128) - same / LD).astype(f4)
    a["mean768"] = np.full((128, 128), 1 / INNER, f4)
    den = zeros((2, 2, PITCH, 2, 2, LD), f4)
    for b in range(2):
        for h in range(2):
            den[b, h, :, b, h] = 1
    a["den_sum"] = den.reshape(128, 2 * 128)
    a["v_mask"] = a["den_sum"]
    pick = zeros((2, LD, CHUNKS, CHUNKS, 2), f4)
    for c in range(CHUNKS):
        for h in range(2):
            pick[h, :, c, c, h] = 1 / LD
    a["var_pick"] = pick.reshape(128, CHUNKS * 2 * CHUNKS)
    a["rstd_pick"] = (pick.transpose(3, 4, 2, 0, 1).reshape(2 * CHUNKS, CHUNKS * 128) != 0).astype(f4)
    slot = np.kron(np.eye(2), np.ones((LD, 1))).astype(f4)
    a["slot_mask"] = np.concatenate([slot, -slot], 1)
    a["head_mask"] = (np.kron(np.eye(HPC), np.ones((HD, 1))) * HD ** -0.5).astype(f4)
    after = np.arange(PATCHES)[None] > np.arange(PITCH)[:, None]
    a["causal"] = np.tile(np.where(after, f4(-1e30), f4(0)), (PER_TILE, 1))
    a["before"] = np.tile((np.arange(E)[None] < np.arange(E)[:, None]).astype(f4).reshape(1, -1), (128, 1))
    a["a0_qkv"], a["a0_proj"] = chunks(x["L0_ffn_qkv_w"].T, FC), chunks(x["L0_ffn_proj_w"].T, FC)
    a["a1_qkv"], a["a1_proj"] = chunks(x["L1_attn_W_attn"], FC), chunks(x["L1_attn_W_proj"], FC)
    a["a2_qkv"], a["a2_proj"] = chunks(x["L1_ffn_Wqkv"], FC), chunks(x["L1_ffn_Wproj"], FC)
    a["a0_projb"], a["a1_projb"] = x["L0_ffn_proj_b"][None], x["L1_attn_b_proj"][None]
    a["a1_qkb"], a["a1_vb"] = cols(x["L1_attn_b_attn"][:2 * D], FC), x["L1_attn_b_attn"][None, 2 * D:]
    for m, pre in (("m0", "L0_ffn_"), ("m1", "L1_ffn_")):
        for n in ("ln1", "ln2"):
            a[f"{m}_{n}"] = np.concatenate([cols(x[f"{pre}{n}_g"], FC), cols(x[f"{pre}{n}_b"], FC)], 1)
    a["m0_gate"], a["m1_gate"] = chunks(x["L0_ffn_gate_w"].T, FC), chunks(x["L1_ffn_Wrouter"], FC)
    w1 = {"m0": x["L0_ffn_w1"].transpose(2, 0, 1), "m1": x["L1_ffn_W1"].transpose(1, 0, 2)}
    w2 = {"m0": x["L0_ffn_w2"].transpose(0, 2, 1), "m1": x["L1_ffn_W2"]}
    for m in ("m0", "m1"):
        a[f"{m}_w1"] = chunks(w1[m].reshape(D, E * FF), FC)
        a[f"{m}_w2"] = w2[m].reshape(E, FM, 128, D).transpose(2, 0, 1, 3).reshape(128, E * FM * D)
    a["m0_gateb"], a["m0_b2"] = x["L0_ffn_gate_b"][None], x["L0_ffn_b2"]
    a["m0_b1"] = x["L0_ffn_b1"].reshape(E, FM, 128).transpose(2, 0, 1).reshape(128, E * FM)
    return a


def program(nc, stages=7):
    dram = {n: nc.dram_tensor(n, tuple(s), F32, kind="ExternalInput").ap() for n, s in load_shapes().items()}
    out = nc.dram_tensor("out", (TILES, 128, D), F32, kind="ExternalOutput").ap()
    build(nc, dram, out, stages)


def kernel(**inputs):
    import concourse.bacc as bacc
    from concourse.bass_utils import run_bass_kernel_spmd

    nc = bacc.Bacc("TRN2", target_bir_lowering=False, num_devices=1)
    program(nc)
    x = {n: np.asarray(v) for n, v in inputs.items()}
    arrays = {n: np.ascontiguousarray(v) for n, v in layout(x).items()}
    r = run_bass_kernel_spmd(nc, [arrays], core_ids=[0])
    got = np.asarray(r.results[0]["out"])
    return got.reshape(IMAGES, PITCH, D)[:, :PATCHES]
```

```python
from contextlib import ExitStack

import concourse.bass as bass
import concourse.mybir as mybir
import numpy as np
from concourse.alu_op_type import AluOpType as ALU

ACT = mybir.ActivationFunctionType
AX = mybir.AxisListType
F32 = mybir.dt.float32
F16 = mybir.dt.float16

IMAGES, PATCHES, PITCH = 64, 25, 32
PER_TILE = 128 // PITCH
TILES = IMAGES // PER_TILE
GROUPS = 4
GT = TILES // GROUPS
GI = GT * PER_TILE
TOK = GI * PATCHES
PAD = GI * PITCH
D, FC = 192, 96
KC = D // FC
PATCH_K = 3 * 16 * 16
PK = PATCH_K // 128
EPS = 1e-5
LH, LD, LG = 12, 64, 4
INNER = LH * LD
PAIRS = LH // 2
CHUNKS = PAIRS * LG
WM = INNER // 128
QQ = LG * PATCHES
NORM_EPS = 1e-6 * float(np.sqrt(2 * LD))
H, HD = 12, 16
HPC = FC // HD
HQ = 128 // 32
HC = H // HQ
E, FF = 8, 768
FM = FF // 128
W_SCALE = 1024.0
UNITS = 2 * E
RING = 8
assert (E * FM) % RING == 0


def load_shapes():
    shapes = {
        "patches": [TILES, 128, PATCH_K], "conv_w": [128, PK * D], "conv_b": [1, D], "pos": [128, D],
        "wk": [FC, KC * INNER], "wv": [FC, KC * INNER], "wqT": [128, CHUNKS * D], "wt2": [128, LG * 128],
        "bt2": [128, LG], "gt2": [128, LG], "betat2": [128, LG],
        "wf": [WM, 128, CHUNKS * 128], "bf": [128, WM], "gf": [128, WM], "betaf": [128, WM],
        "wo": [128, WM * D], "bo": [1, D],
        "ident": [128, 128], "center": [128, 128], "mean768": [128, 128], "key_sum": [128, 128],
        "var_pick": [128, CHUNKS * 2 * CHUNKS], "rstd_pick": [FC, CHUNKS * 128],
        "slot_mask": [128, 2 * 2], "v_mask": [128, 2 * 128],
        "head_mask": [FC, HPC], "causal": [128, PATCHES], "before": [128, E * E],
    }
    for a in ("a0", "a1", "a2"):
        shapes |= {f"{a}_qkv": [FC, KC * 3 * D], f"{a}_proj": [128, HC * D]}
    shapes |= {"a0_projb": [1, D], "a1_projb": [1, D], "a1_qkb": [FC, 2 * KC], "a1_vb": [1, D]}
    for m in ("m0", "m1"):
        shapes |= {f"{m}_ln1": [FC, 2 * KC], f"{m}_ln2": [FC, 2 * KC], f"{m}_gate": [FC, KC * E],
                   f"{m}_w1": [FC, KC * E * FF], f"{m}_w2": [128, E * FM * D]}
    shapes |= {"m0_gateb": [1, E], "m0_b1": [128, E * FM], "m0_b2": [E, D]}
    return shapes


def build(nc, dram, out, stages=7):
    ctx = ExitStack()
    with ctx:
        def sem(name):
            return ctx.enter_context(nc.semaphore(name))

        def sb(name, shape, scope=ctx, dtype=F32):
            return scope.enter_context(nc.sbuf_tensor(name, shape, dtype))

        bank = [ctx.enter_context(nc.psum_tensor(f"bank{k}", [128, 512], F32)) for k in range(2)]
        psum_s = ctx.enter_context(nc.psum_tensor("psum_s", [128, H, 128], F32))
        psum_o = ctx.enter_context(nc.psum_tensor("psum_o", [128, H, 128], F32))
        s_flat = psum_s[:, :, :].rearrange("p h f -> p (h f)")
        o_flat = psum_o[:, :, :].rearrange("p h f -> p (h f)")
        PB = [bank[0][:, :], bank[1][:, :]] + [s_flat[:, 512 * k:512 * k + 512] for k in range(3)] \
            + [o_flat[:, 512 * k:512 * k + 512] for k in range(3)]

        hid = sb("hid", [128, TILES, D])
        ident = sb("ident_sb", [128, 128])
        half = sb("half", [128, GT])
        eps = sb("eps_sb", [128, 1])
        neps = sb("neps_sb", [128, 1])
        stats = sb("stats", [128, GT, 6])
        mv = sb("mv", [128, GT, 2])
        ve = sb("ve", [128, GT])
        rstd = sb("rstd", [128, GT])
        junk = sb("junk", [128, 1])
        pool_junk = sb("pool_junk", [128, 1])
        xn = sb("xn", [128, GT, D])
        xT = sb("xT", [FC, KC, PAD])

        ident_in = sem("ident_in")
        fills = sem("fills")

        lin = ExitStack()
        patch_t = sb("patch_t", [128, GT, PK, 128], lin)
        conv_w = sb("conv_w_sb", [128, PK, D], lin)
        posb = sb("posb", [128, D], lin)
        feat = sb("feat", [128, CHUNKS, TOK], lin)
        wqt = sb("wqt", [FC, KC, CHUNKS, 128], lin)
        wfs = [sb(f"wfs{k}", [128, CHUNKS, 128], lin) for k in range(2)]
        kpos = sb("kpos", [128, GI, 2, PITCH], lin)
        kneg = sb("kneg", [128, GI, 2, PITCH], lin)
        upos = sb("upos", [128, 2, LG, TOK], lin)
        uneg = sb("uneg", [128, 2, LG, TOK], lin)
        vblk = sb("vblk", [128, 2, 2, 2, 128], lin)
        scor = sb("scor", [128, 3, 2 * QQ], lin)
        denb = sb("denb", [128, 2, TOK], lin)
        rec = sb("rec", [128, TOK], lin)
        gq = sb("gq", [128, 2, TOK], lin)
        wk = sb("wk_sb", [FC, KC, INNER], lin)
        wv = sb("wv_sb", [FC, KC, INNER], lin)
        wo = sb("wo_sb", [128, WM, D], lin)
        bob = sb("bob", [128, D], lin)
        center = sb("center_sb", [128, 128], lin)
        mean768 = sb("mean768_sb", [128, 128], lin)
        key_sum = sb("key_sum_sb", [128, 128], lin)
        var_pick = sb("var_pick_sb", [128, CHUNKS, 2 * CHUNKS], lin)
        rstd_pick = sb("rstd_pick_sb", [FC, CHUNKS, 128], lin)
        slot_mask = sb("slot_mask_sb", [128, 2, 2], lin)
        v_mask = sb("v_mask_sb", [128, 2, 128], lin)
        lcol = sb("lcol", [128, 5, LG], lin)
        fcol = sb("fcol", [128, 3, WM], lin)
        sqb = denb
        xdup = patch_t[0:FC, :, :, :].rearrange("p t k n -> p (t k n)")[:, 0:KC * GI * 2 * PITCH]\
            .rearrange("p (k b h t) -> p k b h t", k=KC, b=GI, h=2)
        qstd = rec[0:2 * CHUNKS, :]
        qrstd = sb("qrstd", [FC, TOK], lin)
        wqT = feat[:, :, :].rearrange("p c t -> p (c t)")[:, 0:CHUNKS * D].rearrange("p (c d) -> p c d", d=D)
        wt2 = upos[:, 0, :, 0:128]
        y768 = upos[:, :, :, :].rearrange("p a g t -> p (a g t)")[:, 0:WM * TOK].rearrange("p (m t) -> p m t", t=TOK)
        ysq = uneg[:, :, :, :].rearrange("p a g t -> p (a g t)")[:, 0:WM * TOK].rearrange("p (m t) -> p m t", t=TOK)
        fused = patch_t[:, :, :, :].rearrange("p t k n -> p (t k n)").rearrange("p (m t) -> p m t", t=PAD)
        ystd = scor[:, :, :].rearrange("p s n -> p (s n)")[:, 0:TOK]
        lin.close()

        late = ExitStack()
        xres = sb("xres", [128, TILES, D], late)
        w1 = [sb(f"w1_{half_name}", [FC, KC, E, FF], late, F16) for half_name in ("high", "low")]
        w2 = [sb(f"w2_{half_name}", [128, E, FM, D], late, F16) for half_name in ("high", "low")]
        arrival = sb("arrival", [128, KC * FF], late)
        xh = [sb(f"x_{half_name}", [FC, KC, PAD], late, F16) for half_name in ("high", "low")]
        gelu_out = sb("gelu_out", [128, 3, TOK], late)
        gate_w = sb("gate_w_sb", [FC, 2, KC, E], late)
        gate_b = sb("gate_b_sb", [128, E], late)
        bias1 = sb("b1_sb", [128, E * FM], late)
        bias2 = sb("b2_sb", [E, D], late)
        before = sb("before_sb", [128, E, E], late)
        head_mask = sb("head_mask_sb", [FC, HPC], late)
        causal = sb("causal_sb", [128, PATCHES], late)
        qkv_w = [sb(f"qkv_w{a}", [FC, KC, 3 * D], late) for a in range(2)]
        proj_w = [sb(f"proj_w{a}", [128, HC, D], late) for a in range(2)]
        proj_b = [sb(f"proj_b{a}", [128, D], late) for a in range(2)]
        qk_b = sb("qk_b", [FC, 2, KC], late)
        v_b = sb("v_b", [128, D], late)
        ln_cols = sb("ln_cols", [FC, 4, 2, KC], late)
        xTa = sb("xTa", [FC, KC, PAD], late)
        qT = sb("qT", [FC, KC, PAD], late)
        kT = xTa
        kexp = sb("kexp", [FC, 2, KC, HPC, 128], late)
        vt = sb("vt", [128, GT, H, 32], late)
        sx = sb("sx", [128, 2, H, PATCHES], late)
        pr = sb("pr", [128, 2, H, PITCH], late)
        pT = sb("pT", [128, H, 128], late)
        smax = sb("smax", [128, 2, H], late)
        ssum = sb("ssum", [128, 2, H], late)
        srec = sb("srec", [128, 2, H], late)
        aoT = sb("aoT", [128, HC, 128], late)
        he = [sb(f"he_{half_name}", [128, RING, GI, PITCH], late, F16) for half_name in ("high", "low")]
        lg = sb("lg", [128, GT, E], late)
        gtr = sb("gtr", [128, GT, E, E], late)
        eqr = sb("eqr", [128, GT, E, E], late)
        rank = sb("rank", [128, GT, E], late)
        picked = sb("picked", [128, GT, E], late)
        lmax = sb("lmax", [128, GT], late)
        lexp = sb("lexp", [128, GT, E], late)
        lsum = sb("lsum", [128, GT], late)
        lrec = sb("lrec", [128, GT], late)
        cw = sb("cw", [128, GT, E], late)
        cw_y = sb("cw_y", [128, GT, E], late)
        cwT = sb("cwT", [E, PAD], late)
        late.close()

        ATT = [dict(double=True, causal=False, ln=0), dict(double=False, causal=True, ln=None),
               dict(double=True, causal=False, ln=2)]
        MOE = [dict(ln=1, biased=True), dict(ln=3, biased=False)]

        patch_in = [sem(f"patch_in{t}") for t in range(GT)]
        conv_in = sem("conv_in")
        emb_ready, emb_free = sem("emb_ready"), sem("emb_free")
        wq_in, lin_in = sem("wq_in"), sem("lin_in")
        wqt_ready, wqt_kept = sem("wqt_ready"), sem("wqt_kept")
        lin_fill = sem("lin_fill")
        lfront = dict(ln=sem("l_ln"), rs=sem("l_rs"), xTp=sem("l_xTp"), xTs=sem("l_xTs"))
        q_ready, gelu_done, c_ready, c_kept, sq_done, var_acc = map(
            sem, ("q_ready", "gelu_done", "c_ready", "c_kept", "sq_done", "var_acc"))
        std_ready, rstd_ready, rb_ready, w_ready, u_done = map(
            sem, ("std_ready", "rstd_ready", "rb_ready", "w_ready", "u_done"))
        xdup_done = sem("xdup_done")
        k_ready, kpm_done, v_ready, vblk_done, st_done = map(
            sem, ("k_ready", "kpm_done", "v_ready", "vblk_done", "st_done"))
        s_ready = [sem(f"s_ready{b2}") for b2 in range(2)]
        den_ready, num_ready, den_kept, rec_done, prob_done, out_done = map(
            sem, ("den_ready", "num_ready", "den_kept", "rec_done", "prob_done", "out_done"))
        wf_in = [sem(f"wf_in{k}") for k in range(2)]
        y_ready, wf_free, mean_ready, yc_done, ysq_done, yvar_ready, ystd_done, yrec_done, yn_done = map(
            sem, ("y_ready", "wf_free", "mean_ready", "yc_done", "ysq_done", "yvar_ready", "ystd_done",
                  "yrec_done", "yn_done"))
        fused_done, z_ready, z_added, hid_done = map(sem, ("fused_done", "z_ready", "z_added", "hid_done"))
        late_in, late_fill = sem("late_in"), sem("late_fill")
        a2_in = sem("a2_in")
        unit_in, unit_high, unit_low = sem("unit_in"), sem("unit_high"), sem("unit_low")
        att_all = {n: sem(f"a_{n}") for n in (
            "xTp", "xTs", "q_p", "q_sb", "k_p", "k_sb", "v_p", "v_sb", "kx", "s_p", "shifted",
            "exp_done", "norm", "p_t", "o_p", "oT_sb", "y_p", "y_done")}
        moe_all = {n: sem(f"m_{n}") for n in (
            "xTp", "xTs", "g_p", "shifted", "exp_done", "cw_ready", "cwT_p", "cwT_sb", "h_p", "h_act", "h_low", "chain",
            "done", "x_high", "x_low")}
        AS = [att_all | {n: sem(f"a{a}_{n}") for n in ("ln", "rs", "chain")} for a in range(3)]
        MS = [moe_all | {n: sem(f"m{m}_{n}") for n in ("ln", "rs", "y_p", "y_acc")} for m in range(2)]
        out_sem = sem("out_sem")

        class Chain:

            def __init__(self, eng, counter, i, per):
                self.eng, self.counter, self.base, self.per, self.n = eng, counter, i * per, per, 0

            def step(self, ins):
                ins.then_inc(self.counter, 1)
                self.n += 1

            def wait(self):
                self.eng.wait_ge(self.counter, self.base + self.n)

            def end(self):
                assert self.n == self.per, (self.n, self.per)

        def row(name, parts, size):
            a = dram[name]
            return bass.AP(a.tensor, 0, [[0, parts], [1, size]])

        def compact(view):
            return view.rearrange("p (b q) -> p b q", q=PITCH)[:, :, 0:PATCHES]

        def front_piece_dve(dve, i, S, src, double, piece):
            rounds = 2 if double else 1
            r, part = piece // 3, piece % 3
            if r >= rounds:
                return
            tiles = src if r == 0 else xres
            ch = Chain(dve, S["ln"], i, 4 * rounds)
            ch.n = 4 * r + (0, 1, 3)[part]
            if part == 0:
                if r:
                    ch.wait()
                    dve.memset(junk[:, :], 0.0)
                for t in range(GT):
                    last = dve.bn_stats(stats[:, t, :], tiles[:, bass.ds(i * GT + t, 1), :])
                ch.step(last)
            if part == 1:
                ch.wait()
                dve.memset(junk[:, :], 0.0)
                for t in range(GT):
                    last = dve.bn_aggr(mv[:, t, :], stats[:, t, :])
                ch.step(last)
                ch.wait()
                ch.step(dve.tensor_scalar(ve[:, :], mv[:, :, 1], EPS, None, ALU.add))
            if part == 2:
                dve.wait_ge(S["rs"], i * rounds + r + 1)
                for t in range(GT):
                    dst = xres[:, bass.ds(i * GT + t, 1), :] if r + 1 < rounds else xn[:, t, :]
                    last = dve.tensor_scalar(dst, tiles[:, bass.ds(i * GT + t, 1), :], mv[:, t, 0:1],
                                             rstd[:, t:t + 1], ALU.subtract, ALU.mult)
                ch.step(last)

        def front_dve(dve, i, S, src, double):
            for piece in range(6):
                front_piece_dve(dve, i, S, src, double, piece)

        def front_round_pool(pool, i, S, double, r):
            rounds = 2 if double else 1
            if r < rounds:
                pool.wait_ge(S["ln"], i * (4 * rounds) + 4 * r + 3)
                pool.tensor_tensor(rstd[:, :], ve[:, :], half[:, :], ALU.pow).then_inc(S["rs"], 1)

        def front_pool(pool, i, S, double):
            for r in range(2):
                front_round_pool(pool, i, S, double, r)

        def front_pe(pe, i, S, double, banks=(0, 1)):
            per = 8 if double else 4
            pe.wait_ge(S["ln"], i * per + per)
            for t in range(GT):
                for k in range(KC):
                    last = pe.transpose(PB[banks[k]][0:FC, 128 * t:128 * t + 128], xn[:, t, FC * k:FC * k + FC],
                                        ident[:, :])
            last.then_inc(S["xTp"], 1)

        def front_act(act, v, S, ln, banks=(0, 1), xT=xT):
            act.wait_ge(S["xTp"], v + 1)
            for k in range(KC):
                if ln is None:
                    last = act.activation(xT[:, k, :], PB[banks[k]][0:FC, :], ACT.Copy)
                else:
                    last = act.activation(xT[:, k, :], PB[banks[k]][0:FC, :], ACT.Identity,
                                          scale=ln_cols[:, ln, 0, k:k + 1], bias=ln_cols[:, ln, 1, k:k + 1])
                last.then_inc(S["xTs"], 1)

        TAIL = dict(mean=1, center=2, square=3, var=6, std=7, rec=8, scale=9, gelu=11, out=19)
        FRONT = 3
        LAG = LG + 1
        LIN_STEPS = CHUNKS + LAG + 2

        def wait_scores(eng, n):
            for b2 in range(2):
                eng.wait_ge(s_ready[b2], n)

        def lin_passes(eng, body):
            body(0, False, True)
            with eng.Fori(1, GROUPS - 1) as i:
                body(i, True, True)
            body(GROUPS - 1, True, False)

        PAIR = lambda e, u: {(e, 0): [f"s{u}"], (e, 1): [f"p{u}"], (e, 2): [f"o{2 * u}"], (e, 3): [f"y{2 * u}"],
                             (e, 4): [f"o{2 * u + 1}"], (e, 5): [f"y{2 * u + 1}"]}
        PLACES = [{(0, 5): ["f0", "f1"], (1, 0): ["f2", "f3"], (1, 1): ["f4", "f5"], (1, 3): ["transpose"], (1, 5): ["q"],
                   (2, 1): ["v"], (2, 3): ["k"], (2, 4): ["kx0"], (2, 5): ["kx1"], **PAIR(3, 0), **PAIR(4, 1)},
                  {(4, 3): ["f0", "f1"], (4, 4): ["f2"], (5, 0): ["transpose"], (5, 1): ["q"], (5, 2): ["v"], (5, 3): ["k"],
                   (5, 4): ["kx0"], (5, 5): ["kx1"], **PAIR(6, 0), **PAIR(7, 1)}]
        for places in PLACES:
            after = [p for p in places if "s1" in places[p]][0]
            places[(after[0] - 1, 4)] = places[(after[0] - 1, 4)] + ["kx2"]
            places[(after[0] - 1, 5)] = places[(after[0] - 1, 5)] + ["kx3"]
        WEIGHTS = (0, 4)
        GATE_EXP = (0, 3)
        NEXT_FRONT = (7, 2)

        HALVES = ((0, 0), (0, 1), (1, 0))

        def passes(eng, run):
            run(0, 0, 1, (0, 1, 1), None, (0, 1))
            with eng.Fori(1, GROUPS - 1) as i:
                run(0, i, i * 2, (0, i + 1, i * 2), (1, i - 1, i * 2 + 1), (0, i + 1))
            run(0, GROUPS - 1, 6, (2, 0, 6), (1, 2, 7), (1, 0))
            run(1, 0, 8, (2, 1, 8), (1, 3, 9), (1, 1))
            with eng.Fori(1, GROUPS - 1) as i:
                run(1, i, i + 9, (2, i + 1, i + 9), None, (1, i + 1))
            run(1, GROUPS - 1, 12, None, None, None)

        def unit(u):
            e = u // 2
            if u % 2 == 0:
                return arrival[0:FC, 0:KC * FF].rearrange("p (k n) -> p k n", k=KC), [w[:, :, e, :] for w in w1]
            return arrival[:, 0:FM * D].rearrange("p (m n) -> p m n", n=D), [w[:, e, :, :] for w in w2]

        def units_after(n, i, e, m):
            first_pass = isinstance(i, int) and (n, i) == (0, 0)
            last_pass = isinstance(i, int) and (n, i) == (0, GROUPS - 1)
            next_pass = isinstance(i, int) and (n, i) == (1, 0)
            at = {2: 0, 4: 1}.get(m)
            if at is None:
                return []
            if first_pass and 2 * e < UNITS // 2:
                return [(0, UNITS // 2 + 2 * e + at)]
            if last_pass and e >= 1:
                return [(1, 2 * (e - 1) + at)]
            if next_pass and e == 0:
                return [(1, UNITS - 2 + at)]
            return []

        BIAS_COPY, BIAS_SUM = (1, 3), (1, 4)

        def order(biased, e):
            return 1 if e < 0 else e + (biased and e >= 1)

        def first_job(v):
            return isinstance(v, int) and v == 0

        def job_steps(step, eng, job1, job2, e, m):
            for job, places in zip((job1, job2), PLACES):
                if job is not None:
                    for name in places.get((e, m), []):
                        step(eng, *job, name)

        def whole_job(step, eng, job, split=None):
            u = 0
            for n, names in enumerate(PLACES[0].values()):
                for name in names:
                    step(eng, *job, name)
                if split is not None and u < UNITS // 2 and n % 2:
                    split(0, u)
                    u += 1
            assert split is None or u == UNITS // 2

        def stage_done(n):
            return [(emb_free, TILES + 2), (hid_done, TILES), (moe_all["done"], 2 * GROUPS)][n]

        block = ctx.enter_context(nc.Block())

        @block.sync
        def _(sp):
            sp.dma_start(conv_w[:, :, :].rearrange("p k d -> p (k d)"), dram["conv_w"][:, :]).then_inc(conv_in, 16)
            sp.dma_start(posb[:, :], dram["pos"][:, :]).then_inc(conv_in, 16)
            sp.dma_start(xn[:, 0, :], row("conv_b", 128, D)).then_inc(conv_in, 16)

            def load_patches(i, t):
                sp.dma_start(patch_t[:, t, :, :].rearrange("p k n -> p (k n)"),
                             dram["patches"][bass.ds(i * GT + t, 1), :, :].rearrange("o p n -> p (o n)"))\
                  .then_inc(patch_in[t], 16)

            for t in range(GT):
                load_patches(0, t)
            with sp.Fori(1, GROUPS) as i:
                for t in range(GT):
                    sp.wait_ge(emb_ready, i * GT + t + 1 - GT)
                    load_patches(i, t)
            if stages < 2:
                sp.wait_ge(*stage_done(0))
            if stages >= 2:
                sp.wait_ge(wf_free, 2)
                with sp.Fori(0, GROUPS) as i:
                    for m in range(WM):
                        sp.wait_ge(wf_free, i * WM + m + 1)
                        sp.dma_start(wfs[m % 2][:, :, :].rearrange("p c n -> p (c n)"), dram["wf"][m, :, :])\
                          .then_inc(wf_in[m % 2], 16)
            if stages >= 3:
                sp.wait_ge(*stage_done(1))
                for a in range(2):
                    sp.dma_start(qkv_w[a][:, :, :].rearrange("p k n -> p (k n)"), dram[f"a{a}_qkv"][:, :]).then_inc(late_in, 16)
                    sp.dma_start(proj_w[a][:, :, :].rearrange("p k n -> p (k n)"), dram[f"a{a}_proj"][:, :]).then_inc(late_in, 16)
                    sp.dma_start(proj_b[a][:, :], row(f"a{a}_projb", 128, D)).then_inc(late_in, 16)
                sp.dma_start(qk_b[:, :, :].rearrange("p a k -> p (a k)"), dram["a1_qkb"][:, :]).then_inc(late_in, 16)
                sp.dma_start(v_b[:, :], row("a1_vb", 128, D)).then_inc(late_in, 16)
                for n, name in enumerate(("m0_ln1", "m0_ln2", "m1_ln1", "m1_ln2")):
                    sp.dma_start(ln_cols[:, n, :, :].rearrange("p a k -> p (a k)"), dram[name][:, :]).then_inc(late_in, 16)
                for m in range(2):
                    sp.dma_start(gate_w[:, m, :, :].rearrange("p k n -> p (k n)"), dram[f"m{m}_gate"][:, :]).then_inc(late_in, 16)
                sp.dma_start(head_mask[:, :], dram["head_mask"][:, :]).then_inc(late_in, 16)
                sp.dma_start(causal[:, :], dram["causal"][:, :]).then_inc(late_in, 16)
                sp.dma_start(before[:, :, :].rearrange("p a b -> p (a b)"), dram["before"][:, :]).then_inc(late_in, 16)
                sp.dma_start(gate_b[:, :], row("m0_gateb", 128, E)).then_inc(late_in, 16)
                sp.dma_start(bias1[:, :], dram["m0_b1"][:, :]).then_inc(late_in, 16)
                sp.dma_start(bias2[:, :], dram["m0_b2"][:, :]).then_inc(late_in, 16)

                def load_unit(n, u):
                    e = u // 2
                    if n or u:
                        sp.wait_ge(unit_low, n * UNITS + u)
                    if u % 2 == 0:
                        part = dram[f"m{n}_w1"].rearrange("p (k e n) -> p k e n", k=KC, e=E)[:, :, e, :]
                    else:
                        part = dram[f"m{n}_w2"][:, FM * D * e:FM * D * e + FM * D].rearrange("p (m n) -> p m n", n=D)
                    sp.dma_start(unit(u)[0], part).then_inc(unit_in, 16)

                for u in range(UNITS):
                    load_unit(0, u)
                sp.wait_ge(att_all["y_done"], 5 * GT)
                sp.dma_start(qkv_w[0][:, :, :].rearrange("p k n -> p (k n)"), dram["a2_qkv"][:, :]).then_inc(a2_in, 16)
                sp.dma_start(proj_w[0][:, :, :].rearrange("p k n -> p (k n)"), dram["a2_proj"][:, :]).then_inc(a2_in, 16)
                for u in range(UNITS):
                    load_unit(1, u)
            if stages < 3:
                sp.wait_ge(*stage_done(stages - 1))
                for t in range(TILES):
                    sp.dma_start(out[t, :, :], hid[:, t, :]).then_inc(out_sem, 16)
                sp.wait_ge(out_sem, 16 * TILES)
            else:
                with sp.Fori(0, GROUPS) as i:
                    sp.wait_ge(MS[1]["done"], i + GROUPS + 1)
                    sp.dma_start(out[bass.ds(i * GT, GT), :, :].rearrange("t p d -> p t d"),
                                 hid[:, bass.ds(i * GT, GT), :]).then_inc(out_sem, 16)
                sp.wait_ge(out_sem, 16 * GROUPS)

        @block.gpsimd
        def _(pool):
            if stages >= 2:
                pool.wait_ge(fills, 3)
                pool.memset(kpos[:, :, :, :], 0.0).then_inc(lin_fill, 1)
                pool.memset(kneg[:, :, :, :], 0.0).then_inc(lin_fill, 1)
                def lin_dup(i, tail):
                    pool.wait_ge(lfront["xTs"], i * 2 + 2)
                    if tail:
                        pool.wait_ge(z_ready, i * GT)
                    pool.tensor_tensor(pool_junk[:, :], half[:, 0:1], half[:, 0:1], ALU.mult)
                    for k in range(KC):
                        pool.tensor_copy(xdup[:, k, :, :, :], xT[:, k, :].rearrange("p (b t) -> p b t", t=PITCH).unsqueeze(2)
                                         .to_broadcast([FC, GI, 2, PITCH])).then_inc(xdup_done, 1)

                def lin_pool(i, tail, front):
                    lin_dup(i, tail)
                    if front:
                        front_pool(pool, i + 1, lfront, False)

                front_pool(pool, 0, lfront, False)
                lin_passes(pool, lin_pool)

            def job_pool(pool, n, g, v, name):
                if name in ("f2", "f5"):
                    front_round_pool(pool, g, AS[n], ATT[n]["double"], int(name[1]) // 3)

            def pass_pool(n, i, jobs, job1, job2, nxt):
                S, v = MS[n], i + GROUPS * n
                for e in range(E):
                    for m in range(FM):
                        k = e * FM + m
                        pool.wait_ge(S["h_act"], v * (E * FM) + k + 1)
                        pool.tensor_tensor(he[1][:, k % RING, :, 0:PATCHES],
                                           gelu_out[:, k % 3, :].rearrange("p (b q) -> p b q", q=PATCHES),
                                           he[0][:, k % RING, :, 0:PATCHES], ALU.subtract).then_inc(S["h_low"], 1)
                        job_steps(job_pool, pool, job1, job2, e, m)
                        if (e, m) == (NEXT_FRONT[0], NEXT_FRONT[1] + 2) and nxt is not None:
                            front_pool(pool, nxt[1], MS[nxt[0]], False)

            if stages >= 3:
                pool.wait_ge(*stage_done(1))
                pool.memset(pr[:, :, :, :], 0.0).then_inc(late_fill, 1)
                pool.memset(pT[:, :, :], 0.0).then_inc(late_fill, 1)
                pool.memset(vt[:, :, :, :], 0.0).then_inc(late_fill, 1)
                for part in he:
                    pool.memset(part[:, :, :, PATCHES:PITCH], 0.0).then_inc(late_fill, 1)
                whole_job(job_pool, pool, (0, 0, 0))
                front_pool(pool, 0, MS[0], False)
                passes(pool, pass_pool)

        @block.scalar
        def _(act):
            act.dma_start(ident[:, :], dram["ident"][:, :]).then_inc(ident_in, 16)
            if stages >= 2:
                act.dma_start(wqT, dram["wqT"].rearrange("p (c d) -> p c d", d=D)).then_inc(wq_in, 16)
                act.dma_start(wt2, dram["wt2"].rearrange("p (g n) -> p g n", g=LG)).then_inc(wq_in, 16)
                for dst, name in ((wk[:, :, :].rearrange("p k n -> p (k n)"), "wk"), (wv[:, :, :].rearrange("p k n -> p (k n)"), "wv"),
                                  (wo[:, :, :].rearrange("p m n -> p (m n)"), "wo"), (center[:, :], "center"), (mean768[:, :], "mean768"),
                                  (key_sum[:, :], "key_sum"),
                                  (var_pick[:, :, :].rearrange("p c n -> p (c n)"), "var_pick"),
                                  (rstd_pick[:, :, :].rearrange("p c n -> p (c n)"), "rstd_pick"),
                                  (slot_mask[:, :, :].rearrange("p a n -> p (a n)"), "slot_mask"),
                                  (v_mask[:, :, :].rearrange("p a n -> p (a n)"), "v_mask"),
                                  (lcol[:, 0, :], "bt2"), (lcol[:, 1, :], "gt2"), (lcol[:, 2, :], "betat2"),
                                  (fcol[:, 0, :], "bf"), (fcol[:, 1, :], "gf"), (fcol[:, 2, :], "betaf")):
                    act.dma_start(dst, dram[name][:, :]).then_inc(lin_in, 16)
                act.dma_start(bob[:, :], row("bo", 128, D)).then_inc(lin_in, 16)
                act.sem_inc(wf_free, 2)
                for c in range(CHUNKS):
                    for k in range(KC):
                        n = c * KC + k
                        act.wait_ge(wqt_ready, n + 1)
                        act.activation(wqt[:, k, c, :], PB[n % 4][0:FC, 0:128], ACT.Copy).then_inc(wqt_kept, 1)
                act.wait_ge(lin_in, LIN_LOADS * 16)
                act.wait_ge(lin_fill, 4)

                def tail_act(i, c):
                    if c == TAIL["square"]:
                        act.wait_ge(yc_done, i + 1)
                        act.activation(ysq, y768, ACT.Square).then_inc(ysq_done, 1)
                    if c == TAIL["std"]:
                        act.wait_ge(yvar_ready, i + 1)
                        act.activation(ystd, PB[5][:, 0:TOK], ACT.Sqrt, bias=eps[:, :]).then_inc(ystd_done, 1)
                    m = c - TAIL["gelu"]
                    if 0 <= m < WM:
                        if m == 0:
                            act.wait_ge(yn_done, i + 1)
                        act.activation(compact(fused[:, m, :]), y768[:, m, :].rearrange("p (b q) -> p b q", q=PATCHES),
                                       ACT.Gelu, scale=fcol[:, 1, m:m + 1], bias=fcol[:, 2, m:m + 1]).then_inc(fused_done, 1)

                def lin_act(i, tail, front):
                    for c in range(CHUNKS + 1):
                        if c < CHUNKS:
                            act.wait_ge(q_ready, i * CHUNKS + c + 1)
                            if c >= 2:
                                act.wait_ge(c_ready, i * CHUNKS + c - 1)
                            act.activation(gq[:, c % 2, :], PB[c % 2][:, 0:TOK], ACT.Gelu,
                                           bias=lcol[:, 0, c % LG:c % LG + 1]).then_inc(gelu_done, 1)
                        if c >= 1:
                            b = c - 1
                            act.wait_ge(c_kept, i * CHUNKS + b + 1)
                            if b >= 2:
                                act.wait_ge(var_acc, i * CHUNKS + b - 1)
                            act.activation(sqb[:, b % 2, :], feat[:, b, :], ACT.Square).then_inc(sq_done, 1)
                        if tail:
                            tail_act(i - 1, c)
                    act.wait_ge(var_acc, i * CHUNKS + CHUNKS)
                    act.activation(qstd, PB[4][0:2 * CHUNKS, 0:TOK], ACT.Sqrt, bias=eps[0:2 * CHUNKS, :])\
                       .then_inc(std_ready, 1)
                    for c in range(LIN_STEPS):
                        n = c - LAG - 1
                        if 0 <= n < CHUNKS:
                            act.wait_ge(den_ready, i * CHUNKS + n + 1)
                            if n >= 2:
                                act.wait_ge(rec_done, i * CHUNKS + n - 1)
                            act.activation(denb[:, n % 2, 0:2 * QQ], PB[7][:, 0:2 * QQ], ACT.Identity, bias=neps[:, :])\
                               .then_inc(den_kept, 1)
                        n = c - 1
                        if 0 <= n < CHUNKS:
                            p, g = n // LG, n % LG
                            act.wait_ge(w_ready, i * CHUNKS + n + 1)
                            if p >= 2:
                                wait_scores(act, i * CHUNKS + LG * (p - 1))
                            act.activation(upos[:, p % 2, g, :], feat[:, n, :], ACT.Relu,
                                           scale=lcol[:, 1, g:g + 1], bias=lcol[:, 2, g:g + 1]).then_inc(u_done, 1)
                            act.activation(uneg[:, p % 2, g, :], feat[:, n, :], ACT.Relu,
                                           scale=lcol[:, 3, g:g + 1], bias=lcol[:, 4, g:g + 1]).then_inc(u_done, 1)
                        n = c - LAG
                        if 0 <= n < CHUNKS:
                            wait_scores(act, i * CHUNKS + n + 1)
                            if n >= 3:
                                act.wait_ge(num_ready, i * CHUNKS + n - 2)
                            act.activation(scor[:, n % 3, :], PB[(1, 4)[n % 2]][:, 0:2 * QQ], ACT.Copy).then_inc(st_done, 1)
                        n = c - 2
                        if 0 <= n < CHUNKS:
                            pp, bg = n // LG, n % LG
                            act.wait_ge(k_ready, i * PAIRS + pp + 1)
                            if pp >= 1:
                                wait_scores(act, i * CHUNKS + n - LG + 1)
                            for dst, sign in ((kpos, 0), (kneg, 1)):
                                for slot in range(2):
                                    last = act.activation(
                                        dst[:, PER_TILE * bg:PER_TILE * bg + PER_TILE, slot, 0:PATCHES],
                                        PB[2][:, QQ * bg:QQ * bg + QQ].rearrange("p (b q) -> p b q", q=PATCHES),
                                        ACT.Relu, scale=slot_mask[:, sign, slot:slot + 1])
                            last.then_inc(kpm_done, 1)
                        n = c - LAG - 2
                        if 0 <= n < CHUNKS:
                            act.wait_ge(num_ready, i * CHUNKS + n + 1)
                            pp, bg = n // LG, n % LG
                            for b2 in range(2):
                                dst = feat[:, LG * pp:LG * pp + LG, :].rearrange(
                                    "p g (n j b q) -> p n b j g q", j=2, b=2, q=PATCHES)[:, bg, b2, :, :, :]
                                part = PB[6][:, 2 * QQ * b2:2 * QQ * b2 + 2 * QQ]
                                last = act.activation(dst, part.rearrange("p (j g q) -> p j g q", j=2, g=LG), ACT.Copy)
                            last.then_inc(out_done, 1)
                    for m in range(WM):
                        act.wait_ge(y_ready, i * WM + m + 1)
                        act.activation(y768[:, m, :], PB[6 + m % 2][:, 0:TOK], ACT.Identity, bias=fcol[:, 0, m:m + 1])\
                           .then_inc(wf_free, 1)
                        if m == FRONT and front:
                            front_act(act, i + 1, lfront, None, (4, 5))

                front_act(act, 0, lfront, None)
                lin_passes(act, lin_act)
                for c in range(CHUNKS):
                    tail_act(GROUPS - 1, c)

            def job_act(act, n, g, v, name):
                S = att_all
                if name == "transpose":
                    front_act(act, v, S, ATT[n]["ln"], (4, 5), xTa)
                if name == "q":
                    for m in range(KC):
                        act.wait_ge(S["q_p"], v * KC + m + 1)
                        if n == 1:
                            last = act.activation(qT[:, m, :], PB[6 + m][0:FC, :], ACT.Identity, bias=qk_b[:, 0, m:m + 1])
                        else:
                            last = act.activation(qT[:, m, :], PB[6 + m][0:FC, :], ACT.Copy)
                        last.then_inc(S["q_sb"], 1)
                if name == "k":
                    act.wait_ge(S["k_p"], v * KC + KC)
                    for m in range(KC):
                        if n == 1:
                            last = act.activation(kT[:, m, :], PB[6 + m][0:FC, :], ACT.Identity, bias=qk_b[:, 1, m:m + 1])
                        else:
                            last = act.activation(kT[:, m, :], PB[6 + m][0:FC, :], ACT.Copy)
                        last.then_inc(S["k_sb"], 1)
                if name[0] == "p":
                    u = int(name[1])
                    act.wait_ge(S["shifted"], v * 2 + u + 1)
                    act.activation(pr[:, :, :, 0:PATCHES], sx[:, :, :, :], ACT.Exp).then_inc(S["exp_done"], 1)
                if name[0] == "o":
                    t = int(name[1])
                    if not (t == 0 and first_job(v)):
                        act.wait_ge(S["y_p"], v * GT + t)
                    act.wait_ge(S["o_p"], v * GT + t + 1)
                    act.activation(aoT[:, :, :].rearrange("p c n -> p (c n)"), PB[6 + t % 2][:, 0:HC * 128], ACT.Copy)\
                       .then_inc(S["oT_sb"], 1)

            def split_act(n, u):
                source, (high, low) = unit(u)
                act.wait_ge(unit_in, 16 * (n * UNITS + u + 1))
                if n == 1:
                    act.wait_ge(MS[0]["y_p"], (GROUPS - 1) * (E + 1) + order(True, u // 2) + 1)
                act.activation(high, source, ACT.Copy, scale=W_SCALE).then_inc(unit_high, 1)

            def x_high_act(v, n):
                act.wait_ge(moe_all["xTp"], v + 1)
                for k in range(KC):
                    ln = MOE[n]["ln"]
                    act.activation(xh[0][:, k, :], PB[k][0:FC, :], ACT.Identity, scale=ln_cols[:, ln, 0, k:k + 1],
                                   bias=ln_cols[:, ln, 1, k:k + 1]).then_inc(moe_all["x_high"], 1)

            def pass_act(n, i, jobs, job1, job2, nxt):
                S, L = MS[n], MOE[n]
                ny = E + L["biased"]
                v = i + GROUPS * n
                for e in range(E):
                    for m in range(FM):
                        k = e * FM + m
                        act.wait_ge(S["h_p"], v * (E * FM) + k + 1)
                        if k >= RING:
                            old = (k - RING) // FM
                            act.wait_ge(S["y_p"], i * ny + order(L["biased"], old) + 1)
                        if k >= 3:
                            act.wait_ge(S["h_low"], v * (E * FM) + k - 2)
                        bias = bias1[:, k:k + 1] if L["biased"] else 0.0
                        act.activation(he[0][:, k % RING, :, 0:PATCHES],
                                       PB[k % 2][:, 0:TOK].rearrange("p (b q) -> p b q", q=PATCHES), ACT.Gelu,
                                       bias=bias, scale=1 / W_SCALE)
                        act.activation(gelu_out[:, k % 3, :], PB[k % 2][:, 0:TOK], ACT.Gelu,
                                       bias=bias, scale=1 / W_SCALE).then_inc(S["h_act"], 1)
                        if (e, m) == GATE_EXP:
                            act.wait_ge(S["shifted"], v + 1)
                            act.activation(lexp[:, :, :], lexp[:, :, :], ACT.Exp).then_inc(S["exp_done"], 1)
                        if (e, m) == BIAS_COPY and L["biased"]:
                            act.wait_ge(S["cwT_p"], i + 1)
                            act.activation(cwT[:, :], PB[6][0:E, :], ACT.Copy).then_inc(S["cwT_sb"], 1)
                        for what in units_after(n, i, e, m):
                            split_act(*what)
                        job_steps(job_act, act, job1, job2, e, m)
                if nxt is not None:
                    front_act(act, nxt[1] + GROUPS * nxt[0], MS[nxt[0]], MOE[nxt[0]]["ln"])
                    x_high_act(nxt[1] + GROUPS * nxt[0], nxt[0])

            if stages >= 3:
                act.wait_ge(*stage_done(1))
                act.wait_ge(late_in, 16 * LATE_LOADS)
                act.wait_ge(late_fill, 5)
                whole_job(job_act, act, (0, 0, 0), split_act)
                front_act(act, 0, MS[0], MOE[0]["ln"])
                x_high_act(0, 0)
                passes(act, pass_act)
            if stages < 2:
                act.wait_ge(ident_in, 16)

        @block.vector
        def _(dve):
            dve.memset(half[:, :], -0.5).then_inc(fills, 1)
            dve.memset(eps[:, :], EPS).then_inc(fills, 1)
            dve.memset(neps[:, :], NORM_EPS).then_inc(fills, 1)
            dve.wait_ge(conv_in, 48)
            dve.tensor_tensor(posb[:, :], posb[:, :], xn[:, 0, :], ALU.add).then_inc(fills, 1)
            dve.wait_ge(fills, 4)
            dve.sem_inc(emb_free, 2)
            with dve.Fori(0, GROUPS) as i:
                for t in range(GT):
                    dve.wait_ge(emb_ready, i * GT + t + 1)
                    dve.tensor_tensor(hid[:, bass.ds(i * GT + t, 1), :], PB[t % 2][:, 0:D], posb[:, :], ALU.add)\
                       .then_inc(emb_free, 1)
            if stages >= 2:
                dve.wait_ge(lin_in, LIN_LOADS * 16)
                dve.tensor_scalar(lcol[:, 3:5, :], lcol[:, 1:3, :], -1.0, None, ALU.mult).then_inc(lin_fill, 1)
                dve.memset(qrstd[:, :], 0.0).then_inc(lin_fill, 1)
                dve.wait_ge(lin_fill, 4)
                dve.wait_ge(*stage_done(0))
                dve.wait_ge(wqt_kept, CHUNKS * KC)

                def tail_dve(i, c):
                    if c == TAIL["center"]:
                        dve.wait_ge(mean_ready, i + 1)
                        dve.tensor_tensor(y768, y768, PB[5][:, 0:TOK].unsqueeze(1).to_broadcast([128, WM, TOK]), ALU.subtract)\
                           .then_inc(yc_done, 1)
                    if c == TAIL["rec"]:
                        dve.wait_ge(ystd_done, i + 1)
                        dve.reciprocal(rec[:, :], ystd).then_inc(yrec_done, 1)
                    if c == TAIL["scale"]:
                        dve.wait_ge(yrec_done, i + 1)
                        dve.tensor_tensor(y768, y768, rec[:, :].unsqueeze(1).to_broadcast([128, WM, TOK]), ALU.mult)\
                           .then_inc(yn_done, 1)
                    t = c - TAIL["out"]
                    if 0 <= t < GT:
                        tile = hid[:, bass.ds(i * GT + t, 1), :]
                        dve.wait_ge(z_ready, i * GT + t + 1)
                        dve.tensor_tensor(tile, tile, PB[6 + t % 2][:, 0:D].unsqueeze(1), ALU.add).then_inc(z_added, 1)
                        dve.wait_ge(z_added, i * GT + t + 1)
                        dve.tensor_tensor(tile, tile, bob[:, :].unsqueeze(1), ALU.add).then_inc(hid_done, 1)

                def lin_dve(i, tail, front):
                    for c in range(CHUNKS):
                        dve.wait_ge(c_ready, i * CHUNKS + c + 1)
                        dve.tensor_copy(feat[:, c, :], PB[2 + c % 2][:, 0:TOK]).then_inc(c_kept, 1)
                        if tail:
                            tail_dve(i - 1, c)
                    dve.wait_ge(std_ready, i + 1)
                    dve.reciprocal(qrstd[0:2 * CHUNKS, :], qstd).then_inc(rstd_ready, 1)
                    for c in range(LIN_STEPS):
                        n = c - LAG - 1
                        if 0 <= n < CHUNKS:
                            dve.wait_ge(den_kept, i * CHUNKS + n + 1)
                            dve.reciprocal(rec[:, 2 * QQ * (n % 2):2 * QQ * (n % 2) + 2 * QQ], denb[:, n % 2, 0:2 * QQ])\
                               .then_inc(rec_done, 1)
                            dve.wait_ge(v_ready, i * CHUNKS + n + 1)
                            if n >= 2:
                                dve.wait_ge(num_ready, i * CHUNKS + n - 1)
                            dve.tensor_tensor(
                                vblk[:, n % 2, :, :, :],
                                PB[3 + 2 * (n % 2)][:, 0:256].rearrange("p (j m) -> p j m", m=128).unsqueeze(2).to_broadcast([128, 2, 2, 128]),
                                v_mask[:, :, :].unsqueeze(1).to_broadcast([128, 2, 2, 128]), ALU.mult).then_inc(vblk_done, 1)
                            dve.wait_ge(rec_done, i * CHUNKS + n + 1)
                            dve.wait_ge(st_done, i * CHUNKS + n + 1)
                            dve.tensor_tensor(scor[:, n % 3, :], scor[:, n % 3, :], rec[:, 2 * QQ * (n % 2):2 * QQ * (n % 2) + 2 * QQ],
                                              ALU.mult).then_inc(prob_done, 1)
                        if c < CHUNKS:
                            dve.wait_ge(rb_ready, i * CHUNKS + c + 1)
                            dve.tensor_tensor(feat[:, c, :], feat[:, c, :], PB[0][:, 0:TOK], ALU.mult)\
                               .then_inc(w_ready, 1)
                    if front:
                        front_dve(dve, i + 1, lfront, hid, False)

                front_dve(dve, 0, lfront, hid, False)
                lin_passes(dve, lin_dve)
                for c in range(CHUNKS):
                    tail_dve(GROUPS - 1, c)

            def job_dve(dve, n, g, v, name):
                S, L = AS[n], ATT[n]
                base = xres if L["double"] else hid
                if name[0] == "f":
                    if name == "f0":
                        if n != 1 and not first_job(v):
                            dve.wait_ge(S["y_done"], v * GT)
                        if n == 1:
                            dve.wait_ge(moe_all["done"], g + 1)
                        dve.memset(junk[:, :], 0.0)
                    front_piece_dve(dve, g, S, hid, L["double"], int(name[1]))
                if name == "v":
                    for j in range(2):
                        dve.wait_ge(S["v_p"], v * 2 + j + 1)
                        for t in range(2):
                            dst = vt[:, 2 * j + t, :, 0:HD]
                            part = PB[4 + j][:, D * t:D * t + D].rearrange("p (h x) -> p h x", x=HD)
                            if n == 1:
                                last = dve.tensor_tensor(dst, part, v_b[:, :].rearrange("p (h x) -> p h x", x=HD), ALU.add)
                            else:
                                last = dve.tensor_copy(dst, part)
                        last.then_inc(S["v_sb"], 1)
                if name[0:2] == "kx":
                    t = int(name[2])
                    dve.wait_ge(S["k_sb"], v * KC + KC)
                    if t >= 2:
                        dve.wait_ge(S["s_p"], v * GT + t - 1)
                    for m in range(KC):
                        last = dve.tensor_tensor(
                            kexp[:, t % 2, m, :, :], kT[:, m, 128 * t:128 * t + 128].unsqueeze(1).to_broadcast([FC, HPC, 128]),
                            head_mask[:, :].unsqueeze(2).to_broadcast([FC, HPC, 128]), ALU.mult)
                    last.then_inc(S["kx"], 1)
                if name[0] in "spy" :
                    u = int(name[1]) if name[0] in "sp" else int(name[1]) // 2
                    per_pair = 2 * (1 + L["causal"]) + 2 + 2 * (n < 2)
                    done = u * per_pair
                    if name[0] == "p":
                        done += 2 * (1 + L["causal"])
                    if name[0] == "y":
                        done += 2 * (1 + L["causal"]) + 2 + int(name[1]) % 2
                    ch = Chain(dve, S["chain"], g, 2 * per_pair)
                    ch.n = done
                if name[0] == "s":
                    for j in range(2):
                        t = 2 * u + j
                        dve.wait_ge(S["s_p"], v * GT + t + 1)
                        scores = PB[4 + j][:, 0:H * PITCH].rearrange("p (h q) -> p h q", q=PITCH)[:, :, 0:PATCHES]
                        if L["causal"]:
                            ch.step(dve.tensor_tensor(sx[:, j, :, :], scores,
                                                      causal[:, :].unsqueeze(1).to_broadcast([128, H, PATCHES]), ALU.add))
                            ch.wait()
                            scores = sx[:, j, :, :]
                        ch.step(dve.tensor_reduce(smax[:, j, :], scores, AX.X, ALU.max))
                        ch.wait()
                        last = dve.tensor_tensor(sx[:, j, :, :], scores,
                                                 smax[:, j, :].unsqueeze(2).to_broadcast([128, H, PATCHES]), ALU.subtract)
                    last.then_inc(S["shifted"], 1)
                if name[0] == "p":
                    dve.wait_ge(S["exp_done"], v * 2 + u + 1)
                    ch.step(dve.tensor_reduce(ssum[:, :, :], pr[:, :, :, 0:PATCHES], AX.X, ALU.add))
                    ch.wait()
                    ch.step(dve.reciprocal(srec[:, :, :], ssum[:, :, :]))
                    ch.wait()
                    dve.tensor_tensor(pr[:, :, :, 0:PATCHES], pr[:, :, :, 0:PATCHES],
                                      srec[:, :, :].unsqueeze(3).to_broadcast([128, 2, H, PATCHES]), ALU.mult)\
                       .then_inc(S["norm"], 1)
                    dve.wait_ge(S["norm"], v * 2 + u + 1)
                if name[0] == "p" or name in ("o0", "o2"):
                    t = 2 * u if name[0] == "p" else int(name[1]) + 1
                    if t >= 1:
                        dve.wait_ge(S["o_p"], v * GT + t)
                    for b in range(PER_TILE):
                        last = dve.transpose(pT[32 * b:32 * b + 32, :, 32 * b:32 * b + 32], pr[32 * b:32 * b + 32, t % 2, :, :])
                    last.then_inc(S["p_t"], 1)
                if name[0] == "y":
                    t = int(name[1])
                    tile = base[:, bass.ds(g * GT + t, 1), :]
                    dve.wait_ge(S["y_p"], v * GT + t + 1)
                    last = dve.tensor_tensor(tile, tile, PB[4 + t % 2][:, 0:D].unsqueeze(1), ALU.add)
                    if n < 2:
                        ch.step(last)
                        ch.wait()
                        last = dve.tensor_tensor(tile, tile, proj_b[n][:, :].unsqueeze(1), ALU.add)
                    last.then_inc(S["y_done"], 1)

            def split_dve(n, u):
                source, (high, low) = unit(u)
                dve.wait_ge(unit_high, n * UNITS + u + 1)
                dve.scalar_tensor_tensor(low, source, W_SCALE, high, ALU.mult, ALU.subtract).then_inc(unit_low, 1)

            def x_low_dve(v):
                dve.wait_ge(moe_all["xTs"], v * KC + KC)
                dve.wait_ge(moe_all["x_high"], v * KC + KC)
                dve.tensor_tensor(xh[1][:, :, :], xT[:, :, :], xh[0][:, :, :], ALU.subtract).then_inc(moe_all["x_low"], 1)

            def pass_dve(n, i, jobs, job1, job2, nxt):
                S, L = MS[n], MOE[n]
                ny = E + L["biased"]
                v = i + GROUPS * n
                ch = Chain(dve, S["chain"], v, 11)
                dve.wait_ge(S["g_p"], v + 1)
                logits = PB[7][:, 0:GT * E].rearrange("p (t e) -> p t e", e=E)
                if L["biased"]:
                    last = dve.tensor_tensor(lg[:, :, :], logits, gate_b[:, :].unsqueeze(1).to_broadcast([128, GT, E]), ALU.add)
                else:
                    last = dve.tensor_copy(lg[:, :, :], logits)
                ch.step(last)
                ch.wait()
                ch.step(dve.tensor_reduce(lmax[:, :], lg[:, :, :], AX.X, ALU.max))
                ch.wait()
                dve.tensor_tensor(lexp[:, :, :], lg[:, :, :], lmax[:, :].unsqueeze(2).to_broadcast([128, GT, E]), ALU.subtract)\
                   .then_inc(S["shifted"], 1)
                other = lg[:, :, :].unsqueeze(2).to_broadcast([128, GT, E, E])
                own = lg[:, :, :].unsqueeze(3).to_broadcast([128, GT, E, E])
                ch.step(dve.tensor_tensor(gtr[:, :, :, :], other, own, ALU.is_gt))
                ch.step(dve.tensor_tensor(eqr[:, :, :, :], other, own, ALU.is_equal))
                ch.wait()
                ch.step(dve.tensor_tensor(eqr[:, :, :, :], eqr[:, :, :, :], before[:, :, :].unsqueeze(1).to_broadcast([128, GT, E, E]), ALU.mult))
                ch.wait()
                ch.step(dve.tensor_tensor(gtr[:, :, :, :], gtr[:, :, :, :], eqr[:, :, :, :], ALU.add))
                ch.wait()
                ch.step(dve.tensor_reduce(rank[:, :, :], gtr[:, :, :, :], AX.X, ALU.add))
                ch.wait()
                def weights():
                    dve.wait_ge(S["exp_done"], v + 1)
                    ch.step(dve.scalar_tensor_tensor(picked[:, :, :], rank[:, :, :], 1.5, lexp[:, :, :], ALU.is_lt, ALU.mult))
                    ch.wait()
                    ch.step(dve.tensor_reduce(lsum[:, :], picked[:, :, :], AX.X, ALU.add))
                    ch.wait()
                    ch.step(dve.reciprocal(lrec[:, :], lsum[:, :]))
                    ch.wait()
                    dve.tensor_tensor(cw[:, :, :], picked[:, :, :], lrec[:, :].unsqueeze(2).to_broadcast([128, GT, E]), ALU.mult)\
                       .then_inc(S["cw_ready"], 1)
                    dve.wait_ge(S["cw_ready"], v + 1)
                    ch.step(dve.tensor_scalar(cw_y[:, :, :], cw[:, :, :], 1 / W_SCALE, None, ALU.mult))
                    ch.wait()
                    ch.end()

                def add(e):
                    q = order(L["biased"], e)
                    dve.wait_ge(S["y_p"], i * ny + q + 1)
                    if q >= 1:
                        dve.wait_ge(S["y_acc"], i * ny + q)
                    for t in range(GT):
                        tile = xres[:, bass.ds(i * GT + t, 1), :]
                        part = PB[2 + t // 2][:, D * (t % 2):D * (t % 2) + D].unsqueeze(1)
                        if e < 0:
                            last = dve.tensor_tensor(tile, tile, part, ALU.add)
                        else:
                            last = dve.scalar_tensor_tensor(tile, part, cw_y[:, t, e:e + 1], tile, ALU.mult, ALU.add)
                    last.then_inc(S["y_acc"], 1)

                for e in range(E):
                    for m in range(FM):
                        if (e, m) == WEIGHTS:
                            weights()
                        for what in units_after(n, i, e, m):
                            split_dve(*what)
                        job_steps(job_dve, dve, job1, job2, e, m)
                        piece = m - NEXT_FRONT[1]
                        if e == NEXT_FRONT[0] and 0 <= piece < 3 and nxt is not None:
                            if piece == 0:
                                dve.wait_ge(att_all["y_done"], (job1[2] + 1) * GT)
                                dve.memset(junk[:, :], 0.0)
                            front_piece_dve(dve, nxt[1], MS[nxt[0]], xres, False, piece)
                        if m == 1 and e >= 1:
                            add(e - 1)
                        if (e, m) == BIAS_SUM and L["biased"]:
                            add(-1)
                if nxt is not None:
                    x_low_dve(nxt[1] + GROUPS * nxt[0])
                add(E - 1)
                dve.wait_ge(S["y_acc"], i * ny + ny)
                for t in range(GT):
                    tile = hid[:, bass.ds(i * GT + t, 1), :]
                    last = dve.tensor_tensor(tile, tile, xres[:, bass.ds(i * GT + t, 1), :], ALU.add)
                last.then_inc(S["done"], 1)

            if stages >= 3:
                dve.wait_ge(*stage_done(1))
                dve.wait_ge(late_in, 16 * LATE_LOADS)
                dve.wait_ge(late_fill, 5)
                whole_job(job_dve, dve, (0, 0, 0), split_dve)
                dve.wait_ge(att_all["y_done"], GT)
                front_dve(dve, 0, MS[0], xres, False)
                x_low_dve(0)
                passes(dve, pass_dve)

        @block.tensor
        def _(pe):
            pe.wait_ge(conv_in, 48)
            with pe.Fori(0, GROUPS) as i:
                for t in range(GT):
                    pe.wait_ge(patch_in[t], i * 16 + 16)
                    pe.wait_ge(emb_free, i * GT + t + 1)
                    for k in range(PK):
                        last = pe.matmul(PB[t % 2][:, 0:D], patch_t[:, t, k, :], conv_w[:, k, :],
                                         start=(k == 0), stop=(k == PK - 1))
                    last.then_inc(emb_ready, 1)
            pe.wait_ge(ident_in, 16)
            if stages >= 2:
                pe.wait_ge(*stage_done(0))
                pe.wait_ge(wq_in, 32)
                for c in range(CHUNKS):
                    for k in range(KC):
                        n = c * KC + k
                        if n >= 4:
                            pe.wait_ge(wqt_kept, n - 3)
                        pe.matmul(PB[n % 4][0:FC, 0:128], wqT[:, c, FC * k:FC * k + FC], wt2[:, c % LG, :],
                                  start=True, stop=True).then_inc(wqt_ready, 1)
                pe.wait_ge(wqt_kept, CHUNKS * KC)
                pe.wait_ge(lin_in, LIN_LOADS * 16)

                def tail_pe(i, s):
                    if s == TAIL["mean"]:
                        pe.wait_ge(wf_free, i * WM + WM + 2)
                        for m in range(WM):
                            last = pe.matmul(PB[5][:, 0:TOK], mean768[:, :], y768[:, m, :], start=(m == 0), stop=(m == WM - 1))
                        last.then_inc(mean_ready, 1)
                    if s == TAIL["var"]:
                        pe.wait_ge(ysq_done, i + 1)
                        for m in range(WM):
                            last = pe.matmul(PB[5][:, 0:TOK], mean768[:, :], ysq[:, m, :], start=(m == 0), stop=(m == WM - 1))
                        last.then_inc(yvar_ready, 1)
                    t = s - TAIL["out"]
                    if 0 <= t < GT:
                        if t == 0:
                            pe.wait_ge(fused_done, i * WM + WM)
                        if t >= 2:
                            pe.wait_ge(z_added, i * GT + t - 1)
                        for m in range(WM):
                            last = pe.matmul(PB[6 + t % 2][:, 0:D], fused[:, m, 128 * t:128 * t + 128], wo[:, m, :],
                                             start=(m == 0), stop=(m == WM - 1))
                        last.then_inc(z_ready, 1)

                def lin_pe(i, tail, front):
                    pe.wait_ge(lfront["xTs"], i * 2 + 2)
                    for s in range(CHUNKS + 2):
                        if s < CHUNKS:
                            if s >= 2:
                                pe.wait_ge(gelu_done, i * CHUNKS + s - 1)
                            for k in range(KC):
                                last = pe.matmul(PB[s % 2][:, 0:TOK], wqt[:, k, s, :], compact(xT[:, k, :]),
                                                 start=(k == 0), stop=(k == KC - 1))
                            last.then_inc(q_ready, 1)
                        if 1 <= s <= CHUNKS:
                            c = s - 1
                            pe.wait_ge(gelu_done, i * CHUNKS + c + 1)
                            if c >= 2:
                                pe.wait_ge(c_kept, i * CHUNKS + c - 1)
                            pe.matmul(PB[2 + c % 2][:, 0:TOK], center[:, :], gq[:, c % 2, :], start=True, stop=True)\
                              .then_inc(c_ready, 1)
                        if s >= 2:
                            c = s - 2
                            pe.wait_ge(sq_done, i * CHUNKS + c + 1)
                            pe.matmul(PB[4][0:2 * CHUNKS, 0:TOK], var_pick[:, c, :], sqb[:, c % 2, :],
                                      start=(c == 0), stop=(c == CHUNKS - 1)).then_inc(var_acc, 1)
                        if tail:
                            tail_pe(i - 1, s)
                    if tail:
                        pe.wait_ge(z_added, i * GT)
                    pe.wait_ge(c_kept, i * CHUNKS + CHUNKS)
                    for c in range(LIN_STEPS):
                        p, g = c // LG, c % LG
                        n = c - LAG - 1
                        if 0 <= n < CHUNKS:
                            pe.wait_ge(st_done, i * CHUNKS + n + 1)
                            if n >= 1:
                                pe.wait_ge(den_kept, i * CHUNKS + n)
                            pe.matmul(PB[7][:, 0:2 * QQ], key_sum[:, :], scor[:, n % 3, :], start=True, stop=True)\
                              .then_inc(den_ready, 1)
                        n = c - LAG
                        if 0 <= n < CHUNKS:
                            pp, bg = n // LG, n % LG
                            if n >= 2:
                                pe.wait_ge(st_done, i * CHUNKS + n - 1)
                            pe.wait_ge(kpm_done, i * CHUNKS + n + 1)
                            if bg == 0:
                                pe.wait_ge(u_done, i * (2 * CHUNKS) + 8 * pp + 8)
                            for j in range(2):
                                for kk, uu in ((kpos, upos), (kneg, uneg)):
                                    for b2 in range(2):
                                        b = PER_TILE * bg + 2 * j + b2
                                        last = pe.matmul(PB[(1, 4)[n % 2]][64 * b2:64 * b2 + 64, QQ * j:QQ * j + QQ], kk[:, b, :, :],
                                                         uu[:, pp % 2, :, PATCHES * b:PATCHES * b + PATCHES],
                                                         start=(kk is kpos), stop=(kk is kneg))
                                        if j == 1 and kk is kneg:
                                            last.then_inc(s_ready[b2], 1)
                        n = c - LAG - 1
                        if 0 <= n < CHUNKS:
                            pp, bg = n // LG, n % LG
                            if n >= 2:
                                pe.wait_ge(vblk_done, i * CHUNKS + n - 1)
                            if n == 0:
                                pe.wait_ge(xdup_done, i * 2 + 2)
                            for j in range(2):
                                for k in range(KC):
                                    b = PER_TILE * bg + 2 * j
                                    image = xdup[:, k, b:b + 2, :, :]
                                    last = pe.matmul(PB[3 + 2 * (n % 2)][:, 128 * j:128 * j + 128], image,
                                                     wv[:, k, 128 * pp:128 * pp + 128], start=(k == 0), stop=(k == KC - 1))
                            last.then_inc(v_ready, 1)
                        if c < CHUNKS:
                            if c == 0:
                                pe.wait_ge(rstd_ready, i + 1)
                            if c >= 1:
                                pe.wait_ge(w_ready, i * CHUNKS + c)
                            pe.matmul(PB[0][:, 0:TOK], rstd_pick[:, c, :], qrstd[:, :], start=True, stop=True)\
                              .then_inc(rb_ready, 1)
                        pk = p if g == 1 and p < PAIRS else None
                        if pk is not None:
                            if pk >= 1:
                                pe.wait_ge(kpm_done, i * CHUNKS + LG * pk)
                            for k in range(KC):
                                last = pe.matmul(PB[2][:, 0:TOK], wk[:, k, 128 * pk:128 * pk + 128], compact(xT[:, k, :]),
                                                 start=(k == 0), stop=(k == KC - 1))
                            last.then_inc(k_ready, 1)
                        n = c - LAG - 2
                        if 0 <= n < CHUNKS:
                            pe.wait_ge(prob_done, i * CHUNKS + n + 1)
                            pe.wait_ge(vblk_done, i * CHUNKS + n + 1)
                            if n >= 1:
                                pe.wait_ge(out_done, i * CHUNKS + n)
                            for b2 in range(2):
                                for j in range(2):
                                    col = 2 * QQ * b2 + QQ * j
                                    last = pe.matmul(PB[6][:, col:col + QQ], vblk[:, n % 2, j, b2, :],
                                                     scor[:, n % 3, QQ * j:QQ * j + QQ], start=True, stop=True)
                            last.then_inc(num_ready, 1)
                    pe.wait_ge(out_done, i * CHUNKS + CHUNKS)
                    for m in range(WM):
                        pe.wait_ge(wf_in[m % 2], i * (16 * WM // 2) + 16 * (m // 2) + 16)
                        if m >= 2:
                            pe.wait_ge(wf_free, i * WM + m + 1)
                        for c in range(CHUNKS):
                            last = pe.matmul(PB[6 + m % 2][:, 0:TOK], wfs[m % 2][:, c, :], feat[:, c, :],
                                             start=(c == 0), stop=(c == CHUNKS - 1))
                        last.then_inc(y_ready, 1)
                        if m == FRONT and front:
                            front_pe(pe, i + 1, lfront, False, (4, 5))

                front_pe(pe, 0, lfront, False)
                lin_passes(pe, lin_pe)
                for s in range(CHUNKS):
                    tail_pe(GROUPS - 1, s)

            def job_pe(pe, n, g, v, name):
                S = att_all
                wq, wp = qkv_w[n % 2], proj_w[n % 2]
                if name == "transpose":
                    if n == 2:
                        pe.wait_ge(a2_in, 32)
                    if not first_job(v):
                        pe.wait_ge(S["y_done"], v * GT)
                    front_pe(pe, g, AS[n] , ATT[n]["double"], (4, 5))
                if name == "q":
                    pe.wait_ge(S["xTs"], v * 2 + 2)
                    if not first_job(v):
                        pe.wait_ge(S["oT_sb"], v * GT)
                    for j in range(KC):
                        for k in range(KC):
                            last = pe.matmul(PB[6 + j][0:FC, :], wq[:, k, FC * j:FC * j + FC], xTa[:, k, :],
                                             start=(k == 0), stop=(k == KC - 1))
                        last.then_inc(S["q_p"], 1)
                if name == "v":
                    for t in range(GT):
                        for k in range(KC):
                            last = pe.matmul(PB[4 + t // 2][:, D * (t % 2):D * (t % 2) + D], xTa[:, k, 128 * t:128 * t + 128],
                                             wq[:, k, 2 * D:3 * D], start=(k == 0), stop=(k == KC - 1))
                        if t % 2:
                            last.then_inc(S["v_p"], 1)
                if name == "k":
                    pe.wait_ge(S["q_sb"], v * KC + KC)
                    for j in range(KC):
                        for k in range(KC):
                            last = pe.matmul(PB[6 + j][0:FC, :], wq[:, k, D + FC * j:D + FC * j + FC], xTa[:, k, :],
                                             start=(k == 0), stop=(k == KC - 1))
                        last.then_inc(S["k_p"], 1)
                if name[0] == "s":
                    for t in (2 * int(name[1]), 2 * int(name[1]) + 1):
                        pe.wait_ge(S["kx"], v * GT + t + 1)
                        if t < 2:
                            pe.wait_ge(S["v_sb"], v * 2 + 2)
                        else:
                            pe.wait_ge(S["y_done"], v * GT + t - 1)
                        for m in range(KC):
                            for b in range(PER_TILE):
                                last = pe.matmul(PB[4 + t % 2][32 * b:32 * b + 32, 32 * HPC * m:32 * HPC * m + 32 * HPC],
                                                 qT[:, m, 128 * t + 32 * b:128 * t + 32 * b + 32],
                                                 kexp[:, t % 2, m, :, 32 * b:32 * b + 32], start=True, stop=True)
                        last.then_inc(S["s_p"], 1)
                if name[0] == "o":
                    t = int(name[1])
                    if t == 0:
                        pe.wait_ge(S["k_sb"], v * KC + KC)
                    pe.wait_ge(S["p_t"], v * GT + t + 1)
                    if t >= 2:
                        pe.wait_ge(S["oT_sb"], v * GT + t - 1)
                    for h in range(H):
                        c, r = h // HQ, 32 * (h % HQ)
                        last = pe.matmul(PB[6 + t % 2][r:r + 32, 128 * c:128 * c + 128], vt[:, t, h, :], pT[:, h, :],
                                         start=True, stop=True)
                    last.then_inc(S["o_p"], 1)
                if name[0] == "y":
                    t = int(name[1])
                    pe.wait_ge(S["oT_sb"], v * GT + t + 1)
                    if t % 2 == 0:
                        pe.wait_ge(S["shifted"], v * 2 + t // 2 + 1)
                    for c in range(HC):
                        last = pe.matmul(PB[4 + t % 2][:, 0:D], aoT[:, c, :], wp[:, c, :], start=(c == 0), stop=(c == HC - 1))
                    last.then_inc(S["y_p"], 1)

            def pass_pe(n, i, jobs, job1, job2, nxt):
                S, L = MS[n], MOE[n]
                ny = E + L["biased"]
                v = i + GROUPS * n
                pe.wait_ge(S["xTs"], v * 2 + 2)
                pe.wait_ge(S["x_low"], v + 1)
                pe.wait_ge(att_all["oT_sb"], jobs * GT)
                for t in range(GT):
                    for k in range(KC):
                        last = pe.matmul(PB[7][:, E * t:E * t + E], xT[:, k, 128 * t:128 * t + 128], gate_w[:, n, k, :],
                                         start=(k == 0), stop=(k == KC - 1))
                last.then_inc(S["g_p"], 1)

                def second(e):
                    q = order(L["biased"], e)
                    if q >= 1 or not isinstance(i, int) or i >= 1:
                        pe.wait_ge(S["y_acc"], i * ny + q)
                    elif n == 1:
                        pe.wait_ge(MS[0]["y_acc"], GROUPS * (E + 1))
                    if e >= 0:
                        pe.wait_ge(S["h_low"], v * (E * FM) + e * FM + FM)
                    for t in range(GT):
                        dst = PB[2 + t // 2][:, D * (t % 2):D * (t % 2) + D]
                        if e < 0:
                            last = pe.matmul(dst, cwT[:, 128 * t:128 * t + 128], bias2[:, :], start=True, stop=True)
                            continue
                        for m in range(FM):
                            for r, (a, b) in enumerate(HALVES):
                                tok = he[b][:, (e * FM + m) % RING, PER_TILE * t:PER_TILE * t + PER_TILE, :]
                                last = pe.matmul(dst, tok, w2[a][:, e, m, :], start=(m == 0 and r == 0),
                                                 stop=(m == FM - 1 and r == 2))
                    last.then_inc(S["y_p"], 1)

                for e in range(E):
                    pe.wait_ge(unit_low, n * UNITS + 2 * e + 2)
                    for m in range(FM):
                        k2 = e * FM + m
                        if k2 >= 2:
                            pe.wait_ge(S["h_act"], v * (E * FM) + k2 - 1)
                        for k in range(KC):
                            for r, (a, b) in enumerate(HALVES):
                                last = pe.matmul(PB[k2 % 2][:, 0:TOK], w1[a][:, k, e, 128 * m:128 * m + 128], compact(xh[b][:, k, :]),
                                                 start=(k == 0 and r == 0), stop=(k == KC - 1 and r == 2))
                        last.then_inc(S["h_p"], 1)
                        if (e, m) == BIAS_COPY and L["biased"]:
                            pe.wait_ge(S["cw_ready"], v + 1)
                            for t in range(GT):
                                last = pe.transpose(PB[6][0:E, 128 * t:128 * t + 128], cw[:, t, :], ident[:, :])
                            last.then_inc(S["cwT_p"], 1)
                        if m == 1 and e >= 1:
                            second(e - 1)
                        if (e, m) == BIAS_SUM and L["biased"]:
                            pe.wait_ge(S["cwT_sb"], i + 1)
                            second(-1)
                        job_steps(job_pe, pe, job1, job2, e, m)
                if nxt is not None:
                    pe.wait_ge(S["h_act"], v * (E * FM) + E * FM)
                    front_pe(pe, nxt[1], MS[nxt[0]] , False)
                second(E - 1)

            if stages >= 3:
                pe.wait_ge(*stage_done(1))
                pe.wait_ge(late_in, 16 * LATE_LOADS)
                pe.wait_ge(late_fill, 5)
                whole_job(job_pe, pe, (0, 0, 0))
                front_pe(pe, 0, MS[0], False)
                passes(pe, pass_pe)


LIN_LOADS = 17
LATE_LOADS = 20


def layout(x):
    def chunks(w, size):
        return w.reshape(w.shape[0] // size, size, -1).transpose(1, 0, 2).reshape(size, -1)

    def cols(v, size):
        return v.reshape(-1, size).T

    zeros = np.zeros
    f4 = np.float32
    a = {}
    pt = x["x"][:, :, :80, :80].reshape(IMAGES, 3, 5, 16, 5, 16).transpose(1, 3, 5, 0, 2, 4)
    padded = zeros((PATCH_K, IMAGES, PITCH), f4)
    padded[:, :, :PATCHES] = pt.reshape(PATCH_K, IMAGES, PATCHES)
    a["patches"] = padded.reshape(PK, 128, TILES, 128).transpose(2, 1, 0, 3).reshape(TILES, 128, PATCH_K)
    a["conv_w"] = chunks(x["L0_tok_conv_w"].reshape(D, PATCH_K).T, 128)
    a["conv_b"] = x["L0_tok_conv_b"][None]
    ids = np.searchsorted(np.arange(1 / 32, 1, 1 / 32, dtype=f4), np.arange(0, 1 - 1e-6, 1 / 5, dtype=f4), side="right")
    rows = (ids[:, None] * 32 + ids).reshape(-1)
    pos = zeros((PER_TILE, PITCH, D), f4)
    pos[:, :PATCHES] = x["L0_tok_pos_table"][rows]
    a["pos"] = pos.reshape(128, D)
    a["wk"], a["wv"] = chunks(x["L0_attn_Wk"], FC), chunks(x["L0_attn_Wv"], FC)
    wq = x["L0_attn_Wq"].reshape(LG, D, PAIRS, 128).transpose(3, 2, 0, 1)
    a["wqT"] = wq.reshape(128, CHUNKS * D)
    wt = zeros((2, LD, LG, 2, LD), f4)
    for h in range(2):
        wt[h, :, :, h, :] = x["L0_attn_Wt"].transpose(1, 0, 2)
    a["wt2"] = wt.reshape(128, LG * 128)
    for n in ("bt", "gt", "betat"):
        a[n + "2"] = np.concatenate([x["L0_attn_" + n].T] * 2, 0)
    wf = x["L0_attn_Wf"].reshape(LG, PAIRS, 128, WM, 128).transpose(3, 2, 1, 0, 4)
    a["wf"] = wf.reshape(WM, 128, CHUNKS * 128)
    a["bf"], a["gf"], a["betaf"] = (cols(x["L0_attn_" + n], 128) for n in ("bf", "gf", "betaf"))
    a["wo"], a["bo"] = chunks(x["L0_attn_Wo"], 128), x["L0_attn_bo"][None]
    a["ident"] = np.eye(128, dtype=f4)
    same = np.kron(np.eye(2), np.ones((LD, LD))).astype(f4)
    a["center"] = (np.eye(128) - same / LD).astype(f4)
    a["mean768"] = np.full((128, 128), 1 / INNER, f4)
    a["key_sum"] = np.kron(np.eye(4), np.ones((PITCH, PITCH))).astype(f4)
    mask = zeros((2, 2, PITCH, 2, 2, LD), f4)
    for b in range(2):
        for h in range(2):
            mask[b, h, :, b, h] = 1
    a["v_mask"] = mask.reshape(128, 2 * 128)
    pick = zeros((2, LD, CHUNKS, CHUNKS, 2), f4)
    for c in range(CHUNKS):
        for h in range(2):
            pick[h, :, c, c, h] = 1 / LD
    a["var_pick"] = pick.reshape(128, CHUNKS * 2 * CHUNKS)
    a["rstd_pick"] = zeros((FC, CHUNKS * 128), f4)
    a["rstd_pick"][:2 * CHUNKS] = pick.transpose(3, 4, 2, 0, 1).reshape(2 * CHUNKS, CHUNKS * 128) != 0
    slot = np.kron(np.eye(2), np.ones((LD, 1))).astype(f4)
    a["slot_mask"] = np.concatenate([slot, -slot], 1)
    a["head_mask"] = (np.kron(np.eye(HPC), np.ones((HD, 1))) * HD ** -0.5).astype(f4)
    after = np.arange(PATCHES)[None] > np.arange(PITCH)[:, None]
    a["causal"] = np.tile(np.where(after, f4(-1e30), f4(0)), (PER_TILE, 1))
    a["before"] = np.tile((np.arange(E)[None] < np.arange(E)[:, None]).astype(f4).reshape(1, -1), (128, 1))
    def spread(w):
        padded = zeros((H, 32, D), f4)
        padded[:, :HD] = w.reshape(H, HD, D)
        return chunks(padded.reshape(H * 32, D), 128)

    a["a0_qkv"], a["a0_proj"] = chunks(x["L0_ffn_qkv_w"].T, FC), spread(x["L0_ffn_proj_w"].T)
    a["a1_qkv"], a["a1_proj"] = chunks(x["L1_attn_W_attn"], FC), spread(x["L1_attn_W_proj"])
    a["a2_qkv"], a["a2_proj"] = chunks(x["L1_ffn_Wqkv"], FC), spread(x["L1_ffn_Wproj"])
    a["a0_projb"], a["a1_projb"] = x["L0_ffn_proj_b"][None], x["L1_attn_b_proj"][None]
    a["a1_qkb"], a["a1_vb"] = cols(x["L1_attn_b_attn"][:2 * D], FC), x["L1_attn_b_attn"][None, 2 * D:]
    for m, pre in (("m0", "L0_ffn_"), ("m1", "L1_ffn_")):
        for n in ("ln1", "ln2"):
            a[f"{m}_{n}"] = np.concatenate([cols(x[f"{pre}{n}_g"], FC), cols(x[f"{pre}{n}_b"], FC)], 1)
    a["m0_gate"], a["m1_gate"] = chunks(x["L0_ffn_gate_w"].T, FC), chunks(x["L1_ffn_Wrouter"], FC)
    w1 = {"m0": x["L0_ffn_w1"].transpose(2, 0, 1), "m1": x["L1_ffn_W1"].transpose(1, 0, 2)}
    w2 = {"m0": x["L0_ffn_w2"].transpose(0, 2, 1), "m1": x["L1_ffn_W2"]}
    for m in ("m0", "m1"):
        a[f"{m}_w1"] = chunks(w1[m].reshape(D, E * FF), FC)
        a[f"{m}_w2"] = w2[m].reshape(E, FM, 128, D).transpose(2, 0, 1, 3).reshape(128, E * FM * D)
    a["m0_gateb"], a["m0_b2"] = x["L0_ffn_gate_b"][None], x["L0_ffn_b2"]
    a["m0_b1"] = x["L0_ffn_b1"].reshape(E, FM, 128).transpose(2, 0, 1).reshape(128, E * FM)
    return a


def program(nc, stages=7):
    dram = {n: nc.dram_tensor(n, tuple(s), F32, kind="ExternalInput").ap() for n, s in load_shapes().items()}
    out = nc.dram_tensor("out", (TILES, 128, D), F32, kind="ExternalOutput").ap()
    build(nc, dram, out, stages)


def kernel(**inputs):
    import concourse.bacc as bacc
    from concourse.bass_utils import run_bass_kernel_spmd

    nc = bacc.Bacc("TRN2", target_bir_lowering=False, num_devices=1)
    program(nc)
    x = {n: np.asarray(v) for n, v in inputs.items()}
    arrays = {n: np.ascontiguousarray(v) for n, v in layout(x).items()}
    r = run_bass_kernel_spmd(nc, [arrays], core_ids=[0])
    got = np.asarray(r.results[0]["out"])
    return got.reshape(IMAGES, PITCH, D)[:, :PATCHES]
```

```python
from contextlib import ExitStack

import concourse.bass as bass
import concourse.mybir as mybir
import numpy as np
from concourse.alu_op_type import AluOpType as ALU

ACT = mybir.ActivationFunctionType
AX = mybir.AxisListType
F32 = mybir.dt.float32
F16 = mybir.dt.float16

IMAGES, PATCHES, PITCH = 64, 25, 32
PER_TILE = 128 // PITCH
TILES = IMAGES // PER_TILE
GROUPS = 4
GT = TILES // GROUPS
GI = GT * PER_TILE
TOK = GI * PATCHES
PAD = GI * PITCH
D, FC = 192, 96
KC = D // FC
PATCH_K = 3 * 16 * 16
PK = PATCH_K // 128
EPS = 1e-5
LH, LD, LG = 12, 64, 4
INNER = LH * LD
PAIRS = LH // 2
CHUNKS = PAIRS * LG
WM = INNER // 128
QQ = LG * PATCHES
NORM_EPS = 1e-6 * float(np.sqrt(2 * LD))
H, HD = 12, 16
HPC = FC // HD
HQ = 128 // 32
HC = H // HQ
E, FF = 8, 768
FM = FF // 128
Q_SCALE, FEAT_SCALE = 8192.0, 64.0
SQ_SCALE = 16.0
QUARTERS = 4
SLOTS = 4
W_SCALE = 1024.0
UNITS = 2 * E
RING = 8
assert (E * FM) % RING == 0


def load_shapes():
    shapes = {
        "patches": [TILES, 128, PATCH_K], "conv_w": [128, PK * D], "conv_b": [1, D], "pos": [128, D],
        "wk": [FC, KC * INNER], "wv": [FC, KC * INNER], "wqT": [128, CHUNKS * D], "wt2": [128, LG * 128],
        "bt2": [128, LG], "gt2": [128, LG], "betat2": [128, LG],
        "wf": [WM, 128, CHUNKS * 128], "bf": [128, WM], "gf": [128, WM], "betaf": [128, WM],
        "wo": [128, WM * D], "bo": [1, D],
        "ident": [128, 128], "center": [128, 128], "mean768": [128, 128], "key_sum": [128, 128],
        "var_pick": [128, CHUNKS * 2 * CHUNKS], "rstd_pick": [FC, CHUNKS * 128],
        "slot_mask": [128, 2 * 2], "v_mask": [128, 2 * 128],
        "head_mask": [FC, HPC], "causal": [128, PATCHES], "before": [128, E * E],
    }
    for a in ("a0", "a1", "a2"):
        shapes |= {f"{a}_qkv": [FC, KC * 3 * D], f"{a}_proj": [128, HC * D]}
    shapes |= {"a0_projb": [1, D], "a1_projb": [1, D], "a1_qkb": [FC, 2 * KC], "a1_vb": [1, D]}
    for m in ("m0", "m1"):
        shapes |= {f"{m}_ln1": [FC, 2 * KC], f"{m}_ln2": [FC, 2 * KC], f"{m}_gate": [FC, KC * E],
                   f"{m}_w1": [FC, KC * E * FF], f"{m}_w2": [128, E * FM * D]}
    shapes |= {"m0_gateb": [1, E], "m0_b1": [128, E * FM], "m0_b2": [E, D]}
    return shapes


def build(nc, dram, out, stages=7):
    ctx = ExitStack()
    with ctx:
        def sem(name):
            return ctx.enter_context(nc.semaphore(name))

        def sb(name, shape, scope=ctx, dtype=F32):
            return scope.enter_context(nc.sbuf_tensor(name, shape, dtype))

        bank = [ctx.enter_context(nc.psum_tensor(f"bank{k}", [128, 512], F32)) for k in range(2)]
        psum_s = ctx.enter_context(nc.psum_tensor("psum_s", [128, H, 128], F32))
        psum_o = ctx.enter_context(nc.psum_tensor("psum_o", [128, H, 128], F32))
        s_flat = psum_s[:, :, :].rearrange("p h f -> p (h f)")
        o_flat = psum_o[:, :, :].rearrange("p h f -> p (h f)")
        PB = [bank[0][:, :], bank[1][:, :]] + [s_flat[:, 512 * k:512 * k + 512] for k in range(3)] \
            + [o_flat[:, 512 * k:512 * k + 512] for k in range(3)]

        hid = sb("hid", [128, TILES, D])
        ident = sb("ident_sb", [128, 128])
        half = sb("half", [128, GT])
        eps = sb("eps_sb", [128, 1])
        neps = sb("neps_sb", [128, 1])
        stats = sb("stats", [128, GT, 6])
        mv = sb("mv", [128, GT, 2])
        ve = sb("ve", [128, GT])
        rstd = sb("rstd", [128, GT])
        junk = sb("junk", [128, 1])
        pool_junk = sb("pool_junk", [128, 1])
        xn = sb("xn", [128, GT, D])
        xT = sb("xT", [FC, KC, PAD])

        ident_in = sem("ident_in")
        fills = sem("fills")

        lin = ExitStack()
        patch_t = sb("patch_t", [128, GT, PK, 128], lin)
        conv_w = sb("conv_w_sb", [128, PK, D], lin)
        posb = sb("posb", [128, D], lin)
        feat = sb("feat", [128, CHUNKS, TOK], lin)
        QC = CHUNKS // QUARTERS
        wqt = [sb(f"wqt_{part}", [FC, KC, CHUNKS, 128], lin, F16) for part in ("high", "low")]
        wf_new = sb("wf_new", [128, SLOTS, QC, 128], lin)
        wf16 = [sb(f"wf_{part}", [128, SLOTS, QC, 128], lin, F16) for part in ("high", "low")]
        kpos = sb("kpos", [128, GI, 2, PITCH], lin)
        kneg = sb("kneg", [128, GI, 2, PITCH], lin)
        upos = sb("upos", [128, 2, LG, TOK], lin)
        uneg = sb("uneg", [128, 2, LG, TOK], lin)
        vblk = sb("vblk", [128, 2, 2, 2, 128], lin)
        scor = sb("scor", [128, 3, 2 * QQ], lin)
        denb = sb("denb", [128, 2, TOK], lin)
        rec = sb("rec", [128, TOK], lin)
        gq = sb("gq", [128, 2, TOK], lin)
        wk = [sb(f"wk_{part}", [FC, KC, INNER], lin, F16) for part in ("high", "low")]
        wv = [sb(f"wv_{part}", [FC, KC, INNER], lin, F16) for part in ("high", "low")]
        wo = sb("wo_sb", [128, WM, D], lin)
        bob = sb("bob", [128, D], lin)
        center = sb("center_sb", [128, 128], lin)
        mean768 = sb("mean768_sb", [128, 128], lin)
        key_sum = sb("key_sum_sb", [128, 128], lin)
        var_pick = sb("var_pick_sb", [128, CHUNKS, 2 * CHUNKS], lin, F16)
        rstd_pick = sb("rstd_pick_sb", [FC, CHUNKS, 128], lin)
        slot_mask = sb("slot_mask_sb", [128, 2, 2], lin)
        v_mask = sb("v_mask_sb", [128, 2, 128], lin)
        lcol = sb("lcol", [128, 4, LG], lin)
        fcol = sb("fcol", [128, 3, WM], lin)
        sqb = denb
        sq16 = vblk[:, :, :, :, :].rearrange("p s j b m -> p (s j b m)")[:, 0:2 * TOK].bitcast(F16)\
            .rearrange("p (s a t) -> p s a t", s=2, a=2)
        dup = patch_t[0:FC, :, :, :].rearrange("p t k n -> p (t k n)")[:, 0:KC * GI * 2 * PITCH].bitcast(F16)
        xdup = [dup[:, a * KC * GI * 2 * PITCH:(a + 1) * KC * GI * 2 * PITCH].rearrange("p (k b h t) -> p k b h t", k=KC, b=GI, h=2)
                for a in range(2)]
        xT16 = xT[:, :, :].bitcast(F16)
        x16 = [xT16[:, :, a * PAD:a * PAD + PAD] for a in range(2)]
        feat16 = feat[:, :, :].bitcast(F16)
        out16 = [feat16[:, :, a * TOK:a * TOK + TOK] for a in range(2)]
        qstd = rec[0:2 * CHUNKS, :]
        qrstd = sb("qrstd", [FC, TOK], lin)
        wqT = feat[:, :, :].rearrange("p c t -> p (c t)")[:, 0:CHUNKS * D].rearrange("p (c d) -> p c d", d=D)
        kv_new = [feat[0:FC, :, :].rearrange("p c t -> p (c t)")[:, CHUNKS * D + a * KC * INNER:CHUNKS * D + (a + 1) * KC * INNER]
                  .rearrange("p (k n) -> p k n", k=KC) for a in range(2)]
        wt2 = upos[:, 0, :, 0:128]
        y768 = upos[:, :, :, :].rearrange("p a g t -> p (a g t)")[:, 0:WM * TOK].rearrange("p (m t) -> p m t", t=TOK)
        ysq = uneg[:, :, :, :].rearrange("p a g t -> p (a g t)")[:, 0:WM * TOK].rearrange("p (m t) -> p m t", t=TOK)
        fused = patch_t[:, :, :, :].rearrange("p t k n -> p (t k n)").rearrange("p (m t) -> p m t", t=PAD)
        ystd = scor[:, :, :].rearrange("p s n -> p (s n)")[:, 0:TOK]
        lin.close()

        late = ExitStack()
        xres = sb("xres", [128, TILES, D], late)
        w1 = [sb(f"w1_{part}", [FC, KC, E, FF], late, F16) for part in ("high", "low")]
        w2 = [sb(f"w2_{part}", [128, E, FM, D], late, F16) for part in ("high", "low")]
        arrival = sb("arrival", [128, KC * FF], late)
        gate_w = sb("gate_w_sb", [FC, 2, KC, E], late)
        gate_b = sb("gate_b_sb", [128, E], late)
        bias1 = sb("b1_sb", [128, E * FM], late)
        bias2 = sb("b2_sb", [E, D], late)
        before = sb("before_sb", [128, E, E], late)
        head_mask = sb("head_mask_sb", [FC, HPC], late)
        causal = sb("causal_sb", [128, PATCHES], late)
        proj_b = [sb(f"proj_b{a}", [128, D], late) for a in range(2)]
        qk_b = sb("qk_b", [FC, 2, KC], late)
        v_b = sb("v_b", [128, D], late)
        ln_cols = sb("ln_cols", [FC, 4, 2, KC], late)
        qkv_w = [sb("qkv_w0", [FC, KC, 3 * D], late)]
        qkv_w.append(sb("qkv_w1", [FC, KC, 3 * D], late))
        proj_w = [sb(f"proj_w{a}", [128, HC, D], late) for a in range(2)]
        xh = [sb(f"x_{part}", [FC, KC, PAD], late, F16) for part in ("high", "low")]
        gelu_out = sb("gelu_out", [128, 3, TOK], late)
        xTa = sb("xTa", [FC, KC, PAD], late)
        qT = sb("qT", [FC, KC, PAD], late)
        kT = xTa
        kexp = sb("kexp", [FC, 2, KC, HPC, 128], late)
        vt = sb("vt", [128, GT, H, 32], late)
        sx = sb("sx", [128, 2, H, PATCHES], late)
        pr = sb("pr", [128, 2, H, PITCH], late)
        pT = sb("pT", [128, H, 128], late)
        smax = sb("smax", [128, 2, H], late)
        ssum = sb("ssum", [128, 2, H], late)
        srec = sb("srec", [128, 2, H], late)
        aoT = sb("aoT", [128, HC, 128], late)
        he = [sb(f"he_{part}", [128, RING, GI, PITCH], late, F16) for part in ("high", "low")]
        lg = sb("lg", [128, GT, E], late)
        gtr = sb("gtr", [128, GT, E, E], late)
        eqr = sb("eqr", [128, GT, E, E], late)
        rank = sb("rank", [128, GT, E], late)
        picked = sb("picked", [128, GT, E], late)
        lmax = sb("lmax", [128, GT], late)
        lexp = sb("lexp", [128, GT, E], late)
        lsum = sb("lsum", [128, GT], late)
        lrec = sb("lrec", [128, GT], late)
        cw = sb("cw", [128, GT, E], late)
        cw_y = sb("cw_y", [128, GT, E], late)
        cwT = sb("cwT", [E, PAD], late)
        late.close()

        ATT = [dict(double=True, causal=False, ln=0), dict(double=False, causal=True, ln=None),
               dict(double=True, causal=False, ln=2)]
        MOE = [dict(ln=1, biased=True), dict(ln=3, biased=False)]

        patch_in = [sem(f"patch_in{t}") for t in range(GT)]
        conv_in = sem("conv_in")
        emb_ready, emb_free = sem("emb_ready"), sem("emb_free")
        wq_in, lin_in = sem("wq_in"), sem("lin_in")
        wqt_ready, wqt_kept = sem("wqt_ready"), sem("wqt_kept")
        lin_fill = sem("lin_fill")
        lfront = dict(ln=sem("l_ln"), rs=sem("l_rs"), xTp=sem("l_xTp"), xTs=sem("l_xTs"))
        q_ready, gelu_done, c_ready, c_kept, sq_done, var_acc = map(
            sem, ("q_ready", "gelu_done", "c_ready", "c_kept", "sq_done", "var_acc"))
        std_ready, rstd_ready, rb_ready, w_ready, u_done = map(
            sem, ("std_ready", "rstd_ready", "rb_ready", "w_ready", "u_done"))
        xdup_done = sem("xdup_done")
        sq_low = sem("sq_low")
        k_ready, kpm_done, v_ready, vblk_done, st_done = map(
            sem, ("k_ready", "kpm_done", "v_ready", "vblk_done", "st_done"))
        s_ready = [sem(f"s_ready{b2}") for b2 in range(2)]
        den_ready, num_ready, den_kept, rec_done, prob_done, out_done = map(
            sem, ("den_ready", "num_ready", "den_kept", "rec_done", "prob_done", "out_done"))
        wf_in = [sem(f"wf_in{k}") for k in range(SLOTS)]
        wf_high, wf_low, wf_used = sem("wf_high"), sem("wf_low"), sem("wf_used")
        wqt_low, kv_high, kv_low, l_xlow, out_high = map(sem, ("wqt_low", "kv_high", "kv_low", "l_xlow", "out_high"))
        wf_free, mean_ready, yc_done, ysq_done, yvar_ready, ystd_done, yrec_done, yn_done = map(
            sem, ("wf_free", "mean_ready", "yc_done", "ysq_done", "yvar_ready", "ystd_done",
                  "yrec_done", "yn_done"))
        fused_done, z_ready, z_added, hid_done = map(sem, ("fused_done", "z_ready", "z_added", "hid_done"))
        late_in, late_fill = sem("late_in"), sem("late_fill")
        late_rest_in = sem("late_rest_in")
        a2_in = sem("a2_in")
        unit_in, unit_high, unit_low = sem("unit_in"), sem("unit_high"), sem("unit_low")
        att_all = {n: sem(f"a_{n}") for n in (
            "xTp", "xTs", "q_p", "q_sb", "k_p", "k_sb", "v_p", "v_sb", "kx", "s_p", "shifted",
            "exp_done", "norm", "p_t", "o_p", "oT_sb", "y_p", "y_done")}
        moe_all = {n: sem(f"m_{n}") for n in (
            "xTp", "xTs", "g_p", "shifted", "exp_done", "cw_ready", "cwT_p", "cwT_sb", "h_p", "h_act", "h_low", "chain",
            "done", "x_high", "x_low")}
        AS = [att_all | {n: sem(f"a{a}_{n}") for n in ("ln", "rs", "chain")} for a in range(3)]
        MS = [moe_all | {n: sem(f"m{m}_{n}") for n in ("ln", "rs", "y_p", "y_acc")} for m in range(2)]
        out_sem = sem("out_sem")

        class Chain:

            def __init__(self, eng, counter, i, per):
                self.eng, self.counter, self.base, self.per, self.n = eng, counter, i * per, per, 0

            def step(self, ins):
                ins.then_inc(self.counter, 1)
                self.n += 1

            def wait(self):
                self.eng.wait_ge(self.counter, self.base + self.n)

            def end(self):
                assert self.n == self.per, (self.n, self.per)

        def row(name, parts, size):
            a = dram[name]
            return bass.AP(a.tensor, 0, [[0, parts], [1, size]])

        def compact(view):
            return view.rearrange("p (b q) -> p b q", q=PITCH)[:, :, 0:PATCHES]

        def front_piece_dve(dve, i, S, src, double, piece):
            rounds = 2 if double else 1
            r, part = piece // 3, piece % 3
            if r >= rounds:
                return
            tiles = src if r == 0 else xres
            ch = Chain(dve, S["ln"], i, 4 * rounds)
            ch.n = 4 * r + (0, 1, 3)[part]
            if part == 0:
                if r:
                    ch.wait()
                    dve.memset(junk[:, :], 0.0)
                for t in range(GT):
                    last = dve.bn_stats(stats[:, t, :], tiles[:, bass.ds(i * GT + t, 1), :])
                ch.step(last)
            if part == 1:
                ch.wait()
                dve.memset(junk[:, :], 0.0)
                for t in range(GT):
                    last = dve.bn_aggr(mv[:, t, :], stats[:, t, :])
                ch.step(last)
                ch.wait()
                ch.step(dve.tensor_scalar(ve[:, :], mv[:, :, 1], EPS, None, ALU.add))
            if part == 2:
                dve.wait_ge(S["rs"], i * rounds + r + 1)
                for t in range(GT):
                    dst = xres[:, bass.ds(i * GT + t, 1), :] if r + 1 < rounds else xn[:, t, :]
                    last = dve.tensor_scalar(dst, tiles[:, bass.ds(i * GT + t, 1), :], mv[:, t, 0:1],
                                             rstd[:, t:t + 1], ALU.subtract, ALU.mult)
                ch.step(last)

        def front_dve(dve, i, S, src, double):
            for piece in range(6):
                front_piece_dve(dve, i, S, src, double, piece)

        def front_round_pool(pool, i, S, double, r):
            rounds = 2 if double else 1
            if r < rounds:
                pool.wait_ge(S["ln"], i * (4 * rounds) + 4 * r + 3)
                pool.tensor_tensor(rstd[:, :], ve[:, :], half[:, :], ALU.pow).then_inc(S["rs"], 1)

        def front_pool(pool, i, S, double):
            for r in range(2):
                front_round_pool(pool, i, S, double, r)

        def front_pe(pe, i, S, double, banks=(0, 1)):
            per = 8 if double else 4
            pe.wait_ge(S["ln"], i * per + per)
            for t in range(GT):
                for k in range(KC):
                    last = pe.transpose(PB[banks[k]][0:FC, 128 * t:128 * t + 128], xn[:, t, FC * k:FC * k + FC],
                                        ident[:, :])
            last.then_inc(S["xTp"], 1)

        def front_act(act, v, S, ln, banks=(0, 1), xT=xT):
            act.wait_ge(S["xTp"], v + 1)
            for k in range(KC):
                if ln is None:
                    last = act.activation(xT[:, k, :], PB[banks[k]][0:FC, :], ACT.Copy)
                else:
                    last = act.activation(xT[:, k, :], PB[banks[k]][0:FC, :], ACT.Identity,
                                          scale=ln_cols[:, ln, 0, k:k + 1], bias=ln_cols[:, ln, 1, k:k + 1])
                last.then_inc(S["xTs"], 1)

        HALVES = ((0, 0), (0, 1), (1, 0))

        TAIL = dict(mean=2, center=3, square=5, var=9, std=10, rec=11, scale=12, gelu=14, out=20)
        FRONT = 3
        LAG = LG + 1
        LIN_STEPS = CHUNKS + LAG + 3
        PIECES = WM * QUARTERS
        WF_BANKS = (0, 2)
        EARLY = {LIN_STEPS - 3: 0, LIN_STEPS - 2: 1, LIN_STEPS - 1: 2}

        def wait_scores(eng, n):
            for b2 in range(2):
                eng.wait_ge(s_ready[b2], n)

        def out_views(a, pp, bg, b2):
            dst = out16[a][:, LG * pp:LG * pp + LG, :].rearrange("p g (n j b q) -> p n b j g q", j=2, b=2, q=PATCHES)[:, bg, b2, :, :, :]
            return dst, PB[6][:, 2 * QQ * b2:2 * QQ * b2 + 2 * QQ].rearrange("p (j g q) -> p j g q", j=2, g=LG)

        def lin_passes(eng, body):
            body(0, False, True)
            with eng.Fori(1, GROUPS - 1) as i:
                body(i, True, True)
            body(GROUPS - 1, True, False)

        PAIR = lambda e, u: {(e, 0): [f"s{u}"], (e, 1): [f"p{u}"], (e, 2): [f"o{2 * u}"], (e, 3): [f"y{2 * u}"],
                             (e, 4): [f"o{2 * u + 1}"], (e, 5): [f"y{2 * u + 1}"]}
        PLACES = [{(0, 5): ["f0", "f1"], (1, 0): ["f2", "f3"], (1, 1): ["f4", "f5"], (1, 3): ["transpose"], (1, 5): ["q"],
                   (2, 1): ["v"], (2, 3): ["k"], (2, 4): ["kx0"], (2, 5): ["kx1"], **PAIR(3, 0), **PAIR(4, 1)},
                  {(4, 3): ["f0", "f1"], (4, 4): ["f2"], (5, 0): ["transpose"], (5, 1): ["q"], (5, 2): ["v"], (5, 3): ["k"],
                   (5, 4): ["kx0"], (5, 5): ["kx1"], **PAIR(6, 0), **PAIR(7, 1)}]
        for places in PLACES:
            after = [p for p in places if "s1" in places[p]][0]
            places[(after[0] - 1, 4)] = places[(after[0] - 1, 4)] + ["kx2"]
            places[(after[0] - 1, 5)] = places[(after[0] - 1, 5)] + ["kx3"]
        WEIGHTS = (0, 4)
        GATE_EXP = (0, 3)
        NEXT_FRONT = (7, 2)

        def passes(eng, run):
            run(0, 0, 1, (0, 1, 1), None, (0, 1))
            with eng.Fori(1, GROUPS - 1) as i:
                run(0, i, i * 2, (0, i + 1, i * 2), (1, i - 1, i * 2 + 1), (0, i + 1))
            run(0, GROUPS - 1, 6, (2, 0, 6), (1, 2, 7), (1, 0))
            run(1, 0, 8, (2, 1, 8), (1, 3, 9), (1, 1))
            with eng.Fori(1, GROUPS - 1) as i:
                run(1, i, i + 9, (2, i + 1, i + 9), None, (1, i + 1))
            run(1, GROUPS - 1, 12, None, None, None)

        def unit(u):
            e = u // 2
            if u % 2 == 0:
                return arrival[0:FC, 0:KC * FF].rearrange("p (k n) -> p k n", k=KC), [w[:, :, e, :] for w in w1]
            return arrival[:, 0:FM * D].rearrange("p (m n) -> p m n", n=D), [w[:, e, :, :] for w in w2]

        def units_after(n, i, e, m):
            first_pass = isinstance(i, int) and (n, i) == (0, 0)
            last_pass = isinstance(i, int) and (n, i) == (0, GROUPS - 1)
            next_pass = isinstance(i, int) and (n, i) == (1, 0)
            at = {2: 0, 4: 1}.get(m)
            if at is None:
                return []
            if first_pass and 2 * e < UNITS // 2:
                return [(0, UNITS // 2 + 2 * e + at)]
            if last_pass and e >= 1:
                return [(1, 2 * (e - 1) + at)]
            if next_pass and e == 0:
                return [(1, UNITS - 2 + at)]
            return []

        BIAS_COPY, BIAS_SUM = (1, 3), (1, 4)

        def order(biased, e):
            return 1 if e < 0 else e + (biased and e >= 1)

        def first_job(v):
            return isinstance(v, int) and v == 0

        def job_steps(step, eng, job1, job2, e, m):
            for job, places in zip((job1, job2), PLACES):
                if job is not None:
                    for name in places.get((e, m), []):
                        step(eng, *job, name)

        TAIL_UNITS = [5, 10, 12, 19]

        def last_tail(tail, split=None):
            for c in range(CHUNKS):
                tail(GROUPS - 1, c)
                if split is not None and stages >= 3 and c in TAIL_UNITS:
                    split(0, TAIL_UNITS.index(c))

        def whole_job(step, eng, job, split=None):
            u = len(TAIL_UNITS)
            for n, names in enumerate(PLACES[0].values()):
                for name in names:
                    step(eng, *job, name)
                if split is not None and u < UNITS // 2 and n % 2:
                    split(0, u)
                    u += 1
            assert split is None or u == UNITS // 2

        def stage_done(n):
            return [(emb_free, TILES + 2), (hid_done, TILES), (moe_all["done"], 2 * GROUPS)][n]

        block = ctx.enter_context(nc.Block())

        @block.sync
        def _(sp):
            sp.dma_start(conv_w[:, :, :].rearrange("p k d -> p (k d)"), dram["conv_w"][:, :]).then_inc(conv_in, 16)
            sp.dma_start(posb[:, :], dram["pos"][:, :]).then_inc(conv_in, 16)
            sp.dma_start(xn[:, 0, :], row("conv_b", 128, D)).then_inc(conv_in, 16)

            def load_patches(i, t):
                sp.dma_start(patch_t[:, t, :, :].rearrange("p k n -> p (k n)"),
                             dram["patches"][bass.ds(i * GT + t, 1), :, :].rearrange("o p n -> p (o n)"))\
                  .then_inc(patch_in[t], 16)

            for t in range(GT):
                load_patches(0, t)
            with sp.Fori(1, GROUPS) as i:
                for t in range(GT):
                    sp.wait_ge(emb_ready, i * GT + t + 1 - GT)
                    load_patches(i, t)
            if stages < 2:
                sp.wait_ge(*stage_done(0))
            if stages >= 2:
                with sp.Fori(0, GROUPS) as i:
                    for q in range(PIECES):
                        m, r = q // QUARTERS, q % QUARTERS
                        sp.wait_ge(wf_low, i * PIECES + q + 1)
                        sp.dma_start(wf_new[:, q % SLOTS, :, :].rearrange("p c n -> p (c n)"),
                                     dram["wf"][m, :, QC * 128 * r:QC * 128 * r + QC * 128]).then_inc(wf_in[q % SLOTS], 16)
            if stages >= 3:
                sp.wait_ge(wf_used, GROUPS * PIECES)
                sp.dma_start(qkv_w[0][:, :, :].rearrange("p k n -> p (k n)"), dram["a0_qkv"][:, :]).then_inc(late_in, 16)
                for a in range(2):
                    sp.dma_start(proj_b[a][:, :], row(f"a{a}_projb", 128, D)).then_inc(late_in, 16)
                sp.dma_start(qk_b[:, :, :].rearrange("p a k -> p (a k)"), dram["a1_qkb"][:, :]).then_inc(late_in, 16)
                sp.dma_start(v_b[:, :], row("a1_vb", 128, D)).then_inc(late_in, 16)
                for n, name in enumerate(("m0_ln1", "m0_ln2", "m1_ln1", "m1_ln2")):
                    sp.dma_start(ln_cols[:, n, :, :].rearrange("p a k -> p (a k)"), dram[name][:, :]).then_inc(late_in, 16)
                for m in range(2):
                    sp.dma_start(gate_w[:, m, :, :].rearrange("p k n -> p (k n)"), dram[f"m{m}_gate"][:, :]).then_inc(late_in, 16)
                sp.dma_start(head_mask[:, :], dram["head_mask"][:, :]).then_inc(late_in, 16)
                sp.dma_start(causal[:, :], dram["causal"][:, :]).then_inc(late_in, 16)
                sp.dma_start(before[:, :, :].rearrange("p a b -> p (a b)"), dram["before"][:, :]).then_inc(late_in, 16)
                sp.dma_start(gate_b[:, :], row("m0_gateb", 128, E)).then_inc(late_in, 16)
                sp.dma_start(bias1[:, :], dram["m0_b1"][:, :]).then_inc(late_in, 16)
                sp.dma_start(bias2[:, :], dram["m0_b2"][:, :]).then_inc(late_in, 16)

                def load_unit(n, u):
                    e = u // 2
                    if n or u:
                        sp.wait_ge(unit_low, n * UNITS + u)
                    if u % 2 == 0:
                        part = dram[f"m{n}_w1"].rearrange("p (k e n) -> p k e n", k=KC, e=E)[:, :, e, :]
                    else:
                        part = dram[f"m{n}_w2"][:, FM * D * e:FM * D * e + FM * D].rearrange("p (m n) -> p m n", n=D)
                    sp.dma_start(unit(u)[0], part).then_inc(unit_in, 16)

                for u in range(len(TAIL_UNITS)):
                    load_unit(0, u)
                sp.wait_ge(*stage_done(1))
                sp.dma_start(qkv_w[1][:, :, :].rearrange("p k n -> p (k n)"), dram["a1_qkv"][:, :]).then_inc(late_rest_in, 16)
                for a in range(2):
                    sp.dma_start(proj_w[a][:, :, :].rearrange("p k n -> p (k n)"), dram[f"a{a}_proj"][:, :]).then_inc(late_rest_in, 16)
                for u in range(len(TAIL_UNITS), UNITS):
                    load_unit(0, u)
                sp.wait_ge(att_all["y_done"], 5 * GT)
                sp.dma_start(qkv_w[0][:, :, :].rearrange("p k n -> p (k n)"), dram["a2_qkv"][:, :]).then_inc(a2_in, 16)
                sp.dma_start(proj_w[0][:, :, :].rearrange("p k n -> p (k n)"), dram["a2_proj"][:, :]).then_inc(a2_in, 16)
                for u in range(UNITS):
                    load_unit(1, u)
            if stages < 3:
                sp.wait_ge(*stage_done(stages - 1))
                for t in range(TILES):
                    sp.dma_start(out[t, :, :], hid[:, t, :]).then_inc(out_sem, 16)
                sp.wait_ge(out_sem, 16 * TILES)
            else:
                with sp.Fori(0, GROUPS) as i:
                    sp.wait_ge(MS[1]["done"], i + GROUPS + 1)
                    sp.dma_start(out[bass.ds(i * GT, GT), :, :].rearrange("t p d -> p t d"),
                                 hid[:, bass.ds(i * GT, GT), :]).then_inc(out_sem, 16)
                sp.wait_ge(out_sem, 16 * GROUPS)

        @block.gpsimd
        def _(pool):
            if stages >= 2:
                pool.wait_ge(fills, 3)
                pool.memset(kpos[:, :, :, :], 0.0).then_inc(lin_fill, 1)
                pool.memset(kneg[:, :, :, :], 0.0).then_inc(lin_fill, 1)
                def lin_dup(i, tail):
                    pool.wait_ge(l_xlow, i + 1)
                    if tail:
                        pool.wait_ge(z_ready, i * GT)
                    pool.tensor_tensor(pool_junk[:, :], half[:, 0:1], half[:, 0:1], ALU.mult)
                    for a in range(2):
                        for k in range(KC):
                            pool.tensor_copy(xdup[a][:, k, :, :, :], x16[a][:, k, :].rearrange("p (b t) -> p b t", t=PITCH)
                                             .unsqueeze(2).to_broadcast([FC, GI, 2, PITCH])).then_inc(xdup_done, 1)

                def lin_pool(i, tail, front):
                    lin_dup(i, tail)
                    for n in range(CHUNKS):
                        pool.wait_ge(rec_done, i * CHUNKS + n + 1)
                        pool.wait_ge(st_done, i * CHUNKS + n + 1)
                        pool.tensor_tensor(scor[:, n % 3, :], scor[:, n % 3, :], rec[:, 2 * QQ * (n % 2):2 * QQ * (n % 2) + 2 * QQ],
                                           ALU.mult).then_inc(prob_done, 1)
                    if front:
                        front_pool(pool, i + 1, lfront, False)

                front_pool(pool, 0, lfront, False)
                lin_passes(pool, lin_pool)

            def job_pool(pool, n, g, v, name):
                if name in ("f2", "f5"):
                    front_round_pool(pool, g, AS[n], ATT[n]["double"], int(name[1]) // 3)

            def pass_pool(n, i, jobs, job1, job2, nxt):
                S, v = MS[n], i + GROUPS * n
                for e in range(E):
                    for m in range(FM):
                        k = e * FM + m
                        pool.wait_ge(S["h_act"], v * (E * FM) + k + 1)
                        pool.tensor_tensor(he[1][:, k % RING, :, 0:PATCHES],
                                           gelu_out[:, k % 3, :].rearrange("p (b q) -> p b q", q=PATCHES),
                                           he[0][:, k % RING, :, 0:PATCHES], ALU.subtract).then_inc(S["h_low"], 1)
                        job_steps(job_pool, pool, job1, job2, e, m)
                        if (e, m) == (NEXT_FRONT[0], NEXT_FRONT[1] + 2) and nxt is not None:
                            front_pool(pool, nxt[1], MS[nxt[0]], False)

            if stages >= 3:
                pool.wait_ge(*stage_done(1))
                pool.memset(pr[:, :, :, :], 0.0).then_inc(late_fill, 1)
                pool.memset(pT[:, :, :], 0.0).then_inc(late_fill, 1)
                pool.memset(vt[:, :, :, :], 0.0).then_inc(late_fill, 1)
                for part in he:
                    pool.memset(part[:, :, :, PATCHES:PITCH], 0.0).then_inc(late_fill, 1)
                whole_job(job_pool, pool, (0, 0, 0))
                front_pool(pool, 0, MS[0], False)
                passes(pool, pass_pool)

        @block.scalar
        def _(act):
            def split_act(n, u):
                source, (high, low) = unit(u)
                act.wait_ge(unit_in, 16 * (n * UNITS + u + 1))
                if n == 1:
                    act.wait_ge(MS[0]["y_p"], (GROUPS - 1) * (E + 1) + order(True, u // 2) + 1)
                act.activation(high, source, ACT.Copy, scale=W_SCALE).then_inc(unit_high, 1)

            act.dma_start(ident[:, :], dram["ident"][:, :]).then_inc(ident_in, 16)
            if stages >= 2:
                act.dma_start(wqT, dram["wqT"].rearrange("p (c d) -> p c d", d=D)).then_inc(wq_in, 16)
                act.dma_start(wt2, dram["wt2"].rearrange("p (g n) -> p g n", g=LG)).then_inc(wq_in, 16)
                for dst, name in ((kv_new[0].rearrange("p k n -> p (k n)"), "wk"), (kv_new[1].rearrange("p k n -> p (k n)"), "wv"),
                                  (wo[:, :, :].rearrange("p m n -> p (m n)"), "wo"), (center[:, :], "center"), (mean768[:, :], "mean768"),
                                  (key_sum[:, :], "key_sum"),
                                  (var_pick[:, :, :].rearrange("p c n -> p (c n)"), "var_pick"),
                                  (rstd_pick[:, :, :].rearrange("p c n -> p (c n)"), "rstd_pick"),
                                  (slot_mask[:, :, :].rearrange("p a n -> p (a n)"), "slot_mask"),
                                  (v_mask[:, :, :].rearrange("p a n -> p (a n)"), "v_mask"),
                                  (lcol[:, 0, :], "bt2"), (lcol[:, 1, :], "gt2"), (lcol[:, 2, :], "betat2"),
                                  (fcol[:, 0, :], "bf"), (fcol[:, 1, :], "gf"), (fcol[:, 2, :], "betaf")):
                    act.dma_start(dst, dram[name][:, :]).then_inc(lin_in, 16)
                act.dma_start(bob[:, :], row("bo", 128, D)).then_inc(lin_in, 16)
                act.sem_inc(wf_free, 2)
                for c in range(CHUNKS):
                    for k in range(KC):
                        n = c * KC + k
                        act.wait_ge(wqt_ready, n + 1)
                        act.activation(wqt[0][:, k, c, :], PB[2 + n % 4][0:FC, 0:128], ACT.Copy, scale=Q_SCALE).then_inc(wqt_kept, 1)
                act.wait_ge(lin_in, LIN_LOADS * 16)
                for w, new in ((wk, kv_new[0]), (wv, kv_new[1])):
                    act.activation(w[0][:, :, :], new, ACT.Copy, scale=W_SCALE).then_inc(kv_high, 1)

                def split_wf_act(i, q):
                    act.wait_ge(wf_in[q % SLOTS], i * (16 * PIECES // SLOTS) + 16 * (q // SLOTS) + 16)
                    if not isinstance(i, int) or i * PIECES + q >= SLOTS:
                        act.wait_ge(wf_used, i * PIECES + q + 1 - SLOTS)
                    act.activation(wf16[0][:, q % SLOTS, :, :], wf_new[:, q % SLOTS, :, :], ACT.Copy, scale=W_SCALE)\
                       .then_inc(wf_high, 1)

                def lin_front_act(i, banks):
                    act.wait_ge(lfront["xTp"], i + 1)
                    for k in range(KC):
                        act.activation(x16[0][:, k, :], PB[banks[k]][0:FC, :], ACT.Copy).then_inc(lfront["xTs"], 1)


                def tail_act(i, c):
                    if c == TAIL["square"]:
                        act.wait_ge(yc_done, i + 1)
                        act.activation(ysq, y768, ACT.Square).then_inc(ysq_done, 1)
                    if c == TAIL["std"]:
                        act.wait_ge(yvar_ready, i + 1)
                        act.activation(ystd, PB[5][:, 0:TOK], ACT.Sqrt, bias=eps[:, :]).then_inc(ystd_done, 1)
                    m = c - TAIL["gelu"]
                    if 0 <= m < WM:
                        if m == 0:
                            act.wait_ge(yn_done, i + 1)
                        act.activation(compact(fused[:, m, :]), y768[:, m, :].rearrange("p (b q) -> p b q", q=PATCHES),
                                       ACT.Gelu, scale=fcol[:, 1, m:m + 1], bias=fcol[:, 2, m:m + 1]).then_inc(fused_done, 1)

                def lin_act(i, tail, front):
                    for c in range(CHUNKS + 1):
                        if c < CHUNKS:
                            act.wait_ge(q_ready, i * CHUNKS + c + 1)
                            if c >= 2:
                                act.wait_ge(c_ready, i * CHUNKS + c - 1)
                            act.activation(gq[:, c % 2, :], PB[c % 2][:, 0:TOK], ACT.Gelu,
                                           bias=lcol[:, 0, c % LG:c % LG + 1], scale=1 / Q_SCALE).then_inc(gelu_done, 1)
                        if c >= 1:
                            b = c - 1
                            act.wait_ge(c_kept, i * CHUNKS + b + 1)
                            if b >= 2:
                                act.wait_ge(var_acc, i * CHUNKS + b - 1)
                            act.activation(sq16[:, b % 2, 0, :], feat[:, b, :], ACT.Square, scale=SQ_SCALE)
                            act.activation(sqb[:, b % 2, :], feat[:, b, :], ACT.Square, scale=SQ_SCALE).then_inc(sq_done, 1)
                        if tail:
                            tail_act(i - 1, c)
                    act.wait_ge(var_acc, i * CHUNKS + CHUNKS)
                    act.activation(qstd, PB[4][0:2 * CHUNKS, 0:TOK], ACT.Sqrt, bias=eps[0:2 * CHUNKS, :], scale=SQ_SCALE ** -2)\
                       .then_inc(std_ready, 1)
                    for c in range(LIN_STEPS):
                        n = c - LAG - 1
                        if 0 <= n < CHUNKS:
                            act.wait_ge(den_ready, i * CHUNKS + n + 1)
                            if n >= 2:
                                act.wait_ge(rec_done, i * CHUNKS + n - 1)
                            act.activation(denb[:, n % 2, 0:2 * QQ], PB[7][:, 0:2 * QQ], ACT.Identity, bias=neps[:, :])\
                               .then_inc(den_kept, 1)
                        n = c - 1
                        if 0 <= n < CHUNKS:
                            p, g = n // LG, n % LG
                            act.wait_ge(w_ready, i * CHUNKS + n + 1)
                            if p >= 2:
                                wait_scores(act, i * CHUNKS + LG * (p - 1))
                            act.activation(upos[:, p % 2, g, :], feat[:, n, :], ACT.Relu,
                                           bias=lcol[:, 2, g:g + 1]).then_inc(u_done, 1)
                            act.activation(uneg[:, p % 2, g, :], feat[:, n, :], ACT.Relu,
                                           scale=-1.0, bias=lcol[:, 3, g:g + 1]).then_inc(u_done, 1)
                        n = c - LAG
                        if 0 <= n < CHUNKS:
                            wait_scores(act, i * CHUNKS + n + 1)
                            if n >= 3:
                                act.wait_ge(num_ready, i * CHUNKS + n - 2)
                            act.activation(scor[:, n % 3, :], PB[(1, 4)[n % 2]][:, 0:2 * QQ], ACT.Copy).then_inc(st_done, 1)
                        n = c - 2
                        if 0 <= n < CHUNKS:
                            pp, bg = n // LG, n % LG
                            act.wait_ge(k_ready, i * PAIRS + pp + 1)
                            if pp >= 1:
                                wait_scores(act, i * CHUNKS + n - LG + 1)
                            for dst, sign in ((kpos, 0), (kneg, 1)):
                                for slot in range(2):
                                    last = act.activation(
                                        dst[:, PER_TILE * bg:PER_TILE * bg + PER_TILE, slot, 0:PATCHES],
                                        PB[2][:, QQ * bg:QQ * bg + QQ].rearrange("p (b q) -> p b q", q=PATCHES),
                                        ACT.Relu, scale=slot_mask[:, sign, slot:slot + 1])
                            last.then_inc(kpm_done, 1)
                        n = c - LAG - 2
                        if 0 <= n < CHUNKS:
                            act.wait_ge(num_ready, i * CHUNKS + n + 1)
                            pp, bg = n // LG, n % LG
                            for b2 in range(2):
                                dst, part = out_views(0, pp, bg, b2)
                                last = act.activation(dst, part, ACT.Copy)
                            last.then_inc(out_high, 1)
                    for m in range(WM):
                        for q in range(QUARTERS * m, QUARTERS * m + QUARTERS):
                            if front or q + SLOTS < PIECES:
                                split_wf_act(i, q + SLOTS)
                        act.wait_ge(wf_used, i * PIECES + QUARTERS * m + QUARTERS)
                        act.activation(y768[:, m, :], PB[WF_BANKS[m % 2]][:, 0:TOK], ACT.Identity, bias=fcol[:, 0, m:m + 1],
                                       scale=1 / (W_SCALE * FEAT_SCALE)).then_inc(wf_free, 1)
                        if m == FRONT and front:
                            lin_front_act(i + 1, (4, 5))

                act.wait_ge(lin_fill, 4)
                lin_front_act(0, (0, 1))
                for q in range(SLOTS):
                    split_wf_act(0, q)
                lin_passes(act, lin_act)
                last_tail(tail_act, split_act)

            def job_act(act, n, g, v, name):
                S = att_all
                if name == "transpose":
                    front_act(act, v, S, ATT[n]["ln"], (4, 5), xTa)
                if name == "q":
                    for m in range(KC):
                        act.wait_ge(S["q_p"], v * KC + m + 1)
                        if n == 1:
                            last = act.activation(qT[:, m, :], PB[6 + m][0:FC, :], ACT.Identity, bias=qk_b[:, 0, m:m + 1])
                        else:
                            last = act.activation(qT[:, m, :], PB[6 + m][0:FC, :], ACT.Copy)
                        last.then_inc(S["q_sb"], 1)
                if name == "k":
                    act.wait_ge(S["k_p"], v * KC + KC)
                    for m in range(KC):
                        if n == 1:
                            last = act.activation(kT[:, m, :], PB[6 + m][0:FC, :], ACT.Identity, bias=qk_b[:, 1, m:m + 1])
                        else:
                            last = act.activation(kT[:, m, :], PB[6 + m][0:FC, :], ACT.Copy)
                        last.then_inc(S["k_sb"], 1)
                if name[0] == "p":
                    u = int(name[1])
                    act.wait_ge(S["shifted"], v * 2 + u + 1)
                    act.activation(pr[:, :, :, 0:PATCHES], sx[:, :, :, :], ACT.Exp).then_inc(S["exp_done"], 1)
                if name[0] == "o":
                    t = int(name[1])
                    if not (t == 0 and first_job(v)):
                        act.wait_ge(S["y_p"], v * GT + t)
                    act.wait_ge(S["o_p"], v * GT + t + 1)
                    act.activation(aoT[:, :, :].rearrange("p c n -> p (c n)"), PB[6 + t % 2][:, 0:HC * 128], ACT.Copy)\
                       .then_inc(S["oT_sb"], 1)

            def x_high_act(v, n):
                act.wait_ge(moe_all["xTp"], v + 1)
                for k in range(KC):
                    ln = MOE[n]["ln"]
                    act.activation(xh[0][:, k, :], PB[k][0:FC, :], ACT.Identity, scale=ln_cols[:, ln, 0, k:k + 1],
                                   bias=ln_cols[:, ln, 1, k:k + 1]).then_inc(moe_all["x_high"], 1)

            def pass_act(n, i, jobs, job1, job2, nxt):
                S, L = MS[n], MOE[n]
                ny = E + L["biased"]
                v = i + GROUPS * n
                for e in range(E):
                    for m in range(FM):
                        k = e * FM + m
                        act.wait_ge(S["h_p"], v * (E * FM) + k + 1)
                        if k >= RING:
                            old = (k - RING) // FM
                            act.wait_ge(S["y_p"], i * ny + order(L["biased"], old) + 1)
                        if k >= 3:
                            act.wait_ge(S["h_low"], v * (E * FM) + k - 2)
                        bias = bias1[:, k:k + 1] if L["biased"] else 0.0
                        act.activation(he[0][:, k % RING, :, 0:PATCHES],
                                       PB[k % 2][:, 0:TOK].rearrange("p (b q) -> p b q", q=PATCHES), ACT.Gelu,
                                       bias=bias, scale=1 / W_SCALE)
                        act.activation(gelu_out[:, k % 3, :], PB[k % 2][:, 0:TOK], ACT.Gelu,
                                       bias=bias, scale=1 / W_SCALE).then_inc(S["h_act"], 1)
                        if (e, m) == GATE_EXP:
                            act.wait_ge(S["shifted"], v + 1)
                            act.activation(lexp[:, :, :], lexp[:, :, :], ACT.Exp).then_inc(S["exp_done"], 1)
                        if (e, m) == BIAS_COPY and L["biased"]:
                            act.wait_ge(S["cwT_p"], i + 1)
                            act.activation(cwT[:, :], PB[6][0:E, :], ACT.Copy).then_inc(S["cwT_sb"], 1)
                        for what in units_after(n, i, e, m):
                            split_act(*what)
                        job_steps(job_act, act, job1, job2, e, m)
                if nxt is not None:
                    front_act(act, nxt[1] + GROUPS * nxt[0], MS[nxt[0]], MOE[nxt[0]]["ln"])
                    x_high_act(nxt[1] + GROUPS * nxt[0], nxt[0])

            if stages >= 3:
                act.wait_ge(*stage_done(1))
                act.wait_ge(late_in, 16 * LATE_LOADS)
                whole_job(job_act, act, (0, 0, 0), split_act)
                front_act(act, 0, MS[0], MOE[0]["ln"])
                x_high_act(0, 0)
                passes(act, pass_act)
            if stages < 2:
                act.wait_ge(ident_in, 16)

        @block.vector
        def _(dve):
            def split_dve(n, u):
                source, (high, low) = unit(u)
                dve.wait_ge(unit_high, n * UNITS + u + 1)
                dve.scalar_tensor_tensor(low, source, W_SCALE, high, ALU.mult, ALU.subtract).then_inc(unit_low, 1)

            dve.memset(half[:, :], -0.5).then_inc(fills, 1)
            dve.memset(eps[:, :], EPS).then_inc(fills, 1)
            dve.memset(neps[:, :], NORM_EPS).then_inc(fills, 1)
            dve.wait_ge(conv_in, 48)
            dve.tensor_tensor(posb[:, :], posb[:, :], xn[:, 0, :], ALU.add).then_inc(fills, 1)
            dve.wait_ge(fills, 4)
            dve.sem_inc(emb_free, 2)

            def embed_dve(i):
                for t in range(GT):
                    dve.wait_ge(emb_ready, i * GT + t + 1)
                    dve.tensor_tensor(hid[:, bass.ds(i * GT + t, 1), :], PB[t % 2][:, 0:D].unsqueeze(1), posb[:, :].unsqueeze(1),
                                      ALU.add).then_inc(emb_free, 1)

            embed_dve(0)
            if stages >= 2:
                for c in range(CHUNKS):
                    for k in range(KC):
                        n = c * KC + k
                        dve.wait_ge(wqt_kept, n + 1)
                        dve.scalar_tensor_tensor(wqt[1][:, k, c, :], PB[2 + n % 4][0:FC, 0:128], Q_SCALE, wqt[0][:, k, c, :],
                                                 ALU.mult, ALU.subtract).then_inc(wqt_low, 1)
                dve.wait_ge(lin_in, LIN_LOADS * 16)
                dve.tensor_scalar(lcol[:, 3, :], lcol[:, 2, :], -1.0, None, ALU.mult).then_inc(lin_fill, 1)
                dve.memset(qrstd[:, :], 0.0).then_inc(lin_fill, 1)
                dve.sem_inc(wf_low, SLOTS)
                for n, (w, new) in enumerate(((wk, kv_new[0]), (wv, kv_new[1]))):
                    dve.wait_ge(kv_high, n + 1)
                    dve.scalar_tensor_tensor(w[1][:, :, :], new, W_SCALE, w[0][:, :, :], ALU.mult, ALU.subtract)\
                       .then_inc(kv_low, 1)

                def split_wf_dve(i, q):
                    dve.wait_ge(wf_high, i * PIECES + q + 1)
                    dve.scalar_tensor_tensor(wf16[1][:, q % SLOTS, :, :], wf_new[:, q % SLOTS, :, :], W_SCALE,
                                             wf16[0][:, q % SLOTS, :, :], ALU.mult, ALU.subtract).then_inc(wf_low, 1)

            with dve.Fori(1, GROUPS) as i:
                embed_dve(i)
            if stages >= 2:
                dve.wait_ge(lin_fill, 4)
                dve.wait_ge(*stage_done(0))
                def x_low(i, banks):
                    dve.wait_ge(lfront["xTs"], i * KC + KC)
                    for k in range(KC):
                        last = dve.tensor_tensor(x16[1][:, k, :], PB[banks[k]][0:FC, :], x16[0][:, k, :], ALU.subtract)
                    last.then_inc(l_xlow, 1)

                def tail_dve(i, c):
                    if c == TAIL["center"]:
                        dve.wait_ge(mean_ready, i + 1)
                        dve.tensor_tensor(y768, y768, PB[5][:, 0:TOK].unsqueeze(1).to_broadcast([128, WM, TOK]), ALU.subtract)\
                           .then_inc(yc_done, 1)
                    if c == TAIL["rec"]:
                        dve.wait_ge(ystd_done, i + 1)
                        dve.reciprocal(rec[:, :], ystd).then_inc(yrec_done, 1)
                    if c == TAIL["scale"]:
                        dve.wait_ge(yrec_done, i + 1)
                        dve.tensor_tensor(y768, y768, rec[:, :].unsqueeze(1).to_broadcast([128, WM, TOK]), ALU.mult)\
                           .then_inc(yn_done, 1)
                    t = c - TAIL["out"]
                    if 0 <= t < GT:
                        tile = hid[:, bass.ds(i * GT + t, 1), :]
                        dve.wait_ge(z_ready, i * GT + t + 1)
                        dve.tensor_tensor(tile, tile, PB[6 + t % 2][:, 0:D].unsqueeze(1), ALU.add).then_inc(z_added, 1)
                        dve.wait_ge(z_added, i * GT + t + 1)
                        dve.tensor_tensor(tile, tile, bob[:, :].unsqueeze(1), ALU.add).then_inc(hid_done, 1)

                def square_low(i, c):
                    dve.wait_ge(sq_done, i * CHUNKS + c + 1)
                    dve.tensor_tensor(sq16[:, c % 2, 1, :], sqb[:, c % 2, :], sq16[:, c % 2, 0, :], ALU.subtract)\
                       .then_inc(sq_low, 1)

                def lin_dve(i, tail, front):
                    for c in range(CHUNKS):
                        dve.wait_ge(c_ready, i * CHUNKS + c + 1)
                        dve.tensor_copy(feat[:, c, :], PB[2 + c % 2][:, 0:TOK]).then_inc(c_kept, 1)
                        if c >= 1:
                            square_low(i, c - 1)
                        if tail:
                            tail_dve(i - 1, c)
                    square_low(i, CHUNKS - 1)
                    dve.wait_ge(std_ready, i + 1)
                    dve.reciprocal(qrstd[0:2 * CHUNKS, :], qstd).then_inc(rstd_ready, 1)
                    for c in range(LIN_STEPS):
                        n = c - LAG - 3
                        if 0 <= n < CHUNKS:
                            dve.wait_ge(out_high, i * CHUNKS + n + 1)
                            for b2 in range(2):
                                dst, part = out_views(1, n // LG, n % LG, b2)
                                last = dve.tensor_tensor(dst, part, out_views(0, n // LG, n % LG, b2)[0], ALU.subtract)
                            last.then_inc(out_done, 1)
                        n = c - LAG - 1
                        if 0 <= n < CHUNKS:
                            dve.wait_ge(den_kept, i * CHUNKS + n + 1)
                            if n >= 2:
                                dve.wait_ge(prob_done, i * CHUNKS + n - 1)
                            dve.reciprocal(rec[:, 2 * QQ * (n % 2):2 * QQ * (n % 2) + 2 * QQ], denb[:, n % 2, 0:2 * QQ])\
                               .then_inc(rec_done, 1)
                            dve.wait_ge(v_ready, i * CHUNKS + n + 1)
                            if n >= 2:
                                dve.wait_ge(num_ready, i * CHUNKS + n - 1)
                            dve.tensor_tensor(
                                vblk[:, n % 2, :, :, :],
                                PB[3 + 2 * (n % 2)][:, 0:256].rearrange("p (j m) -> p j m", m=128).unsqueeze(2).to_broadcast([128, 2, 2, 128]),
                                v_mask[:, :, :].unsqueeze(1).to_broadcast([128, 2, 2, 128]), ALU.mult).then_inc(vblk_done, 1)
                        if c < CHUNKS:
                            dve.wait_ge(rb_ready, i * CHUNKS + c + 1)
                            dve.scalar_tensor_tensor(feat[:, c, :], feat[:, c, :], lcol[:, 1, c % LG:c % LG + 1], PB[0][:, 0:TOK],
                                                     ALU.mult, ALU.mult).then_inc(w_ready, 1)
                    for q in range(PIECES):
                        if front or q + SLOTS < PIECES:
                            split_wf_dve(i, q + SLOTS)
                        if front and q == QUARTERS:
                            front_dve(dve, i + 1, lfront, hid, False)
                        if front and q == FRONT * QUARTERS + QUARTERS - 1:
                            x_low(i + 1, (4, 5))

                front_dve(dve, 0, lfront, hid, False)
                x_low(0, (0, 1))
                for q in range(SLOTS):
                    split_wf_dve(0, q)
                lin_passes(dve, lin_dve)
                last_tail(tail_dve, split_dve)

            def job_dve(dve, n, g, v, name):
                S, L = AS[n], ATT[n]
                base = xres if L["double"] else hid
                if name[0] == "f":
                    if name == "f0":
                        if n != 1 and not first_job(v):
                            dve.wait_ge(S["y_done"], v * GT)
                        if n == 1:
                            dve.wait_ge(moe_all["done"], g + 1)
                        dve.memset(junk[:, :], 0.0)
                    front_piece_dve(dve, g, S, hid, L["double"], int(name[1]))
                if name == "v":
                    if first_job(v):
                        dve.wait_ge(late_fill, 5)
                    for j in range(2):
                        dve.wait_ge(S["v_p"], v * 2 + j + 1)
                        for t in range(2):
                            dst = vt[:, 2 * j + t, :, 0:HD]
                            part = PB[4 + j][:, D * t:D * t + D].rearrange("p (h x) -> p h x", x=HD)
                            if n == 1:
                                last = dve.tensor_tensor(dst, part, v_b[:, :].rearrange("p (h x) -> p h x", x=HD), ALU.add)
                            else:
                                last = dve.tensor_copy(dst, part)
                        last.then_inc(S["v_sb"], 1)
                if name[0:2] == "kx":
                    t = int(name[2])
                    dve.wait_ge(S["k_sb"], v * KC + KC)
                    if t >= 2:
                        dve.wait_ge(S["s_p"], v * GT + t - 1)
                    for m in range(KC):
                        last = dve.tensor_tensor(
                            kexp[:, t % 2, m, :, :], kT[:, m, 128 * t:128 * t + 128].unsqueeze(1).to_broadcast([FC, HPC, 128]),
                            head_mask[:, :].unsqueeze(2).to_broadcast([FC, HPC, 128]), ALU.mult)
                    last.then_inc(S["kx"], 1)
                if name[0] in "spy" :
                    u = int(name[1]) if name[0] in "sp" else int(name[1]) // 2
                    per_pair = 2 * (1 + L["causal"]) + 2 + 2 * (n < 2)
                    done = u * per_pair
                    if name[0] == "p":
                        done += 2 * (1 + L["causal"])
                    if name[0] == "y":
                        done += 2 * (1 + L["causal"]) + 2 + int(name[1]) % 2
                    ch = Chain(dve, S["chain"], g, 2 * per_pair)
                    ch.n = done
                if name[0] == "s":
                    for j in range(2):
                        t = 2 * u + j
                        dve.wait_ge(S["s_p"], v * GT + t + 1)
                        scores = PB[4 + j][:, 0:H * PITCH].rearrange("p (h q) -> p h q", q=PITCH)[:, :, 0:PATCHES]
                        if L["causal"]:
                            ch.step(dve.tensor_tensor(sx[:, j, :, :], scores,
                                                      causal[:, :].unsqueeze(1).to_broadcast([128, H, PATCHES]), ALU.add))
                            ch.wait()
                            scores = sx[:, j, :, :]
                        ch.step(dve.tensor_reduce(smax[:, j, :], scores, AX.X, ALU.max))
                        ch.wait()
                        last = dve.tensor_tensor(sx[:, j, :, :], scores,
                                                 smax[:, j, :].unsqueeze(2).to_broadcast([128, H, PATCHES]), ALU.subtract)
                    last.then_inc(S["shifted"], 1)
                if name[0] == "p":
                    dve.wait_ge(S["exp_done"], v * 2 + u + 1)
                    ch.step(dve.tensor_reduce(ssum[:, :, :], pr[:, :, :, 0:PATCHES], AX.X, ALU.add))
                    ch.wait()
                    ch.step(dve.reciprocal(srec[:, :, :], ssum[:, :, :]))
                    ch.wait()
                    dve.tensor_tensor(pr[:, :, :, 0:PATCHES], pr[:, :, :, 0:PATCHES],
                                      srec[:, :, :].unsqueeze(3).to_broadcast([128, 2, H, PATCHES]), ALU.mult)\
                       .then_inc(S["norm"], 1)
                    dve.wait_ge(S["norm"], v * 2 + u + 1)
                if name[0] == "p" or name in ("o0", "o2"):
                    t = 2 * u if name[0] == "p" else int(name[1]) + 1
                    if t >= 1:
                        dve.wait_ge(S["o_p"], v * GT + t)
                    for b in range(PER_TILE):
                        last = dve.transpose(pT[32 * b:32 * b + 32, :, 32 * b:32 * b + 32], pr[32 * b:32 * b + 32, t % 2, :, :])
                    last.then_inc(S["p_t"], 1)
                if name[0] == "y":
                    t = int(name[1])
                    tile = base[:, bass.ds(g * GT + t, 1), :]
                    dve.wait_ge(S["y_p"], v * GT + t + 1)
                    last = dve.tensor_tensor(tile, tile, PB[4 + t % 2][:, 0:D].unsqueeze(1), ALU.add)
                    if n < 2:
                        ch.step(last)
                        ch.wait()
                        last = dve.tensor_tensor(tile, tile, proj_b[n][:, :].unsqueeze(1), ALU.add)
                    last.then_inc(S["y_done"], 1)

            def x_low_dve(v):
                dve.wait_ge(moe_all["xTs"], v * KC + KC)
                dve.wait_ge(moe_all["x_high"], v * KC + KC)
                dve.tensor_tensor(xh[1][:, :, :], xT[:, :, :], xh[0][:, :, :], ALU.subtract).then_inc(moe_all["x_low"], 1)

            def pass_dve(n, i, jobs, job1, job2, nxt):
                S, L = MS[n], MOE[n]
                ny = E + L["biased"]
                v = i + GROUPS * n
                ch = Chain(dve, S["chain"], v, 11)
                dve.wait_ge(S["g_p"], v + 1)
                logits = PB[7][:, 0:GT * E].rearrange("p (t e) -> p t e", e=E)
                if L["biased"]:
                    last = dve.tensor_tensor(lg[:, :, :], logits, gate_b[:, :].unsqueeze(1).to_broadcast([128, GT, E]), ALU.add)
                else:
                    last = dve.tensor_copy(lg[:, :, :], logits)
                ch.step(last)
                ch.wait()
                ch.step(dve.tensor_reduce(lmax[:, :], lg[:, :, :], AX.X, ALU.max))
                ch.wait()
                dve.tensor_tensor(lexp[:, :, :], lg[:, :, :], lmax[:, :].unsqueeze(2).to_broadcast([128, GT, E]), ALU.subtract)\
                   .then_inc(S["shifted"], 1)
                other = lg[:, :, :].unsqueeze(2).to_broadcast([128, GT, E, E])
                own = lg[:, :, :].unsqueeze(3).to_broadcast([128, GT, E, E])
                ch.step(dve.tensor_tensor(gtr[:, :, :, :], other, own, ALU.is_gt))
                ch.step(dve.tensor_tensor(eqr[:, :, :, :], other, own, ALU.is_equal))
                ch.wait()
                ch.step(dve.tensor_tensor(eqr[:, :, :, :], eqr[:, :, :, :], before[:, :, :].unsqueeze(1).to_broadcast([128, GT, E, E]), ALU.mult))
                ch.wait()
                ch.step(dve.tensor_tensor(gtr[:, :, :, :], gtr[:, :, :, :], eqr[:, :, :, :], ALU.add))
                ch.wait()
                ch.step(dve.tensor_reduce(rank[:, :, :], gtr[:, :, :, :], AX.X, ALU.add))
                ch.wait()
                def weights():
                    dve.wait_ge(S["exp_done"], v + 1)
                    ch.step(dve.scalar_tensor_tensor(picked[:, :, :], rank[:, :, :], 1.5, lexp[:, :, :], ALU.is_lt, ALU.mult))
                    ch.wait()
                    ch.step(dve.tensor_reduce(lsum[:, :], picked[:, :, :], AX.X, ALU.add))
                    ch.wait()
                    ch.step(dve.reciprocal(lrec[:, :], lsum[:, :]))
                    ch.wait()
                    dve.tensor_tensor(cw[:, :, :], picked[:, :, :], lrec[:, :].unsqueeze(2).to_broadcast([128, GT, E]), ALU.mult)\
                       .then_inc(S["cw_ready"], 1)
                    dve.wait_ge(S["cw_ready"], v + 1)
                    ch.step(dve.tensor_scalar(cw_y[:, :, :], cw[:, :, :], 1 / W_SCALE, None, ALU.mult))
                    ch.wait()
                    ch.end()

                def add(e):
                    q = order(L["biased"], e)
                    dve.wait_ge(S["y_p"], i * ny + q + 1)
                    if q >= 1:
                        dve.wait_ge(S["y_acc"], i * ny + q)
                    for t in range(GT):
                        tile = xres[:, bass.ds(i * GT + t, 1), :]
                        part = PB[2 + t // 2][:, D * (t % 2):D * (t % 2) + D].unsqueeze(1)
                        if e < 0:
                            last = dve.tensor_tensor(tile, tile, part, ALU.add)
                        else:
                            last = dve.scalar_tensor_tensor(tile, part, cw_y[:, t, e:e + 1], tile, ALU.mult, ALU.add)
                    last.then_inc(S["y_acc"], 1)

                for e in range(E):
                    for m in range(FM):
                        if (e, m) == WEIGHTS:
                            weights()
                        for what in units_after(n, i, e, m):
                            split_dve(*what)
                        job_steps(job_dve, dve, job1, job2, e, m)
                        piece = m - NEXT_FRONT[1]
                        if e == NEXT_FRONT[0] and 0 <= piece < 3 and nxt is not None:
                            if piece == 0:
                                dve.wait_ge(att_all["y_done"], (job1[2] + 1) * GT)
                                dve.memset(junk[:, :], 0.0)
                            front_piece_dve(dve, nxt[1], MS[nxt[0]], xres, False, piece)
                        if m == 1 and e >= 1:
                            add(e - 1)
                        if (e, m) == BIAS_SUM and L["biased"]:
                            add(-1)
                if nxt is not None:
                    x_low_dve(nxt[1] + GROUPS * nxt[0])
                add(E - 1)
                dve.wait_ge(S["y_acc"], i * ny + ny)
                for t in range(GT):
                    tile = hid[:, bass.ds(i * GT + t, 1), :]
                    last = dve.tensor_tensor(tile, tile, xres[:, bass.ds(i * GT + t, 1), :], ALU.add)
                last.then_inc(S["done"], 1)

            if stages >= 3:
                dve.wait_ge(*stage_done(1))
                dve.wait_ge(late_in, 16 * LATE_LOADS)
                whole_job(job_dve, dve, (0, 0, 0), split_dve)
                dve.wait_ge(att_all["y_done"], GT)
                front_dve(dve, 0, MS[0], xres, False)
                x_low_dve(0)
                passes(dve, pass_dve)

        @block.tensor
        def _(pe):
            pe.wait_ge(conv_in, 48)
            def embed_pe(i):
                for t in range(GT):
                    pe.wait_ge(patch_in[t], i * 16 + 16)
                    pe.wait_ge(emb_free, i * GT + t + 1)
                    for k in range(PK):
                        last = pe.matmul(PB[t % 2][:, 0:D], patch_t[:, t, k, :], conv_w[:, k, :],
                                         start=(k == 0), stop=(k == PK - 1))
                    last.then_inc(emb_ready, 1)

            embed_pe(0)
            pe.wait_ge(ident_in, 16)
            if stages >= 2:
                pe.wait_ge(wq_in, 32)
                for c in range(CHUNKS):
                    for k in range(KC):
                        n = c * KC + k
                        if n >= 4:
                            pe.wait_ge(wqt_low, n - 3)
                        pe.matmul(PB[2 + n % 4][0:FC, 0:128], wqT[:, c, FC * k:FC * k + FC], wt2[:, c % LG, :],
                                  start=True, stop=True).then_inc(wqt_ready, 1)
            with pe.Fori(1, GROUPS) as i:
                embed_pe(i)
            if stages >= 2:
                pe.wait_ge(*stage_done(0))
                pe.wait_ge(wqt_low, CHUNKS * KC)
                pe.wait_ge(kv_low, 2)
                pe.wait_ge(lin_in, LIN_LOADS * 16)

                def tail_pe(i, s):
                    if s == TAIL["mean"]:
                        pe.wait_ge(wf_free, i * WM + WM + 2)
                        for m in range(WM):
                            last = pe.matmul(PB[5][:, 0:TOK], mean768[:, :], y768[:, m, :], start=(m == 0), stop=(m == WM - 1))
                        last.then_inc(mean_ready, 1)
                    if s == TAIL["var"]:
                        pe.wait_ge(ysq_done, i + 1)
                        for m in range(WM):
                            last = pe.matmul(PB[5][:, 0:TOK], mean768[:, :], ysq[:, m, :], start=(m == 0), stop=(m == WM - 1))
                        last.then_inc(yvar_ready, 1)
                    t = s - TAIL["out"]
                    if 0 <= t < GT:
                        if t == 0:
                            pe.wait_ge(fused_done, i * WM + WM)
                        if t >= 2:
                            pe.wait_ge(z_added, i * GT + t - 1)
                        for m in range(WM):
                            last = pe.matmul(PB[6 + t % 2][:, 0:D], fused[:, m, 128 * t:128 * t + 128], wo[:, m, :],
                                             start=(m == 0), stop=(m == WM - 1))
                        last.then_inc(z_ready, 1)

                def fuse_piece(i, q):
                    m, piece = q // QUARTERS, q % QUARTERS
                    if piece == 0 and m >= 2:
                        pe.wait_ge(wf_free, i * WM + m + 1)
                    if q in EARLY.values():
                        pairs = ((piece + 1) * QC - 1) // LG + 1
                        pe.wait_ge(out_done, i * CHUNKS + LG * pairs)
                    if q == 0:
                        pe.wait_ge(w_ready, i * CHUNKS + CHUNKS)
                    if q == QUARTERS:
                        pe.wait_ge(kpm_done, i * CHUNKS + CHUNKS)
                    pe.wait_ge(wf_low, i * PIECES + q + 1 + SLOTS)
                    for c in range(piece * QC, piece * QC + QC):
                        for r, (a, b) in enumerate(HALVES):
                            last = pe.matmul(PB[WF_BANKS[m % 2]][:, 0:TOK], wf16[a][:, q % SLOTS, c % QC, :], out16[b][:, c, :],
                                             start=(c == 0 and r == 0), stop=(c == CHUNKS - 1 and r == 2))
                    last.then_inc(wf_used, 1)

                def lin_pe(i, tail, front):
                    pe.wait_ge(l_xlow, i + 1)
                    for s in range(CHUNKS + 3):
                        if s < CHUNKS:
                            if s == 0 and tail:
                                pe.wait_ge(wf_free, i * WM + 1)
                            if s >= 2:
                                pe.wait_ge(gelu_done, i * CHUNKS + s - 1)
                            for k in range(KC):
                                for r, (a, b) in enumerate(HALVES):
                                    last = pe.matmul(PB[s % 2][:, 0:TOK], wqt[a][:, k, s, :], compact(x16[b][:, k, :]),
                                                     start=(k == 0 and r == 0), stop=(k == KC - 1 and r == 2))
                            last.then_inc(q_ready, 1)
                        if s == 1 and tail:
                            pe.wait_ge(wf_free, i * WM + 2)
                        if 1 <= s <= CHUNKS:
                            c = s - 1
                            pe.wait_ge(gelu_done, i * CHUNKS + c + 1)
                            if c >= 2:
                                pe.wait_ge(c_kept, i * CHUNKS + c - 1)
                            pe.matmul(PB[2 + c % 2][:, 0:TOK], center[:, :], gq[:, c % 2, :], start=True, stop=True)\
                              .then_inc(c_ready, 1)
                        if s >= 3:
                            c = s - 3
                            pe.wait_ge(sq_low, i * CHUNKS + c + 1)
                            for a in range(2):
                                last = pe.matmul(PB[4][0:2 * CHUNKS, 0:TOK], var_pick[:, c, :], sq16[:, c % 2, a, :],
                                                 start=(c == 0 and a == 0), stop=(c == CHUNKS - 1 and a == 1))
                            last.then_inc(var_acc, 1)
                        if tail:
                            tail_pe(i - 1, s)
                    if tail:
                        pe.wait_ge(z_added, i * GT)
                    pe.wait_ge(c_kept, i * CHUNKS + CHUNKS)
                    for c in range(LIN_STEPS):
                        p, g = c // LG, c % LG
                        n = c - LAG - 1
                        if 0 <= n < CHUNKS:
                            pe.wait_ge(st_done, i * CHUNKS + n + 1)
                            if n >= 1:
                                pe.wait_ge(den_kept, i * CHUNKS + n)
                            pe.matmul(PB[7][:, 0:2 * QQ], key_sum[:, :], scor[:, n % 3, :], start=True, stop=True)\
                              .then_inc(den_ready, 1)
                        n = c - LAG
                        if 0 <= n < CHUNKS:
                            pp, bg = n // LG, n % LG
                            if n >= 2:
                                pe.wait_ge(st_done, i * CHUNKS + n - 1)
                            pe.wait_ge(kpm_done, i * CHUNKS + n + 1)
                            if bg == 0:
                                pe.wait_ge(u_done, i * (2 * CHUNKS) + 8 * pp + 8)
                            for j in range(2):
                                for kk, uu in ((kpos, upos), (kneg, uneg)):
                                    for b2 in range(2):
                                        b = PER_TILE * bg + 2 * j + b2
                                        last = pe.matmul(PB[(1, 4)[n % 2]][64 * b2:64 * b2 + 64, QQ * j:QQ * j + QQ], kk[:, b, :, :],
                                                         uu[:, pp % 2, :, PATCHES * b:PATCHES * b + PATCHES],
                                                         start=(kk is kpos), stop=(kk is kneg))
                                        if j == 1 and kk is kneg:
                                            last.then_inc(s_ready[b2], 1)
                        n = c - LAG - 1
                        if 0 <= n < CHUNKS:
                            pp, bg = n // LG, n % LG
                            if n >= 2:
                                pe.wait_ge(vblk_done, i * CHUNKS + n - 1)
                            if n == 0:
                                pe.wait_ge(xdup_done, i * (2 * KC) + 2 * KC)
                            for j in range(2):
                                for k in range(KC):
                                    b = PER_TILE * bg + 2 * j
                                    for r, (wa, xa) in enumerate(HALVES):
                                        last = pe.matmul(PB[3 + 2 * (n % 2)][:, 128 * j:128 * j + 128], xdup[xa][:, k, b:b + 2, :, :],
                                                         wv[wa][:, k, 128 * pp:128 * pp + 128], start=(k == 0 and r == 0),
                                                         stop=(k == KC - 1 and r == 2))
                            last.then_inc(v_ready, 1)
                        if c < CHUNKS:
                            if c == 0:
                                pe.wait_ge(rstd_ready, i + 1)
                            if c >= 1:
                                pe.wait_ge(w_ready, i * CHUNKS + c)
                            pe.matmul(PB[0][:, 0:TOK], rstd_pick[:, c, :], qrstd[:, :], start=True, stop=True)\
                              .then_inc(rb_ready, 1)
                        pk = p if g == 1 and p < PAIRS else None
                        if pk is not None:
                            if pk >= 1:
                                pe.wait_ge(kpm_done, i * CHUNKS + LG * pk)
                            for k in range(KC):
                                for r, (a, b) in enumerate(HALVES):
                                    last = pe.matmul(PB[2][:, 0:TOK], wk[a][:, k, 128 * pk:128 * pk + 128], compact(x16[b][:, k, :]),
                                                     start=(k == 0 and r == 0), stop=(k == KC - 1 and r == 2))
                            last.then_inc(k_ready, 1)
                        n = c - LAG - 2
                        if 0 <= n < CHUNKS:
                            pe.wait_ge(prob_done, i * CHUNKS + n + 1)
                            pe.wait_ge(vblk_done, i * CHUNKS + n + 1)
                            if n >= 1:
                                pe.wait_ge(out_done, i * CHUNKS + n)
                            for b2 in range(2):
                                for j in range(2):
                                    col = 2 * QQ * b2 + QQ * j
                                    last = pe.matmul(PB[6][:, col:col + QQ], vblk[:, n % 2, j, b2, :],
                                                     scor[:, n % 3, QQ * j:QQ * j + QQ], start=True, stop=True)
                            last.then_inc(num_ready, 1)
                        if c in EARLY:
                            fuse_piece(i, EARLY[c])
                    pe.wait_ge(out_done, i * CHUNKS + CHUNKS)
                    for m in range(WM):
                        for q in range(m * QUARTERS, m * QUARTERS + QUARTERS):
                            if q not in EARLY.values():
                                fuse_piece(i, q)
                        if m == FRONT and front:
                            front_pe(pe, i + 1, lfront, False, (4, 5))

                front_pe(pe, 0, lfront, False)
                lin_passes(pe, lin_pe)
                last_tail(tail_pe)

            def job_pe(pe, n, g, v, name):
                S = att_all
                wq, wp = qkv_w[n % 2], proj_w[n % 2]
                if name == "transpose":
                    if n == 2:
                        pe.wait_ge(a2_in, 32)
                    if not first_job(v):
                        pe.wait_ge(S["y_done"], v * GT)
                    front_pe(pe, g, AS[n] , ATT[n]["double"], (4, 5))
                if name == "q":
                    pe.wait_ge(S["xTs"], v * 2 + 2)
                    if not first_job(v):
                        pe.wait_ge(S["oT_sb"], v * GT)
                    for j in range(KC):
                        for k in range(KC):
                            last = pe.matmul(PB[6 + j][0:FC, :], wq[:, k, FC * j:FC * j + FC], xTa[:, k, :],
                                             start=(k == 0), stop=(k == KC - 1))
                        last.then_inc(S["q_p"], 1)
                if name == "v":
                    for t in range(GT):
                        for k in range(KC):
                            last = pe.matmul(PB[4 + t // 2][:, D * (t % 2):D * (t % 2) + D], xTa[:, k, 128 * t:128 * t + 128],
                                             wq[:, k, 2 * D:3 * D], start=(k == 0), stop=(k == KC - 1))
                        if t % 2:
                            last.then_inc(S["v_p"], 1)
                if name == "k":
                    pe.wait_ge(S["q_sb"], v * KC + KC)
                    for j in range(KC):
                        for k in range(KC):
                            last = pe.matmul(PB[6 + j][0:FC, :], wq[:, k, D + FC * j:D + FC * j + FC], xTa[:, k, :],
                                             start=(k == 0), stop=(k == KC - 1))
                        last.then_inc(S["k_p"], 1)
                if name[0] == "s":
                    for t in (2 * int(name[1]), 2 * int(name[1]) + 1):
                        pe.wait_ge(S["kx"], v * GT + t + 1)
                        if t < 2:
                            pe.wait_ge(S["v_sb"], v * 2 + 2)
                        else:
                            pe.wait_ge(S["y_done"], v * GT + t - 1)
                        for m in range(KC):
                            for b in range(PER_TILE):
                                last = pe.matmul(PB[4 + t % 2][32 * b:32 * b + 32, 32 * HPC * m:32 * HPC * m + 32 * HPC],
                                                 qT[:, m, 128 * t + 32 * b:128 * t + 32 * b + 32],
                                                 kexp[:, t % 2, m, :, 32 * b:32 * b + 32], start=True, stop=True)
                        last.then_inc(S["s_p"], 1)
                if name[0] == "o":
                    t = int(name[1])
                    if t == 0:
                        pe.wait_ge(S["k_sb"], v * KC + KC)
                    pe.wait_ge(S["p_t"], v * GT + t + 1)
                    if t >= 2:
                        pe.wait_ge(S["oT_sb"], v * GT + t - 1)
                    for h in range(H):
                        c, r = h // HQ, 32 * (h % HQ)
                        last = pe.matmul(PB[6 + t % 2][r:r + 32, 128 * c:128 * c + 128], vt[:, t, h, :], pT[:, h, :],
                                         start=True, stop=True)
                    last.then_inc(S["o_p"], 1)
                if name[0] == "y":
                    t = int(name[1])
                    if t == 0 and first_job(v):
                        pe.wait_ge(late_rest_in, 16 * LATE_REST_LOADS)
                    pe.wait_ge(S["oT_sb"], v * GT + t + 1)
                    if t % 2 == 0:
                        pe.wait_ge(S["shifted"], v * 2 + t // 2 + 1)
                    for c in range(HC):
                        last = pe.matmul(PB[4 + t % 2][:, 0:D], aoT[:, c, :], wp[:, c, :], start=(c == 0), stop=(c == HC - 1))
                    last.then_inc(S["y_p"], 1)

            def pass_pe(n, i, jobs, job1, job2, nxt):
                S, L = MS[n], MOE[n]
                ny = E + L["biased"]
                v = i + GROUPS * n
                pe.wait_ge(S["xTs"], v * 2 + 2)
                pe.wait_ge(S["x_low"], v + 1)
                pe.wait_ge(att_all["oT_sb"], jobs * GT)
                for t in range(GT):
                    for k in range(KC):
                        last = pe.matmul(PB[7][:, E * t:E * t + E], xT[:, k, 128 * t:128 * t + 128], gate_w[:, n, k, :],
                                         start=(k == 0), stop=(k == KC - 1))
                last.then_inc(S["g_p"], 1)

                def second(e):
                    q = order(L["biased"], e)
                    if q >= 1 or not isinstance(i, int) or i >= 1:
                        pe.wait_ge(S["y_acc"], i * ny + q)
                    elif n == 1:
                        pe.wait_ge(MS[0]["y_acc"], GROUPS * (E + 1))
                    if e >= 0:
                        pe.wait_ge(S["h_low"], v * (E * FM) + e * FM + FM)
                    for t in range(GT):
                        dst = PB[2 + t // 2][:, D * (t % 2):D * (t % 2) + D]
                        if e < 0:
                            last = pe.matmul(dst, cwT[:, 128 * t:128 * t + 128], bias2[:, :], start=True, stop=True)
                            continue
                        for m in range(FM):
                            for r, (a, b) in enumerate(HALVES):
                                tok = he[b][:, (e * FM + m) % RING, PER_TILE * t:PER_TILE * t + PER_TILE, :]
                                last = pe.matmul(dst, tok, w2[a][:, e, m, :], start=(m == 0 and r == 0),
                                                 stop=(m == FM - 1 and r == 2))
                    last.then_inc(S["y_p"], 1)

                for e in range(E):
                    pe.wait_ge(unit_low, n * UNITS + 2 * e + 2)
                    for m in range(FM):
                        k2 = e * FM + m
                        if k2 >= 2:
                            pe.wait_ge(S["h_act"], v * (E * FM) + k2 - 1)
                        for k in range(KC):
                            for r, (a, b) in enumerate(HALVES):
                                last = pe.matmul(PB[k2 % 2][:, 0:TOK], w1[a][:, k, e, 128 * m:128 * m + 128], compact(xh[b][:, k, :]),
                                                 start=(k == 0 and r == 0), stop=(k == KC - 1 and r == 2))
                        last.then_inc(S["h_p"], 1)
                        if (e, m) == BIAS_COPY and L["biased"]:
                            pe.wait_ge(S["cw_ready"], v + 1)
                            for t in range(GT):
                                last = pe.transpose(PB[6][0:E, 128 * t:128 * t + 128], cw[:, t, :], ident[:, :])
                            last.then_inc(S["cwT_p"], 1)
                        if m == 1 and e >= 1:
                            second(e - 1)
                        if (e, m) == BIAS_SUM and L["biased"]:
                            pe.wait_ge(S["cwT_sb"], i + 1)
                            second(-1)
                        job_steps(job_pe, pe, job1, job2, e, m)
                if nxt is not None:
                    pe.wait_ge(S["h_act"], v * (E * FM) + E * FM)
                    front_pe(pe, nxt[1], MS[nxt[0]] , False)
                second(E - 1)

            if stages >= 3:
                pe.wait_ge(*stage_done(1))
                pe.wait_ge(late_in, 16 * LATE_LOADS)
                whole_job(job_pe, pe, (0, 0, 0))
                front_pe(pe, 0, MS[0], False)
                passes(pe, pass_pe)


HALF_CONSTANTS = ("var_pick",)
LIN_LOADS = 17
LATE_LOADS = 17
LATE_REST_LOADS = 3


def layout(x):
    def chunks(w, size):
        return w.reshape(w.shape[0] // size, size, -1).transpose(1, 0, 2).reshape(size, -1)

    def cols(v, size):
        return v.reshape(-1, size).T

    zeros = np.zeros
    f4 = np.float32
    a = {}
    pt = x["x"][:, :, :80, :80].reshape(IMAGES, 3, 5, 16, 5, 16).transpose(1, 3, 5, 0, 2, 4)
    padded = zeros((PATCH_K, IMAGES, PITCH), f4)
    padded[:, :, :PATCHES] = pt.reshape(PATCH_K, IMAGES, PATCHES)
    a["patches"] = padded.reshape(PK, 128, TILES, 128).transpose(2, 1, 0, 3).reshape(TILES, 128, PATCH_K)
    a["conv_w"] = chunks(x["L0_tok_conv_w"].reshape(D, PATCH_K).T, 128)
    a["conv_b"] = x["L0_tok_conv_b"][None]
    ids = np.searchsorted(np.arange(1 / 32, 1, 1 / 32, dtype=f4), np.arange(0, 1 - 1e-6, 1 / 5, dtype=f4), side="right")
    rows = (ids[:, None] * 32 + ids).reshape(-1)
    pos = zeros((PER_TILE, PITCH, D), f4)
    pos[:, :PATCHES] = x["L0_tok_pos_table"][rows]
    a["pos"] = pos.reshape(128, D)
    a["wk"], a["wv"] = chunks(x["L0_attn_Wk"], FC), chunks(x["L0_attn_Wv"], FC)
    wq = x["L0_attn_Wq"].reshape(LG, D, PAIRS, 128).transpose(3, 2, 0, 1)
    a["wqT"] = wq.reshape(128, CHUNKS * D)
    wt = zeros((2, LD, LG, 2, LD), f4)
    for h in range(2):
        wt[h, :, :, h, :] = x["L0_attn_Wt"].transpose(1, 0, 2)
    a["wt2"] = wt.reshape(128, LG * 128)
    for n in ("bt", "gt", "betat"):
        a[n + "2"] = np.concatenate([x["L0_attn_" + n].T] * 2, 0)
    wf = x["L0_attn_Wf"].reshape(LG, PAIRS, 128, WM, 128).transpose(3, 2, 1, 0, 4)
    a["wf"] = wf.reshape(WM, 128, CHUNKS * 128)
    a["bf"], a["gf"], a["betaf"] = (cols(x["L0_attn_" + n], 128) for n in ("bf", "gf", "betaf"))
    a["wo"], a["bo"] = chunks(x["L0_attn_Wo"], 128), x["L0_attn_bo"][None]
    a["ident"] = np.eye(128, dtype=f4)
    same = np.kron(np.eye(2), np.ones((LD, LD))).astype(f4)
    a["center"] = (np.eye(128) - same / LD).astype(f4)
    a["mean768"] = np.full((128, 128), 1 / INNER, f4)
    a["key_sum"] = np.kron(np.eye(4), np.ones((PITCH, PITCH))).astype(f4)
    mask = zeros((2, 2, PITCH, 2, 2, LD), f4)
    for b in range(2):
        for h in range(2):
            mask[b, h, :, b, h] = 1
    a["v_mask"] = mask.reshape(128, 2 * 128) * f4(FEAT_SCALE / W_SCALE)
    pick = zeros((2, LD, CHUNKS, CHUNKS, 2), f4)
    for c in range(CHUNKS):
        for h in range(2):
            pick[h, :, c, c, h] = 1 / LD
    a["var_pick"] = pick.reshape(128, CHUNKS * 2 * CHUNKS).astype(np.float16)
    a["rstd_pick"] = zeros((FC, CHUNKS * 128), f4)
    a["rstd_pick"][:2 * CHUNKS] = pick.transpose(3, 4, 2, 0, 1).reshape(2 * CHUNKS, CHUNKS * 128) != 0
    slot = np.kron(np.eye(2), np.ones((LD, 1))).astype(f4)
    a["slot_mask"] = np.concatenate([slot, -slot], 1) / f4(W_SCALE)
    a["head_mask"] = (np.kron(np.eye(HPC), np.ones((HD, 1))) * HD ** -0.5).astype(f4)
    after = np.arange(PATCHES)[None] > np.arange(PITCH)[:, None]
    a["causal"] = np.tile(np.where(after, f4(-1e30), f4(0)), (PER_TILE, 1))
    a["before"] = np.tile((np.arange(E)[None] < np.arange(E)[:, None]).astype(f4).reshape(1, -1), (128, 1))
    def spread(w):
        padded = zeros((H, 32, D), f4)
        padded[:, :HD] = w.reshape(H, HD, D)
        return chunks(padded.reshape(H * 32, D), 128)

    a["a0_qkv"], a["a0_proj"] = chunks(x["L0_ffn_qkv_w"].T, FC), spread(x["L0_ffn_proj_w"].T)
    a["a1_qkv"], a["a1_proj"] = chunks(x["L1_attn_W_attn"], FC), spread(x["L1_attn_W_proj"])
    a["a2_qkv"], a["a2_proj"] = chunks(x["L1_ffn_Wqkv"], FC), spread(x["L1_ffn_Wproj"])
    a["a0_projb"], a["a1_projb"] = x["L0_ffn_proj_b"][None], x["L1_attn_b_proj"][None]
    a["a1_qkb"], a["a1_vb"] = cols(x["L1_attn_b_attn"][:2 * D], FC), x["L1_attn_b_attn"][None, 2 * D:]
    for m, pre in (("m0", "L0_ffn_"), ("m1", "L1_ffn_")):
        for n in ("ln1", "ln2"):
            a[f"{m}_{n}"] = np.concatenate([cols(x[f"{pre}{n}_g"], FC), cols(x[f"{pre}{n}_b"], FC)], 1)
    a["m0_gate"], a["m1_gate"] = chunks(x["L0_ffn_gate_w"].T, FC), chunks(x["L1_ffn_Wrouter"], FC)
    w1 = {"m0": x["L0_ffn_w1"].transpose(2, 0, 1), "m1": x["L1_ffn_W1"].transpose(1, 0, 2)}
    w2 = {"m0": x["L0_ffn_w2"].transpose(0, 2, 1), "m1": x["L1_ffn_W2"]}
    for m in ("m0", "m1"):
        a[f"{m}_w1"] = chunks(w1[m].reshape(D, E * FF), FC)
        a[f"{m}_w2"] = w2[m].reshape(E, FM, 128, D).transpose(2, 0, 1, 3).reshape(128, E * FM * D)
    a["m0_gateb"], a["m0_b2"] = x["L0_ffn_gate_b"][None], x["L0_ffn_b2"]
    a["m0_b1"] = x["L0_ffn_b1"].reshape(E, FM, 128).transpose(2, 0, 1).reshape(128, E * FM)
    return a


def program(nc, stages=7):
    dram = {n: nc.dram_tensor(n, tuple(s), F16 if n in HALF_CONSTANTS else F32, kind="ExternalInput").ap()
            for n, s in load_shapes().items()}
    out = nc.dram_tensor("out", (TILES, 128, D), F32, kind="ExternalOutput").ap()
    build(nc, dram, out, stages)


def kernel(**inputs):
    import concourse.bacc as bacc
    from concourse.bass_utils import run_bass_kernel_spmd

    nc = bacc.Bacc("TRN2", target_bir_lowering=False, num_devices=1)
    program(nc)
    x = {n: np.asarray(v) for n, v in inputs.items()}
    arrays = {n: np.ascontiguousarray(v) for n, v in layout(x).items()}
    r = run_bass_kernel_spmd(nc, [arrays], core_ids=[0])
    got = np.asarray(r.results[0]["out"])
    return got.reshape(IMAGES, PITCH, D)[:, :PATCHES]
```
